# Optimizing a Trainium2 kernel written in Bass

```python
import numpy as np
import jax
import jax.numpy as jnp

def _softmax(x, axis=-1):
    return jax.nn.softmax(x, axis=axis)

def _gelu(x):
    return jax.nn.gelu(x, approximate=True)

def _silu(x):
    return jax.nn.silu(x)

def _sigmoid(x):
    return jax.nn.sigmoid(x)

def _layernorm(x, axis=-1, eps=1e-05):
    m = jnp.mean(x, axis=axis, keepdims=True)
    v = jnp.var(x, axis=axis, keepdims=True)
    return (x - m) / jnp.sqrt(v + eps)

def _scatter_add(tgt, idx, src, axis=0):
    return tgt.at[idx].add(src)

def _segment_sum(src, seg, n):
    return jax.ops.segment_sum(src, seg, n)
kernel_name = 'mk_gps_d2_gnn_r32_4143d0'

def setup_inputs(seed: int=0):
    np.random.seed(seed)
    _w = jnp.asarray

    def _rec_inputs():
        import jax
        import jax.numpy as jnp
        _gk = jax.random.key(seed)
        x = -0.0002117 + 1 * jax.random.normal(jax.random.fold_in(_gk, 1), (3125, 256), jnp.float32)
        _s = jax.random.randint(jax.random.fold_in(_gk, 2), (25000,), 0, 3125, jnp.int32)
        _d = jax.random.randint(jax.random.fold_in(_gk, 3), (25000,), 0, 3125, jnp.int32)
        _loop = jnp.arange(3125, dtype=jnp.int32)
        src = jnp.concatenate([_s, _d, _loop])
        dst = jnp.concatenate([_d, _s, _loop])
        _o = jnp.argsort(dst, stable=True)
        src = src[_o]
        dst = dst[_o]
        return (x, src, dst)
    x, src, dst = _rec_inputs()

    def _L0_gnn_setup():
        import jax, jax.numpy as jnp
        import numpy as np
        NUM_NODES = 3125
        HIDDEN = 256
        NUM_EDGES = 50000

        def _sage_conv(x, edge_index, w_l, w_r, b):
            src, dst = (edge_index[0], edge_index[1])
            n = x.shape[0]
            nbr_sum = jax.ops.segment_sum(x[src], dst, num_segments=n)
            deg = jax.ops.segment_sum(jnp.ones((src.shape[0],), x.dtype), dst, num_segments=n)
            nbr_mean = nbr_sum / jnp.maximum(deg, 1.0)[:, None]
            return nbr_mean @ w_l.T + x @ w_r.T + b
        key = jax.random.key(seed)
        ks = jax.random.split(key, 8)

        def glorot(k, shape):
            lim = float(np.sqrt(6.0 / (shape[0] + shape[1])))
            return jax.random.uniform(k, shape, jnp.float32, -lim, lim)
        return {'node_features': jax.random.normal(ks[0], (NUM_NODES, HIDDEN), jnp.float32), 'w1_l': glorot(ks[1], (HIDDEN, HIDDEN)), 'w1_r': glorot(ks[2], (HIDDEN, HIDDEN)), 'b1': jnp.zeros((HIDDEN,), jnp.float32), 'w2_l': glorot(ks[3], (HIDDEN, HIDDEN)), 'w2_r': glorot(ks[4], (HIDDEN, HIDDEN)), 'b2': jnp.zeros((HIDDEN,), jnp.float32), 'edge_index': jax.random.randint(ks[5], (2, NUM_EDGES), 0, NUM_NODES, jnp.int64)}
    _L0_gnn_all = _L0_gnn_setup()
    _L0_gnn_in = {k: v for k, v in _L0_gnn_all.items() if k in ('w1_l', 'w1_r', 'b1', 'w2_l', 'w2_r', 'b2')}
    del _L0_gnn_all

    def _L0_mix_setup():
        import jax, jax.numpy as jnp
        import numpy as np
        A, Bc, Cc = (0.5, 1.0, 1.0)
        H = 8
        EPS = 1e-12

        def _normalize(t):
            n = jnp.linalg.norm(t, axis=-1, keepdims=True)
            return t / jnp.maximum(n, EPS)
        key = jax.random.key(seed)
        ks = jax.random.split(key, 5)
        B, N, C = (8, 64, 256)
        D = C // H
        x = jax.random.normal(ks[0], (B, N, C), dtype=jnp.float32)
        Wqkv = jax.random.normal(ks[1], (3 * H * D, C), dtype=jnp.float32) * 0.02
        bqkv = jnp.zeros((3 * H * D,), dtype=jnp.float32)
        Wproj = jax.random.normal(ks[2], (C, H * D), dtype=jnp.float32) * 0.02
        bproj = jnp.zeros((C,), dtype=jnp.float32)
        temperature = jnp.ones((1, H, 1, 1), dtype=jnp.float32)
        return {'x': x, 'Wqkv': Wqkv, 'bqkv': bqkv, 'Wproj': Wproj, 'bproj': bproj, 'temperature': temperature}
    _L0_mix_all = _L0_mix_setup()
    _L0_mix_in = {k: v for k, v in _L0_mix_all.items() if k in ('Wqkv', 'bqkv', 'Wproj', 'bproj', 'temperature')}
    del _L0_mix_all

    def _L0_ffn_setup():
        import jax, jax.numpy as jnp
        import numpy as np
        D_MODEL = 256
        N_EXPERTS = 16
        HIDDEN = 512
        SCALE = 0.02
        key = jax.random.key(seed)
        ks = jax.random.split(key, 5)
        x = jax.random.normal(ks[0], (4, 256, D_MODEL), dtype=jnp.float32)
        gate_w = jax.random.normal(ks[1], (D_MODEL, N_EXPERTS), dtype=jnp.float32) * SCALE
        gate_b = jnp.zeros((N_EXPERTS,), dtype=jnp.float32)
        w1 = jax.random.normal(ks[2], (N_EXPERTS, D_MODEL, HIDDEN), dtype=jnp.float32) * SCALE
        w2 = jax.random.normal(ks[3], (N_EXPERTS, D_MODEL, HIDDEN), dtype=jnp.float32) * SCALE
        w3 = jax.random.normal(ks[4], (N_EXPERTS, HIDDEN, D_MODEL), dtype=jnp.float32) * SCALE
        return {'x': x, 'gate_w': gate_w, 'gate_b': gate_b, 'w1': w1, 'w2': w2, 'w3': w3}
    _L0_ffn_all = _L0_ffn_setup()
    _L0_ffn_in = {k: v for k, v in _L0_ffn_all.items() if k in ('gate_w', 'gate_b', 'w1', 'w2', 'w3')}
    del _L0_ffn_all

    def _L1_gnn_setup():
        import jax, jax.numpy as jnp
        import numpy as np
        N, E, C_IN = (50000, 25000, 256)
        H = 2
        C1 = 64
        C2 = 128
        NEG_SLOPE = 0.2

        def glorot(key, shape):
            fan_in, fan_out = (shape[0], shape[1])
            lim = jnp.sqrt(6.0 / (fan_in + fan_out))
            return jax.random.uniform(key, shape, jnp.float32, -lim, lim)

        def gatv2_conv(x, src, dst, Wl, Wr, att, b, heads, c_out):
            n = x.shape[0]
            xl = (x @ Wl).reshape(n, heads, c_out)
            xr = (x @ Wr).reshape(n, heads, c_out)
            e = jax.nn.leaky_relu(xl[src] + xr[dst], NEG_SLOPE)
            logit = jnp.einsum('ehc,hc->eh', e, att)
            m = jax.ops.segment_max(logit, dst, num_segments=n)
            a = jnp.exp(logit - m[dst])
            denom = jax.ops.segment_sum(a, dst, num_segments=n)
            alpha = a / denom[dst]
            out = jax.ops.segment_sum(alpha[:, :, None] * xl[src], dst, num_segments=n)
            return out.reshape(n, heads * c_out) + b
        key = jax.random.key(seed)
        ks = jax.random.split(key, 12)
        x = jax.random.normal(ks[0], (N, C_IN), jnp.float32)
        edge_index = jax.random.randint(ks[1], (2, E), 0, N, jnp.int64)
        Wl0 = glorot(ks[2], (C_IN, H * C1))
        Wr0 = glorot(ks[3], (C_IN, H * C1))
        att0 = glorot(ks[4], (H, C1))
        b0 = jnp.zeros((H * C1,), jnp.float32)
        Wl1 = glorot(ks[5], (H * C1, H * C2))
        Wr1 = glorot(ks[6], (H * C1, H * C2))
        att1 = glorot(ks[7], (H, C2))
        b1 = jnp.zeros((H * C2,), jnp.float32)
        return {'x': x, 'edge_index': edge_index, 'Wl0': Wl0, 'Wr0': Wr0, 'att0': att0, 'b0': b0, 'Wl1': Wl1, 'Wr1': Wr1, 'att1': att1, 'b1': b1}
    _L1_gnn_all = _L1_gnn_setup()
    _L1_gnn_in = {k: v for k, v in _L1_gnn_all.items() if k in ('Wl0', 'Wr0', 'att0', 'b0', 'Wl1', 'Wr1', 'att1', 'b1')}
    del _L1_gnn_all

    def _L1_mix_setup():
        import jax, jax.numpy as jnp
        import numpy as np
        DIM = 256
        HEADS = 4
        DIM_HEAD = 32
        NUM_MEM = 4
        HIDDEN = HEADS * DIM_HEAD
        SCALE = DIM_HEAD ** (-0.5)

        def rmsnorm(x, g):
            n = jnp.linalg.norm(x, axis=-1, keepdims=True)
            return x / jnp.maximum(n, 1e-12) * g * x.shape[-1] ** 0.5
        key = jax.random.key(seed)
        ks = jax.random.split(key, 8)
        B, N = (4, 512)
        return {'x': jax.random.normal(ks[0], (B, N, DIM), jnp.float32), 't': jax.random.normal(ks[1], (B,), jnp.float32), 'w_qkv': jax.random.normal(ks[2], (DIM, 3 * HIDDEN), jnp.float32) * 0.02, 'mem_kv': jax.random.normal(ks[3], (2, HEADS, DIM_HEAD, NUM_MEM), jnp.float32), 'w_out': jax.random.normal(ks[4], (HIDDEN, DIM), jnp.float32) * 0.02, 'b_out': jnp.zeros((DIM,), jnp.float32), 'g_out': jnp.ones((DIM,), jnp.float32), 'g_pre': jnp.ones((DIM,), jnp.float32)}
    _L1_mix_all = _L1_mix_setup()
    _L1_mix_in = {k: v for k, v in _L1_mix_all.items() if k in ('t', 'w_qkv', 'mem_kv', 'w_out', 'b_out', 'g_out', 'g_pre')}
    del _L1_mix_all

    def _L1_ffn_setup():
        import jax, jax.numpy as jnp
        import numpy as np
        B, T, D, H, E = (16, 128, 256, 512, 8)
        key = jax.random.key(seed)
        ks = jax.random.split(key, 5)
        x = jax.random.normal(ks[0], (B, T, D), dtype=jnp.float32)
        gate_w = jax.random.normal(ks[1], (D, E), dtype=jnp.float32) * 0.02
        gate_b = jnp.zeros((E,), dtype=jnp.float32)
        W1 = jax.random.normal(ks[2], (E, D, H), dtype=jnp.float32) * 0.02
        b1 = jnp.zeros((E, H), dtype=jnp.float32)
        W2 = jax.random.normal(ks[3], (E, H, D), dtype=jnp.float32) * 0.02
        b2 = jnp.zeros((E, D), dtype=jnp.float32)
        return {'x': x, 'gate_w': gate_w, 'gate_b': gate_b, 'W1': W1, 'b1': b1, 'W2': W2, 'b2': b2}
    _L1_ffn_all = _L1_ffn_setup()
    _L1_ffn_in = {k: v for k, v in _L1_ffn_all.items() if k in ('gate_w', 'gate_b', 'W1', 'b1', 'W2', 'b2')}
    del _L1_ffn_all
    return {'x': x, 'src': src, 'dst': dst, 'L0_gnn_w1_l': _L0_gnn_in['w1_l'], 'L0_gnn_w1_r': _L0_gnn_in['w1_r'], 'L0_gnn_b1': _L0_gnn_in['b1'], 'L0_gnn_w2_l': _L0_gnn_in['w2_l'], 'L0_gnn_w2_r': _L0_gnn_in['w2_r'], 'L0_gnn_b2': _L0_gnn_in['b2'], 'L0_mix_Wqkv': _L0_mix_in['Wqkv'], 'L0_mix_bqkv': _L0_mix_in['bqkv'], 'L0_mix_Wproj': _L0_mix_in['Wproj'], 'L0_mix_bproj': _L0_mix_in['bproj'], 'L0_mix_temperature': _L0_mix_in['temperature'], 'L0_ffn_gate_w': _L0_ffn_in['gate_w'], 'L0_ffn_gate_b': _L0_ffn_in['gate_b'], 'L0_ffn_w1': _L0_ffn_in['w1'], 'L0_ffn_w2': _L0_ffn_in['w2'], 'L0_ffn_w3': _L0_ffn_in['w3'], 'L1_gnn_Wl0': _L1_gnn_in['Wl0'], 'L1_gnn_Wr0': _L1_gnn_in['Wr0'], 'L1_gnn_att0': _L1_gnn_in['att0'], 'L1_gnn_b0': _L1_gnn_in['b0'], 'L1_gnn_Wl1': _L1_gnn_in['Wl1'], 'L1_gnn_Wr1': _L1_gnn_in['Wr1'], 'L1_gnn_att1': _L1_gnn_in['att1'], 'L1_gnn_b1': _L1_gnn_in['b1'], 'L1_mix_t': _L1_mix_in['t'], 'L1_mix_w_qkv': _L1_mix_in['w_qkv'], 'L1_mix_mem_kv': _L1_mix_in['mem_kv'], 'L1_mix_w_out': _L1_mix_in['w_out'], 'L1_mix_b_out': _L1_mix_in['b_out'], 'L1_mix_g_out': _L1_mix_in['g_out'], 'L1_mix_g_pre': _L1_mix_in['g_pre'], 'L1_ffn_gate_w': _L1_ffn_in['gate_w'], 'L1_ffn_gate_b': _L1_ffn_in['gate_b'], 'L1_ffn_W1': _L1_ffn_in['W1'], 'L1_ffn_b1': _L1_ffn_in['b1'], 'L1_ffn_W2': _L1_ffn_in['W2'], 'L1_ffn_b2': _L1_ffn_in['b2']}

def reference(x, src, dst, L0_gnn_w1_l, L0_gnn_w1_r, L0_gnn_b1, L0_gnn_w2_l, L0_gnn_w2_r, L0_gnn_b2, L0_mix_Wqkv, L0_mix_bqkv, L0_mix_Wproj, L0_mix_bproj, L0_mix_temperature, L0_ffn_gate_w, L0_ffn_gate_b, L0_ffn_w1, L0_ffn_w2, L0_ffn_w3, L1_gnn_Wl0, L1_gnn_Wr0, L1_gnn_att0, L1_gnn_b0, L1_gnn_Wl1, L1_gnn_Wr1, L1_gnn_att1, L1_gnn_b1, L1_mix_t, L1_mix_w_qkv, L1_mix_mem_kv, L1_mix_w_out, L1_mix_b_out, L1_mix_g_out, L1_mix_g_pre, L1_ffn_gate_w, L1_ffn_gate_b, L1_ffn_W1, L1_ffn_b1, L1_ffn_W2, L1_ffn_b2):
    import jax
    import jax.numpy as jnp

    def _L0_gnn_ref(node_features, w1_l, w1_r, b1, w2_l, w2_r, b2, edge_index):
        import jax, jax.numpy as jnp
        import numpy as np
        NUM_NODES = 3125
        HIDDEN = 256
        NUM_EDGES = 50000

        def _sage_conv(x, edge_index, w_l, w_r, b):
            src, dst = (edge_index[0], edge_index[1])
            n = x.shape[0]
            nbr_sum = jax.ops.segment_sum(x[src], dst, num_segments=n)
            deg = jax.ops.segment_sum(jnp.ones((src.shape[0],), x.dtype), dst, num_segments=n)
            nbr_mean = nbr_sum / jnp.maximum(deg, 1.0)[:, None]
            return nbr_mean @ w_l.T + x @ w_r.T + b
        h = _sage_conv(node_features, edge_index, w1_l, w1_r, b1)
        h = jax.nn.relu(h)
        out = _sage_conv(h, edge_index, w2_l, w2_r, b2)
        return out

    def _L0_mix_ref(x, Wqkv, bqkv, Wproj, bproj, temperature):
        import jax, jax.numpy as jnp
        import numpy as np
        A, Bc, Cc = (0.5, 1.0, 1.0)
        H = 8
        EPS = 1e-12

        def _normalize(t):
            n = jnp.linalg.norm(t, axis=-1, keepdims=True)
            return t / jnp.maximum(n, EPS)
        B, N, C = x.shape
        D = C // H
        scale = float(D) ** 0.25
        qkv = (x @ Wqkv.T + bqkv).reshape(B, N, 3, H, D)
        qkv = jnp.transpose(qkv, (2, 0, 3, 1, 4))
        q, k, v = (qkv[0], qkv[1], qkv[2])
        q = q * scale
        v1 = jnp.concatenate([jnp.ones((B, H, N, 1), dtype=v.dtype), v], axis=-1)
        qn = _normalize(q) * (scale * temperature)
        kn = _normalize(k) * scale
        vN = v1 / N
        kv_mod = jnp.einsum('bhni,bhnj,bhne->bhije', kn, kn, vN)
        kv = jnp.einsum('bhnd,bhne->bhde', kn, vN)
        vsum = jnp.sum(vN, axis=-2)[:, :, None, :]
        y = A * jnp.einsum('bhni,bhnj,bhije->bhne', qn, qn, kv_mod) + scale ** 2 * Bc * jnp.einsum('bhnd,bhde->bhne', qn, kv) + scale ** 4 * Cc * vsum
        y_norm, y = (y[..., :1], y[..., 1:])
        y = y / y_norm
        out = jnp.transpose(y, (0, 2, 1, 3)).reshape(B, N, H * D)
        return out @ Wproj.T + bproj

    def _L0_ffn_ref(x, gate_w, gate_b, w1, w2, w3):
        import jax, jax.numpy as jnp
        import numpy as np
        D_MODEL = 256
        N_EXPERTS = 16
        HIDDEN = 512
        SCALE = 0.02
        n_experts = w1.shape[0]
        logits = jnp.einsum('bsd,de->bse', x, gate_w) + gate_b
        probs = jax.nn.softmax(logits, axis=-1)
        top_probs, top_idx = jax.lax.top_k(probs, 2)
        top_probs = top_probs / jnp.sum(top_probs, axis=-1, keepdims=True)
        dispatch = jnp.sum(jax.nn.one_hot(top_idx, n_experts, dtype=x.dtype) * top_probs[..., None], axis=-2)
        h1 = jnp.einsum('bsd,edh->bseh', x, w1)
        h2 = jnp.einsum('bsd,edh->bseh', x, w2)
        hidden = jax.nn.silu(h1) * h2
        expert_out = jnp.einsum('bseh,eho->bseo', hidden, w3)
        return jnp.einsum('bseo,bse->bso', expert_out, dispatch)

    def _L1_gnn_ref(x, edge_index, Wl0, Wr0, att0, b0, Wl1, Wr1, att1, b1):
        import jax, jax.numpy as jnp
        import numpy as np
        N, E, C_IN = (50000, 25000, 256)
        H = 2
        C1 = 64
        C2 = 128
        NEG_SLOPE = 0.2

        def glorot(key, shape):
            fan_in, fan_out = (shape[0], shape[1])
            lim = jnp.sqrt(6.0 / (fan_in + fan_out))
            return jax.random.uniform(key, shape, jnp.float32, -lim, lim)

        def gatv2_conv(x, src, dst, Wl, Wr, att, b, heads, c_out):
            n = x.shape[0]
            xl = (x @ Wl).reshape(n, heads, c_out)
            xr = (x @ Wr).reshape(n, heads, c_out)
            e = jax.nn.leaky_relu(xl[src] + xr[dst], NEG_SLOPE)
            logit = jnp.einsum('ehc,hc->eh', e, att)
            m = jax.ops.segment_max(logit, dst, num_segments=n)
            a = jnp.exp(logit - m[dst])
            denom = jax.ops.segment_sum(a, dst, num_segments=n)
            alpha = a / denom[dst]
            out = jax.ops.segment_sum(alpha[:, :, None] * xl[src], dst, num_segments=n)
            return out.reshape(n, heads * c_out) + b
        n = x.shape[0]
        loops = jnp.arange(n, dtype=edge_index.dtype)
        src = jnp.concatenate([edge_index[0], loops])
        dst = jnp.concatenate([edge_index[1], loops])
        h = gatv2_conv(x, src, dst, Wl0, Wr0, att0, b0, H, C1)
        h = jax.nn.relu(h)
        out = gatv2_conv(h, src, dst, Wl1, Wr1, att1, b1, H, C2)
        return out

    def _L1_mix_ref(x, t, w_qkv, mem_kv, w_out, b_out, g_out, g_pre):
        import jax, jax.numpy as jnp
        import numpy as np
        DIM = 256
        HEADS = 4
        DIM_HEAD = 32
        NUM_MEM = 4
        HIDDEN = HEADS * DIM_HEAD
        SCALE = DIM_HEAD ** (-0.5)

        def rmsnorm(x, g):
            n = jnp.linalg.norm(x, axis=-1, keepdims=True)
            return x / jnp.maximum(n, 1e-12) * g * x.shape[-1] ** 0.5
        b, n, c = x.shape
        xn = rmsnorm(x, g_pre)
        qkv = xn @ w_qkv
        q, k, v = jnp.split(qkv, 3, axis=-1)

        def to_heads(z):
            return z.reshape(b, n, HEADS, DIM_HEAD).transpose(0, 2, 3, 1)
        q, k, v = map(to_heads, (q, k, v))
        mk = jnp.broadcast_to(mem_kv[0], (b, HEADS, DIM_HEAD, NUM_MEM))
        mv = jnp.broadcast_to(mem_kv[1], (b, HEADS, DIM_HEAD, NUM_MEM))
        k = jnp.concatenate([mk, k], axis=-1)
        v = jnp.concatenate([mv, v], axis=-1)
        q = jax.nn.softmax(q, axis=-2) * SCALE
        k = jax.nn.softmax(k, axis=-1)
        context = jnp.einsum('bhdn,bhen->bhde', k, v)
        out = jnp.einsum('bhde,bhdn->bhen', context, q)
        out = out.transpose(0, 3, 1, 2).reshape(b, n, HIDDEN)
        out = rmsnorm(out @ w_out + b_out, g_out)
        return out + x

    def _L1_ffn_ref(x, gate_w, gate_b, W1, b1, W2, b2):
        import jax, jax.numpy as jnp
        import numpy as np
        B, T, D, H, E = (16, 128, 256, 512, 8)
        Bb, Tt, Dd = x.shape
        Ee = gate_w.shape[1]
        xf = x.reshape(-1, Dd)
        N = xf.shape[0]
        logits = xf @ gate_w + gate_b
        probs = jax.nn.softmax(logits, axis=-1)
        top2_vals, top2_idx = jax.lax.top_k(probs, 2)
        cw = jnp.zeros((N, Ee), dtype=xf.dtype).at[jnp.arange(N)[:, None], top2_idx].add(top2_vals)

        def step(acc, params):
            w1, bb1, w2, bb2, we = params
            h = jax.nn.gelu(xf @ w1 + bb1, approximate=False)
            y = h @ w2 + bb2
            return (acc + we[:, None] * y, None)
        out, _ = jax.lax.scan(step, jnp.zeros_like(xf), (W1, b1, W2, b2, cw.T))
        return out.reshape(Bb, Tt, Dd)
    edge_index = jnp.stack([src, dst])
    xn = _layernorm(x, axis=-1)
    x = x + _L0_gnn_ref(xn, L0_gnn_w1_l, L0_gnn_w1_r, L0_gnn_b1, L0_gnn_w2_l, L0_gnn_w2_r, L0_gnn_b2, edge_index) + _L0_mix_ref(xn[None], L0_mix_Wqkv, L0_mix_bqkv, L0_mix_Wproj, L0_mix_bproj, L0_mix_temperature)[0]
    x = x + _L0_ffn_ref(_layernorm(x, axis=-1)[None], L0_ffn_gate_w, L0_ffn_gate_b, L0_ffn_w1, L0_ffn_w2, L0_ffn_w3)[0]
    xn = _layernorm(x, axis=-1)
    x = x + _L1_gnn_ref(xn, edge_index, L1_gnn_Wl0, L1_gnn_Wr0, L1_gnn_att0, L1_gnn_b0, L1_gnn_Wl1, L1_gnn_Wr1, L1_gnn_att1, L1_gnn_b1) + _L1_mix_ref(xn[None], L1_mix_t, L1_mix_w_qkv, L1_mix_mem_kv, L1_mix_w_out, L1_mix_b_out, L1_mix_g_out, L1_mix_g_pre)[0]
    x = x + _L1_ffn_ref(_layernorm(x, axis=-1)[None], L1_ffn_gate_w, L1_ffn_gate_b, L1_ffn_W1, L1_ffn_b1, L1_ffn_W2, L1_ffn_b2)[0]
    return x

_drawn_inputs = setup_inputs


def setup_inputs(seed=0):
    import zlib

    import numpy as np

    out = dict(_drawn_inputs(seed))
    spreads = {'L0_gnn_b1': (0.0, 0.1),
     'L0_gnn_b2': (0.0, 0.1),
     'L0_mix_bqkv': (0.0, 0.383),
     'L0_mix_bproj': (0.0, 0.1),
     'L0_mix_temperature': (1.0, 0.6),
     'L0_ffn_gate_b': (0.0, 0.8),
     'L1_gnn_b0': (0.0, 0.397),
     'L1_gnn_b1': (0.0, 0.1),
     'L1_mix_b_out': (0.0, 0.1),
     'L1_mix_g_out': (1.0, 0.2),
     'L1_mix_g_pre': (1.0, 0.6),
     'L1_ffn_gate_b': (0.0, 0.8),
     'L1_ffn_b1': (0.0, 0.8),
     'L1_ffn_b2': (0.0, 0.8)}
    factors = {'L0_mix_Wqkv': 8.0,
     'L0_ffn_gate_w': 5.321,
     'L0_ffn_w1': 4.884,
     'L0_ffn_w2': 4.817,
     'L0_ffn_w3': 4.81,
     'L1_gnn_Wr0': 6.84,
     'L1_gnn_Wr1': 8.0,
     'L1_gnn_att1': 8.0,
     'L1_mix_mem_kv': 8.0,
     'L1_ffn_gate_w': 5.012,
     'L1_ffn_W1': 7.581,
     'L1_ffn_W2': 6.932}
    for name, (base, spread) in spreads.items():
        noise = np.random.default_rng([zlib.crc32(name.encode()), seed]).standard_normal(out[name].shape)
        drawn = base * np.exp(spread * noise) if base else spread * noise
        out[name] = jnp.asarray(drawn.astype(out[name].dtype))
    for name, factor in factors.items():
        out[name] = (out[name] * factor).astype(out[name].dtype)
    return out
```

```python
from contextlib import ExitStack

import concourse.bass as bass
from concourse import mybir

ALU = mybir.AluOpType
ACT = mybir.ActivationFunctionType
F32 = mybir.dt.float32
I32 = mybir.dt.int32
U32 = mybir.dt.uint32
AX = mybir.AxisListType.X

P = 128
N = 3125
T = -(-N // P)
TAIL = N - (T - 1) * P
D = 256
E = 53125
CHUNKS = -(-E // P)
CB = -(-CHUNKS // P)
BODY = 16
GROUP = 4
ROUND = 512
MAX_ROUNDS = -(-(CHUNKS * T + 2 * BODY) // ROUND)
MAX_BODIES = MAX_ROUNDS * ROUND // BODY
UN = 5
LN_EPS = 1e-5
FAR = 1.0e6
LOW = -1.0e30


def link(eng, sem, i=0, per=0, base=0):
    count = [0]

    def step(ins):
        count[0] += 1
        ins.then_inc(sem, 1)
        eng.wait_ge(sem, base + i * per + count[0])
        return count[0]

    step.count = count
    return step


def back(u, slots, unroll):
    d = 1
    while ((u - d) % unroll) % slots != u % slots:
        d += 1
    return d


def tile(buf, k):
    return buf[:, bass.ds(k, 1), :].rearrange("p a f -> p (a f)")


def settle(eng, c):
    eng.sem_inc(c.settled, 1)


def bcast(ap, n):
    return ap.unsqueeze(2).to_broadcast([ap.shape[0], ap.shape[1], n])


def rows(dram, n=T):
    return dram.rearrange("(t p) f -> p t f", p=P)


def constants(nc, s, c):
    made, dve = s("const_made"), s("const_dve")
    with nc.sbuf_tensor("quadrant", [P, 2], I32) as quad, nc.Block() as block:

        @block.gpsimd
        def _(pool):
            fl = dict(allow_small_or_imprecise_dtypes=True)
            nc.gpsimd.iota(c.col[:], [[1, P]], base=0, channel_multiplier=0, **fl).then_inc(made, 1)
            nc.gpsimd.iota(c.part[:], [[0, 1]], base=0, channel_multiplier=1, **fl).then_inc(made, 1)
            nc.gpsimd.iota(c.pair_no[:], [[1, ROUND]], base=0, channel_multiplier=0, **fl).then_inc(made, 1)
            nc.gpsimd.iota(c.valid[:], [[P, T]], base=0, channel_multiplier=1, **fl).then_inc(made, 1)
            nc.gpsimd.iota(c.row8[:], [[1, 8], [0, P]], base=0, channel_multiplier=0, **fl).then_inc(made, 1)
            nc.gpsimd.iota(c.head[:], [[1, 4], [0, 32]], base=0, channel_multiplier=0, **fl).then_inc(made, 1)
            nc.gpsimd.iota(quad[:, 0:1], [[0, 1]], base=0, channel_multiplier=1).then_inc(made, 1)

        @block.vector
        def _(dve_):
            v = nc.vector
            lk = link(dve_, dve)
            dve_.wait_ge(made, 7)
            v.memset(c.ones[:], 1.0)
            v.memset(c.low[:], LOW)
            v.tensor_scalar(c.ident[:], c.col[:], c.part[:, 0:1], None, ALU.is_equal)
            v.tensor_scalar(c.after[:], c.col[:], c.part[:, 0:1], None, ALU.is_gt)
            v.tensor_single_scalar(c.valid[:], c.valid[:], float(N), ALU.is_lt)
            v.tensor_scalar(c.row8[:], c.row8[:], c.part[0:8, 0:1], None, ALU.is_equal)
            lk(v.tensor_single_scalar(quad[:, 1:2], quad[:, 0:1], 5, ALU.arith_shift_right))
            lk(v.tensor_copy(c.quadf[:], quad[:, 1:2]))
            lk(v.tensor_scalar(c.head[:], c.head[:], c.quadf[:, 0:1], None, ALU.is_equal))


def pair_tables(nc, s, c, src, dst, table_a, table_b):
    loaded, dve, act, ready, got, pe_s, prefix = (s("tab_" + x) for x in ("loaded", "dve", "act", "ready", "got", "pe", "prefix"))
    chosen, summed, staged, stored, filled = (s("tab_" + x) for x in ("chosen", "summed", "staged", "stored", "filled"))
    full = E // P
    with ExitStack() as x:
        sb = lambda n, sh, d=F32: x.enter_context(nc.sbuf_tensor("tab_" + n, sh, d))
        ii = sb("ii", [P, 2, CB, P], I32)
        srcf, dstf = sb("srcf", [P, CB, P]), sb("dstf", [P, CB, P])
        low = sb("low", [P, CB, P])
        lo, hi = sb("lo", [P, CB]), sb("hi", [P, CB])
        lo_i, hi_i = sb("lo_i", [P, CB], I32), sb("hi_i", [P, CB], I32)
        cnt, start, end, rel = sb("cnt", [P, CB]), sb("start", [P, CB]), sb("end", [P, CB]), sb("rel", [P, CB])
        tot = sb("tot", [P, CB])
        relb = sb("relb", [P, CB, P])
        pick = sb("pick", [P, CB, ROUND])
        jcur = sb("jcur", [P, ROUND])
        val, tl, dr, m1 = sb("val", [P, ROUND]), sb("tl", [P, ROUND]), sb("dr", [P, ROUND]), sb("m1", [P, ROUND])
        sa, sbb = sb("sa", [P, 2 * ROUND], I32), sb("sb", [P, 2 * ROUND], I32)
        ps = [x.enter_context(nc.psum_tensor(f"tab_ps{i}", [P, ROUND], F32)) for i in range(5)]
        ga = sa[:].rearrange("p (g w) -> p g w", w=2 * GROUP)
        gb = sbb[:].rearrange("p (g w) -> p g w", w=2 * GROUP)
        four = lambda a: a.rearrange("p (g u) -> p g u", u=GROUP)
        block = x.enter_context(nc.Block())

        @block.sync
        def _(sp):
            sp.wait_ge(filled, 1)
            for w, a in enumerate((src, dst)):
                cut = (CB - 1) * P * P
                sp.dma_start(ii[:, w, 0:CB - 1, :], a[0:cut].rearrange("(k p e) -> p k e", p=P, e=P)).then_inc(loaded, 16)
                sp.dma_start(ii[0:full - (CB - 1) * P, w, CB - 1, :], a[cut:full * P].rearrange("(p e) -> p e", e=P)).then_inc(loaded, 16)
                sp.dma_start(ii[full - (CB - 1) * P:full - (CB - 1) * P + 1, w, CB - 1, 0:E - full * P],
                             a[full * P:E].rearrange("(o e) -> o e", o=1)).then_inc(loaded, 16)
            sp.wait_ge(ready, 1)
            rounds = sp.value_load(c.loops[0:1, 1:2], min_val=1, max_val=MAX_ROUNDS)
            per = ROUND // BODY
            with sp.Fori(0, rounds) as r:
                sp.wait_ge(staged, r + 1)
                settle(sp, c)
                sp.dma_start(table_a[bass.ds(r * per, per), :, :].rearrange("b p w -> p b w"),
                             sa[:].rearrange("p (b w) -> p b w", w=2 * BODY)).then_inc(stored, 16)
                sp.dma_start(table_b[bass.ds(r * per, per), :, :].rearrange("b p w -> p b w"),
                             sbb[:].rearrange("p (b w) -> p b w", w=2 * BODY)).then_inc(stored, 16)
                sp.wait_ge(stored, r * 32 + 32)
                settle(sp, c)

        @block.vector
        def _(ve):
            v = nc.vector
            lk = link(ve, dve)
            lk(v.memset(ii[:, 0, :, :], 0))
            v.memset(ii[:, 1, :, :], -1).then_inc(filled, 1)
            ve.wait_ge(loaded, 16 * 6)
            ve.wait_ge(filled, 1)
            lk(v.tensor_copy(srcf[:], ii[:, 0, :, :]))
            lk(v.tensor_copy(dstf[:], ii[:, 1, :, :]))
            lk(v.tensor_scalar(low[:], dstf[:], 0.0, FAR, ALU.is_lt, ALU.mult))
            lk(v.tensor_tensor(low[:], low[:], dstf[:], ALU.add))
            lk(v.tensor_reduce(lo[:], low[:], AX, ALU.min))
            lk(v.tensor_reduce(hi[:], dstf[:], AX, ALU.max))
            lk(v.tensor_copy(lo_i[:], lo[:]))
            lk(v.tensor_copy(hi_i[:], hi[:]))
            lk(v.tensor_single_scalar(lo_i[:], lo_i[:], 7, ALU.arith_shift_right))
            lk(v.tensor_single_scalar(hi_i[:], hi_i[:], 7, ALU.arith_shift_right))
            lk(v.tensor_copy(lo[:], lo_i[:]))
            lk(v.tensor_copy(hi[:], hi_i[:]))
            lk(v.tensor_tensor(cnt[:], hi[:], lo[:], ALU.subtract))
            v.tensor_scalar(cnt[:], cnt[:], 1.0, 0.0, ALU.add, ALU.max).then_inc(got, 1)
            ve.wait_ge(prefix, 1)
            lk(v.tensor_copy(start[:], ps[0][:, 0:CB]))
            lk(v.tensor_copy(tot[:], ps[0][:, CB:2 * CB]))
            for k in range(1, CB):
                lk(v.tensor_tensor(start[:, k:k + 1], start[:, k:k + 1], tot[:, k - 1:k], ALU.add))
                lk(v.tensor_tensor(tot[:, k:k + 1], tot[:, k:k + 1], tot[:, k - 1:k], ALU.add))
            lk(v.tensor_tensor(end[:], start[:], cnt[:], ALU.add))
            lk(v.tensor_tensor(rel[:], lo[:], start[:], ALU.subtract))
            lk(v.tensor_copy(relb[:], bcast(rel[:], P)))
            lk(v.tensor_scalar(m1[0:1, 0:1], tot[0:1, CB - 1:CB], float(BODY - 1), None, ALU.add))
            lk(v.tensor_scalar(m1[0:1, 1:2], tot[0:1, CB - 1:CB], float(2 * BODY - 1 + ROUND - 1), None, ALU.add))
            lk(v.tensor_copy(c.loops[0:1, 0:2], m1[0:1, 0:2]))
            lk(v.tensor_single_scalar(c.loops[0:1, 0:1], c.loops[0:1, 0:1], BODY.bit_length() - 1, ALU.arith_shift_right))
            lk(v.tensor_single_scalar(c.loops[0:1, 1:2], c.loops[0:1, 1:2], ROUND.bit_length() - 1, ALU.arith_shift_right))
            v.tensor_copy(jcur[:], c.pair_no[:]).then_inc(ready, 1)
            ve.wait_ge(ready, 1)
            rounds = ve.value_load(c.loops[0:1, 1:2], min_val=1, max_val=MAX_ROUNDS)
            per = CB + 12
            n0 = lk.count[0]
            with ve.Fori(0, rounds) as r:
                ll = link(ve, dve, r, per, n0)
                for k in range(CB):
                    ll(v.tensor_scalar(pick[:, k, :], jcur[:], start[:, k:k + 1], None, ALU.is_ge))
                for k in range(CB):
                    v.scalar_tensor_tensor(pick[:, k, :], jcur[:], end[:, k:k + 1], pick[:, k, :], ALU.is_lt, ALU.mult).then_inc(chosen, 1)
                ve.wait_ge(summed, r + 1)
                ll(v.tensor_copy(val[:], ps[3][:]))
                ll(v.tensor_tensor(tl[:], jcur[:], val[:], ALU.mult))
                ll(v.tensor_tensor(tl[:], tl[:], ps[2][:], ALU.add))
                ll(v.scalar_tensor_tensor(dr[:], tl[:], -float(P), ps[1][:], ALU.mult, ALU.add))
                ll(v.tensor_scalar(m1[:], val[:], FAR, -FAR, ALU.mult, ALU.add))
                ll(v.tensor_tensor(dr[:], dr[:], m1[:], ALU.add))
                ll(v.tensor_copy(ga[:, :, 0:GROUP], four(ps[0][:])))
                ll(v.tensor_copy(ga[:, :, GROUP:2 * GROUP].bitcast(F32), four(dr[:])))
                ll(v.tensor_copy(gb[:, :, GROUP:2 * GROUP], four(tl[:])))
                ll(v.tensor_scalar(m1[:], dr[:], 0.0, None, ALU.is_ge))
                ll(v.scalar_tensor_tensor(m1[:], dr[:], float(P) - 0.5, m1[:], ALU.is_lt, ALU.mult))
                ll(v.tensor_scalar(jcur[:], jcur[:], float(ROUND), None, ALU.add))
                v.tensor_scalar(gb[:, :, 0:GROUP].bitcast(F32), four(m1[:]), -LOW, LOW, ALU.mult, ALU.add).then_inc(staged, 1)
                ve.wait_ge(stored, r * 32 + 32)
                assert ll.count[0] == per, ll.count

        @block.tensor
        def _(pe):
            pe.wait_ge(got, 1)
            nc.tensor.matmul(ps[0][:, 0:CB], c.after[:], cnt[:], start=True, stop=True)
            nc.tensor.matmul(ps[0][:, CB:2 * CB], c.ones[:], cnt[:], start=True, stop=True).then_inc(prefix, 1)
            pe.wait_ge(ready, 1)
            rounds = pe.value_load(c.loops[0:1, 1:2], min_val=1, max_val=MAX_ROUNDS)
            with pe.Fori(0, rounds) as r:
                pe.wait_ge(chosen, CB * r + CB)
                for q in range(4):
                    for k in range(CB):
                        w = (srcf[:, k, :], dstf[:, k, :], relb[:, k, :], c.ones[:])[q]
                        last = nc.tensor.matmul(ps[q][:], w, pick[:, k, :], start=(k == 0), stop=(k == CB - 1))
                last.then_inc(summed, 1)


def turned(nc, s, c, name, weights):
    loaded, done, copied = s(name + "_loaded"), s(name + "_turned"), s(name + "_copied")
    jobs = []
    for src, n_out, dst, col in weights:
        for r in range(n_out // P):
            jobs.append((len(jobs), src[r * P:(r + 1) * P, :], dst, col + r * P))
    with ExitStack() as x:
        raw = x.enter_context(nc.sbuf_tensor(name + "_raw", [P, len(jobs), D], F32))
        ps = x.enter_context(nc.psum_tensor(name + "_ps", [P, 2, 512], F32))
        block = x.enter_context(nc.Block())

        @block.sync
        def _(sp):
            for n, src, _, _ in jobs:
                sp.dma_start(raw[:, n, :], src).then_inc(loaded, 16)

        @block.tensor
        def _(pe):
            pe.wait_ge(loaded, 16 * len(jobs))
            for n, _, _, _ in jobs:
                if n >= 2:
                    pe.wait_ge(copied, n - 1)
                for b in range(2):
                    last = nc.tensor.transpose(ps[:, n % 2, b * P:(b + 1) * P], raw[:, n, b * P:(b + 1) * P], c.ident[:])
                last.then_inc(done, 1)

        @block.vector
        def _(ve):
            for n, _, dst, col in jobs:
                ve.wait_ge(done, n + 1)
                nc.vector.tensor_copy(dst[:, :, col:col + P], ps[:, n % 2, 0:D].rearrange("p (b o) -> p b o", b=2)).then_inc(copied, 1)


def stats(nc, s, name, x, mv):
    dve, act = s(name + "_dve"), s(name + "_act")
    with nc.sbuf_tensor(name + "_bn", [P, T, 6], F32) as bn, nc.sbuf_tensor(name + "_sd", [P, T], F32) as sd, nc.Block() as block:

        @block.vector
        def _(ve):
            v = nc.vector
            for t in range(T):
                v.bn_stats(bn[:, t, :], x[:, t, :]).then_inc(dve, 1)
            for t in range(T):
                ve.wait_ge(dve, t + 1)
                v.bn_aggr(mv[:, t, :], bn[:, t, :]).then_inc(dve, 1)
            ve.wait_ge(dve, 2 * T)
            v.tensor_scalar(sd[:], mv[:, :, 1], LN_EPS, None, ALU.add).then_inc(dve, 1)
            ve.wait_ge(act, 1)
            v.reciprocal(mv[:, :, 1], sd[:]).then_inc(dve, 1)

        @block.scalar
        def _(ac):
            ac.wait_ge(dve, 2 * T + 1)
            nc.scalar.activation(sd[:], sd[:], ACT.Sqrt).then_inc(act, 1)


def uses(u, slots, unroll):
    same = [w for w in range(unroll) if w % slots == u % slots]
    return same.index(u), len(same)


def project(nc, s, c, name, kin, weight, parts, fill, take_dve, take_act, links, store=None):
    rows_ready, turned_s, copied, product, act_done, dve_done, chain = (
        s(name + "_" + w) for w in ("rows", "turned", "copied", "product", "act", "dve", "chain"))
    stored = [s(f"{name}_stored{n}") for n in range(2)]
    steps = [(u, u % 2) for u in range(UN)]
    made = lambda i, u: i * UN + u + 1 + UN
    free = lambda i, u: i * UN + u + 1 + UN - back(u, 2, UN)
    with ExitStack() as x:
        row = x.enter_context(nc.sbuf_tensor(name + "_row", [P, 2, kin * P], F32))
        rowT = x.enter_context(nc.sbuf_tensor(name + "_rowT", [P, 2, kin * P], F32))
        ps_t = x.enter_context(nc.psum_tensor(name + "_ps_t", [P, 2, 512], F32))
        ps = [x.enter_context(nc.psum_tensor(f"{name}_ps{n}", [P, 512], F32)) for n in range(2 * len(parts))]
        block = x.enter_context(nc.Block())
        bank = lambda slot: (lambda n: ps[slot * len(parts) + n])

        @block.vector
        def _(ve):
            ve.sem_inc(rows_ready, UN)
            ve.sem_inc(dve_done, UN)
            with ve.Fori(0, T // UN) as i:
                lk = link(ve, chain, i, links * UN)

                def take(u):
                    ve.wait_ge(product, made(i, u))
                    take_dve(i * UN + u, bank(u % 2), lk).then_inc(dve_done, 1)

                for u, slot in steps:
                    ve.wait_ge(turned_s, free(i, u))
                    fill(row[:, slot, :], i * UN + u, lk).then_inc(rows_ready, 1)
                    if u:
                        take(u - 1)
                take(UN - 1)
                assert lk.count[0] == links * UN, lk.count

        @block.tensor
        def _(pe):
            pe.sem_inc(turned_s, UN)
            pe.sem_inc(product, UN)
            with pe.Fori(0, T // UN) as i:
                for u, slot in steps:
                    pe.wait_ge(rows_ready, made(i, u))
                    pe.wait_ge(copied, free(i, u))
                    for b in range(kin):
                        last = nc.tensor.transpose(ps_t[:, slot, b * P:(b + 1) * P], row[:, slot, b * P:(b + 1) * P], c.ident[:])
                    last.then_inc(turned_s, 1)
                    pe.wait_ge(copied, made(i, u))
                    if take_act:
                        pe.wait_ge(act_done, free(i, u))
                    pe.wait_ge(dve_done, free(i, u))
                    for m, (col, w) in enumerate(parts):
                        for b in range(kin):
                            last = nc.tensor.matmul(bank(slot)(m)[:, 0:w], rowT[:, slot, b * P:(b + 1) * P],
                                                    weight[:, b, col:col + w], start=(b == 0), stop=(b == kin - 1))
                    last.then_inc(product, 1)

        @block.scalar
        def _(ac):
            ac.sem_inc(copied, UN)
            ac.sem_inc(act_done, UN)
            with ac.Fori(0, T // UN) as i:
                def take(u):
                    ac.wait_ge(product, made(i, u))
                    if store:
                        before, per = uses(u, 2, UN)
                        ac.wait_ge(stored[u % 2], (i * per + before + 1) * 16)
                    take_act(i * UN + u, bank(u % 2), u % 2).then_inc(act_done, 1)

                for u, slot in steps:
                    ac.wait_ge(turned_s, made(i, u))
                    ac.wait_ge(product, free(i, u))
                    nc.scalar.copy(rowT[:, slot, :], ps_t[:, slot, 0:kin * P]).then_inc(copied, 1)
                    if u and take_act:
                        take(u - 1)
                if take_act:
                    take(UN - 1)

        if store:
            @block.sync
            def _(sp):
                dram, out = store
                for slot in range(2):
                    sp.sem_inc(stored[slot], 16)
                with sp.Fori(0, T // UN) as i:
                    for u, slot in steps:
                        sp.wait_ge(act_done, made(i, u))
                        settle(sp, c)
                        sp.dma_start(dram[bass.ds((i * UN + u) * P, P), :], out[:, slot, :]).then_inc(stored[slot], 16)
                for slot in range(2):
                    sp.wait_ge(stored[slot], 16 * (1 + T // UN * uses(slot, 2, UN)[1]))


H0, HD = 8, 32
QUAD = 17 * HD
FEAT = QUAD + HD + 1
BLOCKS = [(b * P, min(P, FEAT - b * P)) for b in range(-(-FEAT // P))]
NB = len(BLOCKS)
WRAP = HD + 16
MIX_SCALE = float(HD) ** 0.25
NORM_EPS = 1e-12


def shifted(buf, h):
    a = buf[:, h, :]
    step = a.ap[0]
    return (bass.AP(a.tensor, a.offset, [step, [1, 17], [1, HD]]), bass.AP(a.tensor, a.offset, [step, [0, 17], [1, HD]]))


def layer0_project(nc, s, c, g):
    with nc.sbuf_tensor("p0_wt", [P, 2, 2 * D + 3 * D], F32) as wt:
        turned(nc, s, c, "w0", [(g.w1_l, D, wt, 0), (g.w1_r, D, wt, D), (g.w_qkv[2 * D:3 * D, :], D, wt, 2 * D),
                                (g.w_qkv[0:2 * D, :], 2 * D, wt, 3 * D)])
        with ExitStack() as x:
            sb = lambda n, sh: x.enter_context(nc.sbuf_tensor("p0_" + n, sh, F32))
            yout, sq, ss = sb("yout", [P, 2, D]), sb("sq", [P, 2 * D]), sb("ss", [P, T, 2 * H0])
            xs, mv = g.x, sb("mv", [P, T, 2])
            bias1, bias_qkv = sb("bias1", [P, D]), sb("bias_qkv", [P, 3 * D])
            pre, post = sb("pre", [P, 2 * H0]), sb("post", [P, 2 * H0])
            loaded, filled, dve, act = s("p0_loaded"), s("p0_filled"), s("p0_dve2"), s("p0_act2")
            with nc.Block() as block:
                @block.vector
                def _(ve):
                    nc.vector.memset(xs[:, T - 1, :], 0.0).then_inc(filled, 1)

                @block.sync
                def _(sp):
                    sp.dma_start(bias1[:], g.b1[None, :].to_broadcast([P, D])).then_inc(loaded, 16)
                    sp.dma_start(bias_qkv[:], g.b_qkv[None, :].to_broadcast([P, 3 * D])).then_inc(loaded, 16)
                    sp.dma_start(post[:, 0:H0], g.temperature[None, :].to_broadcast([P, H0])).then_inc(loaded, 16)
                    sp.wait_ge(filled, 1)
                    full = (T - 1) * P
                    sp.dma_start(xs[:, 0:T - 1, :], g.x_in[0:full, :].rearrange("(t p) f -> p t f", p=P)).then_inc(loaded, 16)
                    sp.dma_start(xs[0:TAIL, T - 1, :], g.x_in[full:N, :]).then_inc(loaded, 16)
                    sp.wait_ge(loaded, 16 * 5)
            stats(nc, s, "ln0", xs, mv)

            def fill(row, k, lk):
                mean_rstd = tile(mv, k)
                return nc.vector.tensor_scalar(row, tile(xs, k), mean_rstd[:, 0:1], mean_rstd[:, 1:2], ALU.subtract, ALU.mult)

            def take_dve(k, bank, lk):
                v = nc.vector
                v.tensor_tensor(tile(g.own, k), bank(1)[:, 0:D], bias1[:], ALU.add)
                lk(v.tensor_tensor(tile(g.qk, k), bank(2)[:], bias_qkv[:, 0:2 * D], ALU.add))
                lk(v.tensor_tensor(sq[:], tile(g.qk, k), tile(g.qk, k), ALU.mult))
                lk(v.tensor_reduce(tile(ss, k), sq[:].rearrange("p (h d) -> p h d", d=HD), AX, ALU.add))
                return v.tensor_tensor(tile(g.v1, k).rearrange("p (h e) -> p h e", h=H0)[:, :, 0:HD],
                                       bank(1)[:, D:2 * D].rearrange("p (h e) -> p h e", h=H0),
                                       bias_qkv[:, 2 * D:3 * D].rearrange("p (h e) -> p h e", h=H0), ALU.add)

            def take_act(k, bank, slot):
                return nc.scalar.copy(yout[:, slot, :], bank(0)[:, 0:D])

            project(nc, s, c, "p0", 2, wt, [(0, D), (D, 2 * D), (3 * D, 2 * D)], fill, take_dve, take_act, 3,
                    store=(g.table_y, yout))
            with nc.Block() as block:
                @block.vector
                def _(ve):
                    v = nc.vector
                    lk = link(ve, dve)
                    v.memset(g.v1[:].rearrange("p t (h e) -> p (t h) e", h=H0)[:, :, HD:HD + 1], 1.0)
                    v.memset(pre[:, 0:H0], MIX_SCALE ** 2)
                    v.memset(pre[:, H0:2 * H0], 1.0)
                    v.tensor_scalar(post[:, 0:H0], post[:, 0:H0], MIX_SCALE ** 2, None, ALU.mult)
                    lk(v.memset(post[:, H0:2 * H0], MIX_SCALE))
                    wide = lambda a: a[:].unsqueeze(1).to_broadcast([P, T, 2 * H0])
                    lk(v.tensor_tensor(ss[:], ss[:], wide(pre), ALU.mult))
                    ve.wait_ge(act, 1)
                    lk(v.tensor_scalar(ss[:], ss[:], NORM_EPS, None, ALU.max))
                    lk(v.reciprocal(ss[:], ss[:]))
                    lk(v.tensor_tensor(ss[:], ss[:], wide(post), ALU.mult))
                    for t in range(0, T, UN):
                        qk = g.qk[:, t:t + UN, :].rearrange("p t (h d) -> p (t h) d", d=HD)
                        v.tensor_tensor(qk, qk, bcast(ss[:, t:t + UN, :].rearrange("p t h -> p (t h)"), HD), ALU.mult)
                    lk(v.tensor_scalar(g.v1[:, T - 1, :], g.v1[:, T - 1, :], c.valid[:, T - 1:T], None, ALU.mult))

                @block.scalar
                def _(ac):
                    ac.wait_ge(dve, 2)
                    nc.scalar.activation(ss[:], ss[:], ACT.Sqrt).then_inc(act, 1)


AHEAD = 4
UNITS = 512 // (HD + 1)
MBANKS = -(-H0 * NB // UNITS)
SLOTS = 4


def sage(nc, s, c, name, table, width, total, g, pre, beside, ring):
    half, quarter = BODY // 2, BODY // GROUP
    got, copied_a = s(name + "_got"), s(name + "_index")
    gathered = [s(f"{name}_gathered{u}") for u in range(BODY)]
    hot_s, summed, added, ones_s = s(name + "_onehot"), s(name + "_summed"), s(name + "_added"), s(name + "_ones")
    with ExitStack() as x:
        rows_ = x.enter_context(nc.sbuf_tensor(name + "_rows", [P, BODY, width], F32))
        hot = x.enter_context(nc.sbuf_tensor(name + "_hot", [P, BODY, P], F32))
        ta = x.enter_context(nc.sbuf_tensor(name + "_ta", [P, AHEAD * 2 * BODY], I32))
        tb = x.enter_context(nc.sbuf_tensor(name + "_tb", [1, AHEAD * 2 * BODY], I32))
        index = x.enter_context(nc.sbuf_tensor(name + "_ix", [P, BODY], I32))
        ps = [x.enter_context(nc.psum_tensor(f"{name}_ps{n}", [P, 512], F32)) for n in range(ring)]
        block = x.enter_context(nc.Block())
        made = lambda i, u: (i + 1) * BODY + u + 1
        added_by = lambda i, u: (i + AHEAD) * BODY + u + 1
        slot = lambda i: (i % AHEAD) * (2 * BODY)

        def loops(eng, body, extra):
            n = eng.value_load(c.loops[0:1, 0:1], min_val=T + 1, max_val=MAX_BODIES)
            with eng.Fori(0, T) as i:
                body(i, extra)
            with eng.Fori(T, n) as i:
                body(i, None)

        @block.sync
        def _(sp):
            def body(i, extra):
                sp.wait_ge(added, added_by(i - AHEAD, BODY - 1))
                settle(sp, c)
                sp.dma_start(ta[:, bass.ds(slot(i), 2 * BODY)], g.table_a[bass.ds(i, 1), :, :].rearrange("b p w -> (b p) w")).then_inc(got, 16)
                sp.dma_start(tb[:, bass.ds(slot(i), 2 * BODY)], g.table_b[bass.ds(i, 1), 0:1, :].rearrange("b p w -> (b p) w")).then_inc(got, 16)
                sp.wait_ge(got, i * 32 + 32)
                settle(sp, c)
            loops(sp, body, None)

        @block.gpsimd
        def _(pool):
            pool.sem_inc(copied_a, quarter)

            def body(i, extra):
                pool.wait_ge(got, i * 32 + 32)
                settle(pool, c)
                for q in range(quarter):
                    pool.wait_ge(summed, made(i, q * GROUP + GROUP - 1) - BODY)
                    settle(pool, c)
                    nc.gpsimd.tensor_copy(index[:, q * GROUP:(q + 1) * GROUP], ta[:, bass.ds(slot(i) + q * 2 * GROUP, GROUP)]).then_inc(copied_a, 1)
                    pool.wait_ge(copied_a, (i + 1) * quarter + q + 1)
                    settle(pool, c)
                    for u in range(q * GROUP, (q + 1) * GROUP):
                        nc.gpsimd.indirect_dma_start(rows_[:, u, 0:D], None, table,
                                                     bass.IndirectOffsetOnAxis(ap=index[:, u:u + 1], axis=0)).then_inc(gathered[u], 16)
            loops(pool, body, None)

        @block.vector
        def _(ve):
            v = nc.vector
            ve.sem_inc(hot_s, quarter)
            ve.sem_inc(added, AHEAD * BODY)
            if width > D:
                v.memset(rows_[:, :, D:width], 1.0).then_inc(ones_s, 1)
            if "dve" in pre:
                pre["dve"](ve)

            def one_hot(i, q):
                ve.wait_ge(summed, made(i, q * GROUP + GROUP - 1) - BODY)
                places = ta[:, bass.ds(slot(i) + q * 2 * GROUP + GROUP, GROUP)].bitcast(F32)
                v.tensor_tensor(hot[:, q * GROUP:(q + 1) * GROUP, :], c.col[:].unsqueeze(1).to_broadcast([P, GROUP, P]),
                                bcast(places, P), ALU.is_equal).then_inc(hot_s, 1)

            def body(i, extra):
                ve.wait_ge(got, i * 32 + 32)
                settle(ve, c)
                one_hot(i, 0)
                one_hot(i, 1)
                for u in range(BODY):
                    q = u // GROUP
                    if u % GROUP == 0 and 1 <= q and q + 1 < quarter:
                        one_hot(i, q + 1)
                    t = ve.value_load(tb[0:1, bass.ds(slot(i) + q * 2 * GROUP + GROUP + u % GROUP, 1)], min_val=0, max_val=T - 1)
                    ve.wait_ge(summed, made(i, u))
                    ve.wait_ge(added, added_by(i, u) - 1)
                    v.tensor_tensor(tile(total, t), tile(total, t), ps[u % ring][:, 0:width], ALU.add).then_inc(added, 1)
                    if extra:
                        extra["dve"](ve, i, u)
            loops(ve, body, beside)

        @block.tensor
        def _(pe):
            pe.sem_inc(summed, BODY)
            if width > D:
                pe.wait_ge(ones_s, 1)
            if "pe" in pre:
                pre["pe"](pe)

            def body(i, extra):
                for u in range(BODY):
                    if u % GROUP == 0:
                        pe.wait_ge(hot_s, (i + 1) * quarter + u // GROUP + 1)
                    pe.wait_ge(gathered[u], i * 16 + 16)
                    pe.wait_ge(added, added_by(i, u) - back(u, ring, BODY))
                    nc.tensor.matmul(ps[u % ring][:, 0:width], hot[:, u, :], rows_[:, u, :], start=True, stop=True).then_inc(summed, 1)
                    if extra:
                        extra["pe"](pe, i, u)
            loops(pe, body, beside)

        if "act" in beside:
            @block.scalar
            def _(ac):
                pre["act"](ac)
                with ac.Fori(0, T) as i:
                    for u in range(BODY):
                        beside["act"](ac, i, u)


def features(nc, s, c, name, g, column, x):
    wrapped, made, linear, used = s(name + "_wrapped"), s(name + "_features"), s(name + "_linear"), s(name + "_used")
    vals = x.enter_context(nc.sbuf_tensor(name + "_vals", [P, H0, WRAP], F32))
    feat = x.enter_context(nc.sbuf_tensor(name + "_feat", [P, SLOTS, FEAT], F32))
    count = lambda i, h: (i + 1) * H0 + h + 1

    def act_start(ac):
        ac.sem_inc(linear, H0)

    def dve_start(ve):
        nc.vector.memset(feat[:, :, FEAT - 1:FEAT], 1.0).then_inc(made, H0)

    def wrap(ac, i):
        ac.wait_ge(made, (i + 1) * H0)
        ac.wait_ge(linear, (i + 1) * H0)
        heads = tile(g.qk, i)[:, column:column + D].rearrange("p (h d) -> p h d", d=HD)
        nc.scalar.copy(vals[:, :, 0:HD], heads).then_inc(wrapped, 1)
        nc.scalar.copy(vals[:, :, HD:WRAP], heads[:, :, 0:WRAP - HD]).then_inc(wrapped, 1)

    def lin(ac, i, h):
        ac.wait_ge(wrapped, i * 2 + 2)
        ac.wait_ge(used, count(i, h) - SLOTS)
        nc.scalar.copy(feat[:, h % SLOTS, QUAD:QUAD + HD], vals[:, h, 0:HD]).then_inc(linear, 1)

    def quad(ve, i, h):
        ve.wait_ge(wrapped, i * 2 + 2)
        ve.wait_ge(used, count(i, h) - SLOTS)
        other, own = shifted(vals, h)
        nc.vector.tensor_tensor(feat[:, h % SLOTS, 0:QUAD].rearrange("p (s i) -> p s i", i=HD), own, other, ALU.mult).then_inc(made, 1)

    def ready(pe, i, h):
        pe.wait_ge(made, count(i, h))
        pe.wait_ge(linear, count(i, h))
    return feat, used, act_start, dve_start, wrap, lin, quad, ready


def sage1_and_keys(nc, s, c, g):
    with ExitStack() as x:
        feat, used, act_start, dve_start, wrap, lin, quad, ready = features(nc, s, c, "kf", g, D, x)
        zero = x.enter_context(nc.sbuf_tensor("kf_zero", [1, P + 512], F32))
        ps_m = [x.enter_context(nc.psum_tensor(f"kf_m{n}", [P, 512], F32)) for n in range(MBANKS)]
        zeroed, weights, cleared = s("kf_zeroed"), s("kf_weights"), s("kf_cleared")
        place = lambda h, b: (ps_m[(h * NB + b) // UNITS], (h * NB + b) % UNITS * (HD + 1))

        def dve_pre(ve):
            nc.vector.memset(zero[:], 0.0).then_inc(zeroed, 1)
            nc.vector.memset(g.agg[:], 0.0).then_inc(cleared, 1)
            ve.wait_ge(cleared, 1)
            dve_start(ve)

        def pe_pre(pe):
            pe.sem_inc(used, H0)
            pe.wait_ge(zeroed, 1)
            pe.wait_ge(made0, H0)
            for m in ps_m:
                nc.tensor.matmul(m[:], zero[:, 0:P], zero[:, P:P + 512], start=True, stop=False, skip_group_check=True)

        def pe_beside(pe, i, u):
            if u % 2:
                h = u // 2
                ready(pe, i, h)
                for b, (f, w) in enumerate(BLOCKS):
                    m, col = place(h, b)
                    last = nc.tensor.matmul(m[0:w, col:col + HD + 1], feat[:, h % SLOTS, f:f + w],
                                            tile(g.v1, i)[:, h * (HD + 1):(h + 1) * (HD + 1)],
                                            start=False, stop=False, skip_group_check=True)
                last.then_inc(used, 1)

        def act_beside(ac, i, u):
            if u == 0:
                wrap(ac, i)
            if u % 2 == 0:
                lin(ac, i, u // 2)

        def dve_beside(ve, i, u):
            if u % 2 == 0:
                quad(ve, i, u // 2)

        made0 = s.known["kf_features"]
        sage(nc, s, c, "sage1", g.table_y, D + 1, g.agg, g, dict(dve=dve_pre, pe=pe_pre, act=act_start),
             dict(dve=dve_beside, pe=pe_beside, act=act_beside), 3)
        with nc.Block() as block:
            @block.vector
            def _(ve):
                v = nc.vector
                lk = link(ve, weights)
                w = g.mix_w[:].rearrange("p (h b) -> p h b", b=NB)
                lk(v.memset(w[:, :, 0:NB - 1], 1.0 / N))
                v.memset(w[0:HD, :, 0:1], 0.5 / N)
                lk(v.memset(w[0:HD, :, NB - 1:NB], 0.5 / N))
                lk(v.memset(w[HD:2 * HD, :, NB - 1:NB], MIX_SCALE ** 2 / N))
                lk(v.memset(w[2 * HD:P, :, NB - 1:NB], MIX_SCALE ** 4 / N))
                for n in range(MBANKS):
                    units = min(UNITS, H0 * NB - n * UNITS)
                    v.tensor_tensor(g.mix[:, n * UNITS:n * UNITS + units, :],
                                    ps_m[n][:, 0:units * (HD + 1)].rearrange("p (n e) -> p n e", e=HD + 1),
                                    bcast(g.mix_w[:, n * UNITS:n * UNITS + units], HD + 1), ALU.mult)


def sage2_and_queries(nc, s, c, g):
    with ExitStack() as x:
        feat, used, act_start, dve_start, wrap, lin, quad, ready = features(nc, s, c, "qf", g, 0, x)
        featT = x.enter_context(nc.sbuf_tensor("qf_featT", [P, 2, NB * P], F32))
        inv = x.enter_context(nc.sbuf_tensor("qf_inv", [P, H0], F32))
        ps_t = [x.enter_context(nc.psum_tensor(f"qf_t{n}", [P, 512], F32)) for n in range(4)]
        ps_y = x.enter_context(nc.psum_tensor("qf_y", [P, 512], F32))
        copied, made_y, taken, inv_s, cleared = s("qf_copied"), s("qf_made_y"), s("qf_taken"), s("qf_inv_s"), s("qf_cleared")
        count = lambda i, h: (i + 1) * H0 + h + 1

        def dve_pre(ve):
            nc.vector.memset(g.agg[:, :, 0:D], 0.0).then_inc(cleared, 1)
            ve.wait_ge(cleared, 1)
            ve.sem_inc(taken, 1)
            dve_start(ve)

        def pe_pre(pe):
            pe.sem_inc(used, H0)
            pe.sem_inc(made_y, H0)

        def turn(pe, i, h):
            ready(pe, i, h)
            pe.wait_ge(copied, count(i, h) - 2)
            for b, (f, w) in enumerate(BLOCKS):
                out = ps_t[2 * (h % 2)][:, b * P:(b + 1) * P] if b < NB - 1 else ps_t[2 * (h % 2) + 1][0:w, 0:P]
                last = nc.tensor.transpose(out, feat[:, h % SLOTS, f:f + w], c.ident[:])
            last.then_inc(used, 1)

        def times_mix(pe, i, h):
            pe.wait_ge(copied, count(i, h))
            if h == 0:
                pe.wait_ge(taken, i + 1)
            for b, (f, w) in enumerate(BLOCKS):
                last = nc.tensor.matmul(ps_y[:, h * (HD + 1):(h + 1) * (HD + 1)], featT[0:w, h % 2, b * P:(b + 1) * P],
                                        g.mix[0:w, h * NB + b, :], start=(b == 0), stop=(b == NB - 1))
            last.then_inc(made_y, 1)

        def pe_beside(pe, i, u):
            if u % 2 == 0:
                turn(pe, i, u // 2)
            elif u > 1:
                times_mix(pe, i, u // 2 - 1)
            if u == BODY - 1:
                times_mix(pe, i, H0 - 1)

        def act_pre(ac):
            act_start(ac)
            ac.sem_inc(copied, H0)

        def act_beside(ac, i, u):
            if u == 0:
                wrap(ac, i)
            if u % 2 == 0:
                lin(ac, i, u // 2)
            else:
                h = u // 2
                ac.wait_ge(used, count(i, h))
                ac.wait_ge(made_y, count(i, h) - 2)
                w = BLOCKS[-1][1]
                nc.scalar.copy(featT[:, h % 2, 0:(NB - 1) * P], ps_t[2 * (h % 2)][:])
                nc.scalar.copy(featT[0:w, h % 2, (NB - 1) * P:NB * P], ps_t[2 * (h % 2) + 1][0:w, 0:P]).then_inc(copied, 1)

        def dve_beside(ve, i, u):
            if u % 2 == 0:
                quad(ve, i, u // 2)
            if u == BODY - 1:
                ve.wait_ge(made_y, (i + 2) * H0)
                y = ps_y[:, 0:H0 * (HD + 1)].rearrange("p (h e) -> p h e", e=HD + 1)
                nc.vector.reciprocal(inv[:], y[:, :, HD]).then_inc(inv_s, 1)
                ve.wait_ge(inv_s, i + 1)
                nc.vector.tensor_tensor(tile(g.qk, i)[:, 0:D].rearrange("p (h e) -> p h e", e=HD), y[:, :, 0:HD],
                                        bcast(inv[:], HD), ALU.mult).then_inc(taken, 1)

        sage(nc, s, c, "sage2", g.table_y, D, g.agg[:, :, 0:D], g, dict(dve=dve_pre, pe=pe_pre, act=act_pre),
             dict(dve=dve_beside, pe=pe_beside, act=act_beside), 3)


def sage1_finish(nc, s, c, g):
    with ExitStack() as x:
        sb = lambda n, sh: x.enter_context(nc.sbuf_tensor("p1_" + n, sh, F32))
        wt, yout, bias2, mid = sb("wt", [P, 2, 2 * D]), sb("yout", [P, 2, D]), sb("bias2", [P, D]), sb("mid", [P, 2, D])
        dve, loaded = s("p1_dve2"), s("p1_loaded")
        turned(nc, s, c, "w1", [(g.w2_l, D, wt, 0), (g.w2_r, D, wt, D)])
        with nc.Block() as block:
            @block.sync
            def _(sp):
                sp.dma_start(bias2[:], g.b2[None, :].to_broadcast([P, D])).then_inc(loaded, 16)
                sp.wait_ge(loaded, 16)

            @block.vector
            def _(ve):
                lk = link(ve, dve)
                lk(nc.vector.tensor_scalar(g.inv_deg[:], g.agg[:, :, D], 1.0, None, ALU.max))
                lk(nc.vector.reciprocal(g.inv_deg[:], g.inv_deg[:]))

        def fill(row, k, lk):
            v = nc.vector
            lk(v.scalar_tensor_tensor(row, tile(g.agg, k)[:, 0:D], tile_col(g.inv_deg, k), tile(g.own, k), ALU.mult, ALU.add))
            return v.tensor_scalar(row, row, 0.0, None, ALU.max)

        def take_dve(k, bank, lk):
            return nc.vector.tensor_tensor(tile(g.own, k), bank(1)[:, 0:D], bias2[:], ALU.add)

        def take_act(k, bank, slot):
            return nc.scalar.copy(yout[:, slot, :], bank(0)[:, 0:D])

        project(nc, s, c, "p1", 2, wt, [(0, D), (D, D)], fill, take_dve, take_act, 1, store=(g.table_y, yout))


def tile_col(buf, k):
    return buf[:, bass.ds(k, 1)]


def normed(nc, s, name, x, out):
    with nc.sbuf_tensor(name + "_mv", [P, T, 2], F32) as mv:
        stats(nc, s, name, x, mv)
        with nc.Block() as block:
            @block.vector
            def _(ve):
                for t in range(T):
                    nc.vector.tensor_scalar(out[:, t, :], x[:, t, :], mv[:, t, 0:1], mv[:, t, 1:2], ALU.subtract, ALU.mult)


def layer0_join(nc, s, c, g):
    with ExitStack() as x:
        sb = lambda n, sh: x.enter_context(nc.sbuf_tensor("j0_" + n, sh, F32))
        wt, bias = sb("wt", [P, 2, D]), sb("bias", [P, D])
        loaded = s("j0_loaded")
        turned(nc, s, c, "wj", [(g.w_proj, D, wt, 0)])
        with nc.Block() as block:
            @block.sync
            def _(sp):
                sp.dma_start(bias[:], g.b_proj[None, :].to_broadcast([P, D])).then_inc(loaded, 16)
                sp.wait_ge(loaded, 16)

        def fill(row, k, lk):
            return nc.vector.tensor_copy(row, tile(g.qk, k)[:, 0:D])

        def take_dve(k, bank, lk):
            v = nc.vector
            lk(v.scalar_tensor_tensor(tile(g.own, k), tile(g.agg, k)[:, 0:D], tile_col(g.inv_deg, k), tile(g.own, k), ALU.mult, ALU.add))
            v.tensor_tensor(tile(g.x, k), tile(g.x, k), bias[:], ALU.add)
            lk(v.tensor_tensor(tile(g.own, k), tile(g.own, k), bank(0)[:, 0:D], ALU.add))
            return v.tensor_tensor(tile(g.x, k), tile(g.x, k), tile(g.own, k), ALU.add)

        project(nc, s, c, "j0", 2, wt, [(0, D)], fill, take_dve, None, 2)


def route(nc, s, c, name, g, ne, tiles, gate_w, gate_b, renorm):
    r = g.route
    with ExitStack() as x:
        sb = lambda n, sh, d=F32: x.enter_context(nc.sbuf_tensor(f"{name}_{n}", sh, d))
        wg, bg = sb("wg", [P, 2, ne]), sb("bg", [P, ne])
        prob = sb("prob", [P, T, ne])
        loaded = s(name + "_loaded")
        with nc.Block() as block:
            @block.sync
            def _(sp):
                sp.dma_start(wg[:], gate_w.rearrange("(b p) e -> p b e", p=P)).then_inc(loaded, 16)
                sp.dma_start(bg[:], gate_b[None, :].to_broadcast([P, ne])).then_inc(loaded, 16)
                sp.wait_ge(loaded, 32)

        def fill(row, k, lk):
            return nc.vector.tensor_copy(row, tile(g.xn, k))

        def take_dve(k, bank, lk):
            return nc.vector.tensor_tensor(tile(prob, k), bank(0)[:, 0:ne], bg[:], ALU.add)

        project(nc, s, c, name + "g", 2, wg, [(0, ne)], fill, take_dve, None, 0)

        one, two, both = sb("one", [P, T, ne]), sb("two", [P, T, ne]), sb("both", [P, T, ne])
        m, top, which = sb("m", [P, T]), sb("top", [P, T, 8]), sb("which", [P, T, 8], U32)
        whichf, eid = sb("whichf", [P, T, 8]), sb("eid", [P, T, ne])
        tot, run, pos = sb("tot", [P, ne, T]), sb("run", [P, ne, T]), sb("pos", [P, T, ne])
        ones_row = sb("ones_row", [P, ne * T])
        cnt, tl, first, tli, base = (sb(n, [P, ne]) for n in ("cnt", "tl", "first", "tli", "base"))
        cnt_i = sb("cnt_i", [P, ne], I32)
        tno, over, sl = sb("tno", [P, tiles, ne]), sb("over", [P, tiles, ne]), sb("sl", [P, T])
        exf = sb("exf", [P, tiles])
        ps_in, ps_all = (x.enter_context(nc.psum_tensor(f"{name}_{n}", [P, 512], F32)) for n in ("ps_in", "ps_all"))
        dve, act, chosen, counted, made, index, sent = (s(f"{name}_{n}") for n in ("dve", "act", "chosen", "counted", "made", "index", "sent"))
        with nc.Block() as block:
            @block.gpsimd
            def _(pool):
                fl = dict(allow_small_or_imprecise_dtypes=True)
                nc.gpsimd.iota(eid[:], [[0, T], [1, ne]], base=0, channel_multiplier=0, **fl).then_inc(made, 1)
                nc.gpsimd.iota(tno[:], [[1, tiles], [0, ne]], base=0, channel_multiplier=0, **fl).then_inc(made, 1)
                for k, (slot, n) in enumerate([(q, t) for t in range(T) for q in (r.slot1, r.slot2)]):
                    rows_n = P if n < T - 1 else TAIL
                    if k == 0:
                        pool.wait_ge(index, 2)
                    nc.gpsimd.indirect_dma_start(g.sorted_x, bass.IndirectOffsetOnAxis(ap=slot[0:rows_n, n:n + 1], axis=0),
                                                 g.xn[0:rows_n, n, :], None).then_inc(sent, 16)
                pool.wait_ge(sent, 16 * 2 * T)

            @block.scalar
            def _(ac):
                ac.wait_ge(dve, 2)
                nc.scalar.activation(prob[:], prob[:], ACT.Exp).then_inc(act, 1)

            @block.tensor
            def _(pe):
                pe.wait_ge(chosen, 1)
                nc.tensor.matmul(ps_in[:, 0:T * ne], c.after[:], both[:].rearrange("p t e -> p (t e)"), start=True, stop=True)
                nc.tensor.matmul(ps_all[:, 0:T * ne], c.ones[:], both[:].rearrange("p t e -> p (t e)"), start=True, stop=True).then_inc(counted, 1)

            @block.vector
            def _(ve):
                v = nc.vector
                lk = link(ve, dve)
                lk(v.tensor_reduce(m[:], prob[:], AX, ALU.max))
                lk(v.tensor_tensor(prob[:], prob[:], bcast(m[:], ne), ALU.subtract))
                ve.wait_ge(act, 1)
                lk(v.tensor_reduce(m[:], prob[:], AX, ALU.add))
                lk(v.reciprocal(m[:], m[:]))
                lk(v.tensor_tensor(prob[:], prob[:], bcast(m[:], ne), ALU.mult))
                for t in range(T):
                    v.max(top[:, t, :], prob[:, t, :]).then_inc(dve, 1)
                lk.count[0] += T
                ve.wait_ge(dve, lk.count[0])
                for t in range(T):
                    v.max_index(which[:, t, :], top[:, t, :], prob[:, t, :]).then_inc(dve, 1)
                lk.count[0] += T
                ve.wait_ge(dve, lk.count[0])
                lk(v.tensor_copy(whichf[:], which[:]))
                ve.wait_ge(made, 2)
                for e, k in ((one, 0), (two, 1)):
                    lk(v.tensor_tensor(e[:], eid[:], bcast(whichf[:, :, k], ne), ALU.is_equal))
                    lk(v.tensor_tensor(e[:], e[:], bcast(c.valid[:], ne), ALU.mult))
                v.tensor_tensor(both[:], one[:], two[:], ALU.add).then_inc(chosen, 1)
                if renorm:
                    lk(v.tensor_tensor(m[:], top[:, :, 0], top[:, :, 1], ALU.add))
                    lk(v.reciprocal(m[:], m[:]))
                    v.tensor_tensor(r.w1[:], top[:, :, 0], m[:], ALU.mult)
                    v.tensor_tensor(r.w2[:], top[:, :, 1], m[:], ALU.mult)
                else:
                    v.tensor_copy(r.w1[:], top[:, :, 0])
                    v.tensor_copy(r.w2[:], top[:, :, 1])
                ve.wait_ge(counted, 1)
                lk(v.memset(ones_row[:], 1.0))
                lk(v.tensor_copy(tot[:], ps_all[:, 0:T * ne].rearrange("p (t e) -> p e t", e=ne)))
                flat = lambda a: a[:].rearrange("p e t -> p (e t)")
                lk(v.tensor_tensor_scan(flat(run), ones_row[:], flat(tot), 0.0, ALU.mult, ALU.add))
                lk(v.tensor_copy(cnt[:, 0:1], run[:, 0:1, T - 1]))
                lk(v.tensor_tensor(cnt[:, 1:ne], run[:, 1:ne, T - 1], run[:, 0:ne - 1, T - 1], ALU.subtract))
                lk(v.tensor_scalar(tl[:], cnt[:], float(P - 1), None, ALU.add))
                lk(v.tensor_copy(cnt_i[:], tl[:]))
                lk(v.tensor_single_scalar(cnt_i[:], cnt_i[:], 7, ALU.arith_shift_right))
                lk(v.tensor_copy(tl[:], cnt_i[:]))
                lk(v.tensor_tensor_scan(tli[:], ones_row[:, 0:ne], tl[:], 0.0, ALU.mult, ALU.add))
                lk(v.tensor_tensor(first[:], tli[:], tl[:], ALU.subtract))
                lk(v.tensor_tensor(base[:], run[:, :, T - 1], cnt[:], ALU.subtract))
                lk(v.scalar_tensor_tensor(base[:], first[:], float(P), base[:], ALU.mult, ALU.subtract))
                lk(v.tensor_tensor(run[:], run[:], tot[:], ALU.subtract))
                lk(v.tensor_tensor(run[:], run[:], bcast(base[:], T), ALU.add))
                lk(v.tensor_tensor(pos[:], ps_in[:, 0:T * ne].rearrange("p (t e) -> p t e", e=ne), run[:].rearrange("p e t -> p t e"), ALU.add))
                for e, slot in ((one, r.slot1), (two, r.slot2)):
                    lk(v.tensor_tensor(e[:], e[:], pos[:], ALU.mult))
                    lk(v.tensor_reduce(sl[:], e[:], AX, ALU.add))
                    v.tensor_copy(slot[:], sl[:]).then_inc(index, 1)
                lk(v.tensor_tensor(over[:], tno[:], tli[:].unsqueeze(1).to_broadcast([P, tiles, ne]), ALU.is_ge))
                lk(v.tensor_reduce(exf[:], over[:], AX, ALU.add))
                lk(v.tensor_scalar(exf[:], exf[:], float(ne - 1), None, ALU.min))
                lk(v.tensor_copy(r.expert[:, 0:tiles], exf[0:1, :]))


def experts(nc, s, c, name, g, tiles, hidden, w_in, w_out, act, b_in=None, b_out=None):
    HB = hidden // P
    nw = len(w_in)
    with ExitStack() as x:
        sb = lambda n, sh: x.enter_context(nc.sbuf_tensor(f"{name}_{n}", sh, F32))
        wi = [sb(f"wi{n}", [P, 2, 2, hidden]) for n in range(nw)]
        wo = sb("wo", [P, 2, HB, D])
        xin, xT, out = sb("xin", [P, 2, D]), sb("xT", [P, 2, D]), sb("out", [P, 2, D])
        gate, hid = sb("gate", [P, 2, hidden]), sb("hid", [P, 2, hidden])
        bias = sb("bias", [1, 2, hidden + D]) if b_in is not None else None
        ps_t = x.enter_context(nc.psum_tensor(name + "_ps_t", [P, 512], F32))
        ps_h = [[x.enter_context(nc.psum_tensor(f"{name}_ps_h{n}{k}", [P, 512], F32)) for k in range(2)] for n in range(nw)]
        ps_o = [x.enter_context(nc.psum_tensor(f"{name}_ps_o{k}", [P, 512], F32)) for k in range(2)]
        more = 1 if bias is not None else 0
        loaded_x, loaded_in, loaded_out = ([s(f"{name}_loaded_{w}{k}") for k in range(2)] for w in ("x", "in", "out"))
        stored = [s(f"{name}_stored{k}") for k in range(2)]
        turned_s, copied, hidden_s, gated, ready, made, taken = (
            s(f"{name}_{n}") for n in ("turned", "copied", "hidden", "gated", "ready", "made", "taken"))
        block = x.enter_context(nc.Block())

        done = lambda i: i + 1 + 2

        def steps(eng, step):
            step(0, 0, 0, first=True)
            with eng.Fori(0, (tiles - 2) // 2) as j:
                step(2 * j + 1, 1, j)
                step(2 * j + 2, 0, j + 1)
            step(tiles - 1, 1, tiles // 2 - 1, last=True)

        before = lambda k, n: n if k else n - 1
        behind = lambda k, n: n + 1 if k else n

        @block.sync
        def _(sp):
            with sp.Fori(0, tiles // 2) as j:
                for k in range(2):
                    i = 2 * j + k
                    e = sp.value_load(g.route.expert[0:1, bass.ds(i, 1)], min_val=0, max_val=w_out.shape[0] - 1)
                    one = lambda a: a[bass.ds(e, 1)]
                    sp.wait_ge(turned_s, done(i) - 2)
                    settle(sp, c)
                    sp.dma_start(xin[:, k, :], g.sorted_x[bass.ds(i * P, P), :]).then_inc(loaded_x[k], 16)
                    sp.wait_ge(hidden_s, done(i) - 2)
                    settle(sp, c)
                    for n in range(nw):
                        sp.dma_start(wi[n][:, k], one(w_in[n]).rearrange("o (b p) f -> p (o b) f", p=P)).then_inc(loaded_in[k], 16)
                    if more:
                        sp.dma_start(bias[:, k, 0:hidden], one(b_in)).then_inc(loaded_in[k], 16)
                    sp.wait_ge(made, done(i) - 2)
                    settle(sp, c)
                    sp.dma_start(wo[:, k], one(w_out).rearrange("o (b p) f -> p (o b) f", p=P)).then_inc(loaded_out[k], 16)
                    if more:
                        sp.dma_start(bias[:, k, hidden:hidden + D], one(b_out)).then_inc(loaded_out[k], 16)

        @block.tensor
        def _(pe):
            for count in (turned_s, hidden_s, made):
                pe.sem_inc(count, 2)

            def turn(i, k, n):
                pe.wait_ge(loaded_x[k], (n + 1) * 16)
                pe.wait_ge(copied, done(i) - 1)
                for b in range(2):
                    last = nc.tensor.transpose(ps_t[:, b * P:(b + 1) * P], xin[:, k, b * P:(b + 1) * P], c.ident[:])
                last.then_inc(turned_s, 1)

            def hide(i, k, n):
                pe.wait_ge(loaded_in[k], (n + 1) * (16 * (nw + more)))
                pe.wait_ge(copied, done(i))
                pe.wait_ge(ready, done(i) - 2)
                for m in range(nw):
                    for hb in range(HB):
                        o = ps_h[m][k][:, hb * P:(hb + 1) * P]
                        if bias is not None:
                            nc.tensor.matmul(o, bias[:, k, hb * P:(hb + 1) * P], c.ones[0:1, :], start=True, stop=False)
                        for b in range(2):
                            last = nc.tensor.matmul(o, wi[m][:, k, b, hb * P:(hb + 1) * P], xT[:, k, b * P:(b + 1) * P],
                                                    start=(b == 0 and bias is None), stop=(b == 1))
                last.then_inc(hidden_s, 1)

            def give(i, k, n):
                pe.wait_ge(loaded_out[k], (n + 1) * (16 * (1 + more)))
                pe.wait_ge(ready, done(i))
                pe.wait_ge(taken, done(i) - 2)
                o = ps_o[k][:, 0:D]
                if bias is not None:
                    nc.tensor.matmul(o, c.ones[0:1, :], bias[:, k, hidden:hidden + D], start=True, stop=False)
                for hb in range(HB):
                    last = nc.tensor.matmul(o, hid[:, k, hb * P:(hb + 1) * P], wo[:, k, hb, :],
                                            start=(hb == 0 and bias is None), stop=(hb == HB - 1))
                last.then_inc(made, 1)

            def step(i, k, n, first=False, last=False):
                if first:
                    turn(i, k, n)
                hide(i, k, n)
                if not last:
                    turn(i + 1, 1 - k, behind(k, n))
                if not first:
                    give(i - 1, 1 - k, before(k, n))
                if last:
                    give(i, k, n)

            steps(pe, step)

        @block.scalar
        def _(ac):
            ac.sem_inc(copied, 2)
            for k in range(2):
                ac.sem_inc(stored[k], 16)
            hidden_by = gated if nw > 1 else ready
            if nw == 1:
                ac.sem_inc(ready, 2)

            def copy(i, k):
                ac.wait_ge(turned_s, done(i))
                ac.wait_ge(hidden_s, done(i) - 2)
                nc.scalar.copy(xT[:, k, :], ps_t[:, 0:D]).then_inc(copied, 1)

            def store(i, k):
                ac.wait_ge(taken, done(i))
                settle(ac, c)
                ac.dma_start(g.sorted_y[bass.ds(i * P, P), :], out[:, k, :]).then_inc(stored[k], 16)

            def step(i, k, n, first=False, last=False):
                if first:
                    copy(i, k)
                ac.wait_ge(hidden_s, done(i))
                ac.wait_ge(ready if nw > 1 else made, done(i) - 2)
                nc.scalar.activation((gate if nw > 1 else hid)[:, k, :], ps_h[0][k][:], act).then_inc(hidden_by, 1)
                if not last:
                    copy(i + 1, 1 - k)
                if not first:
                    store(i - 1, 1 - k)
                if last:
                    store(i, k)

            steps(ac, step)
            for k in range(2):
                ac.wait_ge(stored[k], 16 * (1 + tiles // 2))

        @block.vector
        def _(ve):
            ve.sem_inc(taken, 2)
            if nw > 1:
                ve.sem_inc(ready, 2)

            def take(i, k, n):
                ve.wait_ge(made, done(i))
                ve.wait_ge(stored[k], (n + 1) * 16)
                nc.vector.tensor_copy(out[:, k, :], ps_o[k][:, 0:D]).then_inc(taken, 1)

            def step(i, k, n, first=False, last=False):
                if nw > 1:
                    ve.wait_ge(gated, i + 1)
                    ve.wait_ge(made, done(i) - 2)
                    nc.vector.tensor_tensor(hid[:, k, :], gate[:, k, :], ps_h[1][k][:], ALU.mult).then_inc(ready, 1)
                if not first:
                    take(i - 1, 1 - k, before(k, n))
                if last:
                    take(i, k, n)

            steps(ve, step)


def combine(nc, s, c, name, g, out=None):
    r = g.route
    SL = 4
    with ExitStack() as x:
        y = [x.enter_context(nc.sbuf_tensor(f"{name}_y{n}", [P, SL, D], F32)) for n in range(2)]
        got = [s(f"{name}_got{n}") for n in range(SL)]
        first, added, stored = s(name + "_first"), s(name + "_added"), s(name + "_stored")
        with nc.Block() as block:
            @block.gpsimd
            def _(pool):
                for t in range(T):
                    if t >= SL:
                        pool.wait_ge(added, t - SL + 1)
                    for n, slot in enumerate((r.slot1, r.slot2)):
                        nc.gpsimd.indirect_dma_start(y[n][:, t % SL, :], None, g.sorted_y,
                                                     bass.IndirectOffsetOnAxis(ap=slot[:, t:t + 1], axis=0)).then_inc(got[t % SL], 16)

            @block.vector
            def _(ve):
                v = nc.vector
                for t in range(T):
                    ve.wait_ge(got[t % SL], 32 * (t // SL + 1))
                    v.scalar_tensor_tensor(g.x[:, t, :], y[0][:, t % SL, :], r.w1[:, t:t + 1], g.x[:, t, :], ALU.mult, ALU.add).then_inc(first, 1)
                    ve.wait_ge(first, t + 1)
                    v.scalar_tensor_tensor(g.x[:, t, :], y[1][:, t % SL, :], r.w2[:, t:t + 1], g.x[:, t, :], ALU.mult, ALU.add).then_inc(added, 1)

            if out is not None:
                @block.sync
                def _(sp):
                    full = (T - 1) * P
                    for t in range(0, T - 1, 4):
                        sp.wait_ge(added, t + 4)
                        sp.dma_start(out[t * P:(t + 4) * P, :].rearrange("(t p) f -> p t f", p=P), g.x[:, t:t + 4, :]).then_inc(stored, 16)
                    sp.wait_ge(added, T)
                    sp.dma_start(out[full:N, :], g.x[0:TAIL, T - 1, :]).then_inc(stored, 16)
                    sp.wait_ge(stored, 16 * ((T - 1) // 4 + 1))


H1, HEADS1 = 32, 4
C1 = H1 * HEADS1
MEM = 4
SLOPE = 0.2
GAT_HEADS = 2
UP = 8


def layer1_project(nc, s, c, g):
    W = 2 * C1 + 3 * C1
    with ExitStack() as x:
        sb = lambda n, sh: x.enter_context(nc.sbuf_tensor("p2_" + n, sh, F32))
        wt, gp, sq, rn = sb("wt", [P, 2, W]), sb("gp", [P, 2]), sb("sq", [P, D]), sb("rn", [P, T])
        loaded, dve, act = s("p2_loaded"), s("p2_dve2"), s("p2_act2")
        with nc.Block() as block:
            @block.sync
            def _(sp):
                k_out = lambda a: a.rearrange("(b p) o -> p b o", p=P)
                sp.dma_start(wt[:, :, 0:C1], k_out(g.wl0)).then_inc(loaded, 16)
                sp.dma_start(wt[:, :, C1:2 * C1], k_out(g.wr0)).then_inc(loaded, 16)
                sp.dma_start(wt[:, :, 2 * C1:3 * C1], k_out(g.w_qkv1[:, 2 * C1:3 * C1])).then_inc(loaded, 16)
                sp.dma_start(wt[:, :, 3 * C1:W], k_out(g.w_qkv1[:, 0:2 * C1])).then_inc(loaded, 16)
                with nc.allow_non_contiguous_dma(reason="256 values, one per weight row"):
                    sp.dma_start(gp[:], g.g_pre.rearrange("(b p) -> p b", p=P)).then_inc(loaded, 16)

            @block.vector
            def _(ve):
                v = nc.vector
                lk = link(ve, dve)
                for t in range(T):
                    lk(v.tensor_tensor_reduce(sq[:], g.xn[:, t, :], g.xn[:, t, :], 1.0, 0.0, ALU.mult, ALU.add, rn[:, t:t + 1]))
                ve.wait_ge(loaded, 80)
                for b in range(2):
                    v.tensor_scalar(wt[:, b, 2 * C1:W], wt[:, b, 2 * C1:W], gp[:, b:b + 1], float(D) ** 0.5, ALU.mult, ALU.mult)
                ve.wait_ge(act, 1)
                lk(v.tensor_scalar(rn[:], rn[:], NORM_EPS, None, ALU.max))
                lk(v.reciprocal(rn[:], rn[:]))

            @block.scalar
            def _(ac):
                ac.wait_ge(dve, T)
                nc.scalar.activation(rn[:], rn[:], ACT.Sqrt).then_inc(act, 1)

        def fill(row, k, lk):
            return nc.vector.tensor_copy(row, tile(g.xn, k))

        def take_dve(k, bank, lk):
            v = nc.vector
            v.tensor_copy(tile(g.xr, k), bank(1)[:, 0:C1])
            v.tensor_scalar(tile(g.vv, k), bank(1)[:, C1:2 * C1], tile_col(rn, k), None, ALU.mult)
            v.tensor_scalar(tile(g.kk, k), bank(2)[:, C1:2 * C1], tile_col(rn, k), None, ALU.mult)
            return v.tensor_scalar(tile(g.qq, k), bank(2)[:, 0:C1], tile_col(rn, k), None, ALU.mult)

        yout = sb("yout", [P, 2, C1])

        def take_act(k, bank, slot):
            nc.scalar.copy(tile(g.att, k), bank(0)[:, 0:C1])
            return nc.scalar.copy(yout[:, slot, :], bank(0)[:, 0:C1])

        project(nc, s, c, "p2", 2, wt, [(0, C1), (C1, 2 * C1), (3 * C1, 2 * C1)], fill, take_dve, take_act, 0, store=(g.table_l, yout))


def attention1(nc, s, c, g):
    with ExitStack() as x:
        sb = lambda n, sh: x.enter_context(nc.sbuf_tensor("la_" + n, sh, F32))
        wp, bias, gout = sb("wp", [P, 1, D]), sb("bias", [P, D]), sb("gout", [P, D])
        o, ss = g.xr2, sb("ss", [P, T])
        with ExitStack() as y:
            sb = lambda n, sh: y.enter_context(nc.sbuf_tensor("la_" + n, sh, F32))
            pen, km, top, mk, mv = sb("pen", [P, 1]), sb("km", [P, C1]), sb("top", [P, 2]), sb("mk", [P, MEM]), sb("mv", [P, MEM])
            diag, mrow, mkT, mvT = sb("diag", [P, P]), sb("mrow", [P, C1]), sb("mkT", [MEM, C1]), sb("mvT", [MEM, C1])
            wout, ctx_m, z = sb("wout", [P, D]), sb("ctx_m", [P, P]), sb("z", [P, 1])
            qm = sb("qm", [P, T * HEADS1])
            ps = [y.enter_context(nc.psum_tensor(f"la_ps{n}", [P, 512], F32)) for n in range(5)]
            loaded, dve, act, pe_s = s("la_loaded"), s("la_dve"), s("la_act"), s("la_pe")
            kmx, qe, ke, cx, ctxd = s("la_keymax"), s("la_q"), s("la_k"), s("la_diag"), s("la_masked")
            with nc.Block() as block:
                @block.sync
                def _(sp):
                    sp.dma_start(mk[:], g.mem_kv[0].rearrange("h d m -> (h d) m")).then_inc(loaded, 16)
                    sp.dma_start(mv[:], g.mem_kv[1].rearrange("h d m -> (h d) m")).then_inc(loaded, 16)
                    sp.dma_start(wout[:], g.w_out1).then_inc(loaded, 16)
                    sp.dma_start(bias[:], g.b_out1[None, :].to_broadcast([P, D])).then_inc(loaded, 16)
                    sp.dma_start(gout[:], g.g_out1[None, :].to_broadcast([P, D])).then_inc(loaded, 16)

                @block.vector
                def _(ve):
                    v = nc.vector
                    lk = link(ve, dve)
                    last = g.kk[:, T - 1, :]
                    lk(v.tensor_scalar(pen[:], c.valid[:, T - 1:T], -LOW, LOW, ALU.mult, ALU.add))
                    lk(v.tensor_scalar(last, last, c.valid[:, T - 1:T], pen[:, 0:1], ALU.mult, ALU.add))
                    v.tensor_reduce(km[:], g.kk[:].rearrange("p t c -> p c t"), AX, ALU.max).then_inc(kmx, 1)
                    q = g.qq[:].rearrange("p t (h d) -> p (t h) d", d=H1)
                    lk(v.tensor_reduce(qm[:], q, AX, ALU.max))
                    v.tensor_tensor(q, q, bcast(qm[:], H1), ALU.subtract).then_inc(qe, 1)
                    ve.wait_ge(loaded, 80)
                    lk(v.tensor_reduce(top[:, 0:1], mk[:], AX, ALU.max))
                    ve.wait_ge(pe_s, 1)
                    lk(v.tensor_reduce(top[:, 1:2], ps[0][:, 0:P], AX, ALU.max))
                    lk(v.tensor_tensor(top[:, 0:1], top[:, 0:1], top[:, 1:2], ALU.max))
                    v.tensor_scalar(diag[:], c.ident[:], top[:, 0:1], None, ALU.mult).then_inc(cx, 1)
                    ve.wait_ge(pe_s, 2)
                    lk(v.tensor_copy(mrow[:], ps[1][:, 0:C1]))
                    lk(v.tensor_tensor(mkT[:], ps[0][0:MEM, P:2 * P], mrow[0:MEM, :], ALU.subtract))
                    lk(v.tensor_copy(mvT[:], ps[0][0:MEM, 2 * P:3 * P]))
                    v.tensor_tensor(g.kk[:], g.kk[:], mrow[:].unsqueeze(1).to_broadcast([P, T, C1]), ALU.subtract).then_inc(ke, 1)
                    ve.wait_ge(act, 1)
                    lk(v.tensor_reduce(qm[:], q, AX, ALU.add))
                    lk(v.reciprocal(qm[:], qm[:]))
                    lk(v.tensor_tensor(q, q, bcast(qm[:], H1), ALU.mult))
                    ve.wait_ge(pe_s, 3)
                    v.tensor_tensor(ctx_m[:], ps[2][:, 0:P], c.head[:].rearrange("p h d -> p (h d)"), ALU.mult).then_inc(ctxd, 1)
                    lk(v.reciprocal(z[:], ps[3][:, 0:1]))
                    lk(v.tensor_scalar(z[:], z[:], float(H1) ** -0.5, None, ALU.mult))
                    lk(v.tensor_scalar(gout[:], gout[:], float(D) ** 0.5, None, ALU.mult))
                    ve.wait_ge(pe_s, 4)
                    lk(v.tensor_scalar(wp[:, 0, :], ps[4][:, 0:D], z[:, 0:1], None, ALU.mult))

                @block.scalar
                def _(ac):
                    ac.wait_ge(qe, 1)
                    nc.scalar.activation(g.qq[:], g.qq[:], ACT.Exp).then_inc(act, 1)
                    ac.wait_ge(ke, 1)
                    nc.scalar.activation(g.kk[:], g.kk[:], ACT.Exp).then_inc(act, 1)
                    nc.scalar.activation(mkT[:], mkT[:], ACT.Exp).then_inc(act, 1)

                @block.tensor
                def _(pe):
                    pe.wait_ge(loaded, 80)
                    pe.wait_ge(kmx, 1)
                    nc.tensor.transpose(ps[0][:, 0:P], km[:], c.ident[:])
                    nc.tensor.transpose(ps[0][0:MEM, P:2 * P], mk[:], c.ident[:])
                    nc.tensor.transpose(ps[0][0:MEM, 2 * P:3 * P], mv[:], c.ident[:]).then_inc(pe_s, 1)
                    pe.wait_ge(cx, 1)
                    nc.tensor.matmul(ps[1][:, 0:C1], c.ones[:], diag[:], start=True, stop=True).then_inc(pe_s, 1)
                    pe.wait_ge(act, 3)
                    for t in range(T):
                        nc.tensor.matmul(ps[2][:, 0:P], g.vv[:, t, :], g.kk[:, t, :], start=(t == 0), stop=False)
                        nc.tensor.matmul(ps[3][:, 0:1], g.kk[:, t, :], c.ones[:, 0:1], start=(t == 0), stop=False)
                    nc.tensor.matmul(ps[2][:, 0:P], mvT[:], mkT[:], start=False, stop=True)
                    nc.tensor.matmul(ps[3][:, 0:1], mkT[:], c.ones[0:MEM, 0:1], start=False, stop=True).then_inc(pe_s, 1)
                    pe.wait_ge(ctxd, 1)
                    nc.tensor.matmul(ps[4][:, 0:D], ctx_m[:], wout[:], start=True, stop=True).then_inc(pe_s, 1)

        def fill(row, k, lk):
            return nc.vector.tensor_copy(row, tile(g.qq, k))

        sq = x.enter_context(nc.sbuf_tensor("la_sq", [P, D], F32))

        def take_dve(k, bank, lk):
            v = nc.vector
            lk(v.tensor_tensor(tile(o, k), bank(0)[:, 0:D], bias[:], ALU.add))
            lk(v.tensor_tensor(sq[:], tile(o, k), tile(o, k), ALU.mult))
            return v.tensor_reduce(tile_col(ss, k), sq[:], AX, ALU.add)

        project(nc, s, c, "p3", 1, wp, [(0, D)], fill, take_dve, None, 2)
        dve, act = s("la_dve2"), s("la_act2")
        with nc.Block() as block:
            @block.scalar
            def _(ac):
                nc.scalar.activation(ss[:], ss[:], ACT.Sqrt).then_inc(act, 1)

            @block.vector
            def _(ve):
                v = nc.vector
                lk = link(ve, dve)
                v.tensor_tensor(g.x[:], g.x[:], g.xn[:], ALU.add)
                ve.wait_ge(act, 1)
                lk(v.tensor_scalar(ss[:], ss[:], NORM_EPS, None, ALU.max))
                lk(v.reciprocal(ss[:], ss[:]))
                lk(v.tensor_tensor(o[:], o[:], bcast(ss[:], D), ALU.mult))
                lk(v.tensor_tensor(o[:], o[:], gout[:].unsqueeze(1).to_broadcast([P, T, D]), ALU.mult))
                lk(v.tensor_tensor(g.x[:], g.x[:], o[:], ALU.add))


def gat(nc, s, c, name, g, table, F, acc, xr, att_w):
    C = F // GAT_HEADS
    Q = BODY // GROUP
    HG = GROUP * GAT_HEADS
    LAG = dict(hot=0, turn=0, hotT=0, mix=1, relu=1, logit=1, flip=2, flipped=2, spread=2, maxed=2,
               scaled=3, seen=3, shifted=3, weighted=3, summed=3, merged=4)
    sem = {k: s(f"{name}_{k}") for k in LAG}
    got, copied_a, dve = s(name + "_got"), s(name + "_index"), s(name + "_dve")
    gathered = [s(f"{name}_gathered{u}") for u in range(BODY)]
    with ExitStack() as x:
        sb = lambda n, sh, d=F32: x.enter_context(nc.sbuf_tensor(f"{name}_{n}", sh, d))
        rows_, hot, hotT, mask = sb("rows", [P, BODY, F]), sb("hot", [P, BODY, P]), sb("hotT", [P, BODY, P]), sb("mask", [P, BODY, P])
        pos_part, leaky, junk = sb("pos", [P, 2, GROUP * F]), sb("leaky", [P, GROUP * F]), sb("junk", [P, HG, P]); junk_m = sb("junk_m", [P, HG, P])
        att = sb("att", [P, F])
        logit, flipped = sb("logit", [P, Q, HG]), sb("flipped", [HG, 2, P])
        high, top_new, drop, scale_ = sb("high", [P, HG]), sb("top_new", [P, Q, HG]), sb("drop", [P, Q, HG]), sb("scale", [P, Q, HG])
        masked, shifted_, weight = sb("masked", [P, HG]), sb("shifted", [P, 2, HG]), sb("weight", [P, 2, HG])
        weighted, dtmp = sb("weighted", [P, GROUP * F]), sb("dtmp", [P, GAT_HEADS])
        zero = sb("zero", [1, P + 512])
        ta = sb("ta", [P, AHEAD * 2 * BODY], I32)
        tb = sb("tb", [P, AHEAD * 2 * BODY], I32)
        index = sb("ix", [P, BODY], I32)
        pb = lambda n, w: x.enter_context(nc.psum_tensor(f"{name}_{n}", [P, w], F32))
        ps_t, ps_x, ps_m, ps_a, ps_s = pb("ps_t", 512), pb("ps_x", GROUP * F), pb("ps_m", 1024), pb("ps_a", GROUP * F), pb("ps_s", 512)
        ps_top, ps_den = ps_s[:, 0:HG], ps_s[:, 64:64 + HG]
        tmp = sb("tmp", [P, UN, F])
        loaded, init = s(name + "_loaded"), s(name + "_init")
        with nc.Block() as block:
            @block.sync
            def _(sp):
                sp.dma_start(att[:], att_w.rearrange("h c -> (h c)")[None, :].to_broadcast([P, F])).then_inc(loaded, 16)

            @block.vector
            def _(ve):
                v = nc.vector
                for b in (rows_, hot, hotT, logit, top_new, drop, zero, shifted_, weight, ta, tb, index):
                    v.memset(b[:], 0)
                v.memset(mask[:], LOW)
                v.memset(scale_[:], 1.0)
                v.memset(g.den[:], 1.0)
                ve.wait_ge(loaded, 16)
                with ve.Fori(0, T // UN) as i:
                    lk = link(ve, init, i, 5)
                    five = lambda b: b[:, bass.ds(i * UN, UN), :]
                    lk(v.tensor_tensor(tmp[:], five(acc), five(xr), ALU.add))
                    lk(v.scalar_tensor_tensor(tmp[:], tmp[:], SLOPE, tmp[:], ALU.mult, ALU.max))
                    lk(v.tensor_tensor(tmp[:], tmp[:], att[:].unsqueeze(1).to_broadcast([P, UN, F]), ALU.mult))
                    lk(v.tensor_reduce(junk[:, 0, 0:UN * GAT_HEADS], tmp[:].rearrange("p t (h c) -> p (t h) c", c=C), AX, ALU.add))
                    lk(v.tensor_copy(five(g.top).rearrange("p t h -> p (t h)"), junk[:, 0, 0:UN * GAT_HEADS]))

        block = x.enter_context(nc.Block())

        def at(stage, i, q, lag, off=0):
            return i * Q + (q - lag + off + LAG[stage] + 1 + UP)

        def body_of(i, q, lag):
            return (((i + AHEAD - 1) if q < lag else i) % AHEAD) * (2 * BODY) + (q - lag) % Q * (2 * GROUP)

        span = lambda q, lag: ((q - lag) % Q * GROUP, ((q - lag) % Q + 1) * GROUP)

        def loop(eng, body, extra=1):
            n = eng.value_load(c.loops[0:1, 0:1], min_val=T + 1, max_val=MAX_BODIES - 1)
            with eng.Fori(0, n + extra) as i:
                body(i)

        @block.sync
        def _(sp):
            def body(i):
                if True:
                    sp.wait_ge(sem["merged"], i * Q + 1)
                settle(sp, c)
                sp.dma_start(ta[:, bass.ds((i % AHEAD) * (2 * BODY), 2 * BODY)], g.table_a[bass.ds(i, 1), :, :].rearrange("b p w -> (b p) w")).then_inc(got, 16)
                sp.dma_start(tb[:, bass.ds((i % AHEAD) * (2 * BODY), 2 * BODY)], g.table_b[bass.ds(i, 1), :, :].rearrange("b p w -> (b p) w")).then_inc(got, 16)
                sp.wait_ge(got, i * 32 + 32)
                settle(sp, c)
            loop(sp, body)

        @block.gpsimd
        def _(pool):
            pool.sem_inc(copied_a, Q)

            def body(i):
                pool.wait_ge(got, i * 32 + 32)
                settle(pool, c)
                for q in range(Q):
                    pool.wait_ge(sem["weighted"], at("weighted", i, q, Q))
                    settle(pool, c)
                    nc.gpsimd.tensor_copy(index[:, q * GROUP:(q + 1) * GROUP], ta[:, bass.ds((i % AHEAD) * (2 * BODY) + q * 2 * GROUP, GROUP)]).then_inc(copied_a, 1)
                    pool.wait_ge(copied_a, (i + 1) * Q + q + 1)
                    settle(pool, c)
                    for u in range(q * GROUP, (q + 1) * GROUP):
                        nc.gpsimd.indirect_dma_start(rows_[:, u, :], None, table,
                                                     bass.IndirectOffsetOnAxis(ap=index[:, u:u + 1], axis=0)).then_inc(gathered[u], 16)
            loop(pool, body)

        @block.vector
        def _(ve):
            v = nc.vector
            for k in ("hot", "logit", "maxed", "shifted", "merged"):
                ve.sem_inc(sem[k], UP)
            PER = Q * (5 * GROUP + 1)

            def body(i):
                lk = link(ve, dve, i, PER)

                def tile_no(q, lag, u):
                    return ve.value_load(tb[0:1, bass.ds(body_of(i, q, lag) + GROUP + u, 1)], min_val=0, max_val=T - 1)

                def merge(q):
                    ve.wait_ge(sem["summed"], at("summed", i, q, 4))
                    ve.wait_ge(sem["scaled"], at("scaled", i, q, 4))
                    settle(ve, c)
                    for u, t in enumerate([tile_no(q, 4, u) for u in range(GROUP)]):
                        sc = scale_[:, (q - 4) % Q, u * GAT_HEADS:(u + 1) * GAT_HEADS]
                        lk(v.tensor_tensor(dtmp[:], tile(g.den, t), sc, ALU.mult))
                        v.tensor_tensor(tile(g.den, t), dtmp[:], ps_den[:, u * GAT_HEADS:(u + 1) * GAT_HEADS], ALU.add)
                        for h in range(GAT_HEADS):
                            col = tile(acc, t)[:, h * C:(h + 1) * C]
                            ins = v.scalar_tensor_tensor(col, col, sc[:, h:h + 1], ps_a[:, u * F + h * C:u * F + (h + 1) * C], ALU.mult, ALU.add)
                        if u < GROUP - 1:
                            lk(ins)
                        else:
                            ins.then_inc(sem["merged"], 1)
                    ve.wait_ge(sem["merged"], at("merged", i, q, 4))

                def shift(q):
                    ve.wait_ge(sem["seen"], at("seen", i, q, 3))
                    pen = tb[:, bass.ds(body_of(i, q, 3), GROUP)].bitcast(F32)
                    lk(v.tensor_tensor(masked[:].rearrange("p (u h) -> p u h", h=GAT_HEADS),
                                       logit[:, (q - 3) % Q, :].rearrange("p (u h) -> p u h", h=GAT_HEADS), bcast(pen, GAT_HEADS), ALU.add))
                    v.tensor_tensor(shifted_[:, (q - 3) % 2, :], masked[:], ps_top, ALU.subtract).then_inc(sem["shifted"], 1)

                def one_hot(q):
                    ve.wait_ge(sem["summed"], at("summed", i, q, Q))
                    lo, hi = span(q, 0)
                    places = ta[:, bass.ds(body_of(i, q, 0) + GROUP, GROUP)].bitcast(F32)
                    v.tensor_tensor(hot[:, lo:hi, :], c.col[:].unsqueeze(1).to_broadcast([P, GROUP, P]), bcast(places, P),
                                    ALU.is_equal).then_inc(sem["hot"], 1)

                def logits(q):
                    ve.wait_ge(sem["relu"], at("relu", i, q, 1))
                    lk(v.scalar_tensor_tensor(leaky[:], ps_x[:], SLOPE, pos_part[:, (q - 1) % 2, :], ALU.mult, ALU.add))
                    for u in range(GROUP):
                        for h in range(GAT_HEADS):
                            k = u * GAT_HEADS + h
                            ins = v.tensor_tensor_reduce(junk[:, k, 0:C], leaky[:, u * F + h * C:u * F + (h + 1) * C], att[:, h * C:(h + 1) * C],
                                                         1.0, 0.0, ALU.mult, ALU.add, logit[:, (q - 1) % Q, k:k + 1])
                    ins.then_inc(sem["logit"], 1)

                def maxima(q):
                    ve.wait_ge(sem["spread"], at("spread", i, q, 2))
                    settle(ve, c)
                    tiles = [tile_no(q, 2, u) for u in range(GROUP)]
                    lo, _ = span(q, 2)
                    for k in range(HG):
                        ins = v.tensor_tensor_reduce(junk_m[:, k, :], ps_m[:, k * P:(k + 1) * P], mask[:, lo + k // GAT_HEADS, :],
                                                     1.0, LOW, ALU.add, ALU.max, high[:, k:k + 1])
                    lk(ins)
                    for u, t in enumerate(tiles):
                        a = slice(u * GAT_HEADS, (u + 1) * GAT_HEADS)
                        new, old = top_new[:, (q - 2) % Q, a], tile(g.top, t)
                        lk(v.tensor_tensor(new, old, high[:, a], ALU.max))
                        lk(v.tensor_tensor(drop[:, (q - 2) % Q, a], old, new, ALU.subtract))
                        if u < GROUP - 1:
                            lk(v.tensor_tensor(old, new, new, ALU.max))
                        else:
                            v.tensor_tensor(old, new, new, ALU.max).then_inc(sem["maxed"], 1)
                    ve.wait_ge(sem["maxed"], at("maxed", i, q, 2))

                ve.wait_ge(got, i * 32 + 32)
                for q in range(Q):
                    merge(q)
                    shift(q)
                    one_hot(q)
                    logits(q)
                    maxima(q)
                assert lk.count[0] == PER, lk.count

            loop(ve, body)

        @block.tensor
        def _(pe):
            for k in ("turn", "mix", "flip", "spread", "seen"):
                pe.sem_inc(sem[k], UP)
            for a in range(0, GROUP * F, 512):
                nc.tensor.matmul(ps_a[:, a:a + 512], zero[:, 0:P], zero[:, P:P + 512], start=True, stop=True)
            nc.tensor.matmul(ps_s[:], zero[:, 0:P], zero[:, P:P + 512], start=True, stop=True).then_inc(sem["summed"], UP)

            def body(i):
                pe.wait_ge(got, i * 32 + 32)
                for q in range(Q):
                    pe.wait_ge(sem["logit"], at("logit", i, q, 2))
                    pe.wait_ge(sem["hotT"], at("hotT", i, q, 1))
                    nc.tensor.transpose(ps_t[0:HG, 0:P], logit[:, (q - 2) % Q, :], c.ident[:]).then_inc(sem["flip"], 1)
                    lo, hi = span(q, 1)
                    pe.wait_ge(sem["logit"], at("logit", i, q, 2))
                    if q:
                        for u in range(lo, hi):
                            pe.wait_ge(gathered[u], i * 16 + 16)
                    settle(pe, c)
                    for n, u in enumerate(range(lo, hi)):
                        t = pe.value_load(tb[0:1, bass.ds(body_of(i, q, 1) + GROUP + n, 1)], min_val=0, max_val=T - 1)
                        nc.tensor.matmul(ps_x[:, n * F:(n + 1) * F], hotT[:, u, :], tile(xr, t), start=True, stop=False)
                        last = nc.tensor.matmul(ps_x[:, n * F:(n + 1) * F], c.ident[:], rows_[:, u, :], start=False, stop=True)
                    last.then_inc(sem["mix"], 1)
                    pe.wait_ge(sem["flipped"], at("flipped", i, q, 2))
                    pe.wait_ge(sem["maxed"], at("maxed", i, q, 3))
                    for k in range(HG):
                        last = nc.tensor.matmul(ps_m[:, k * P:(k + 1) * P], c.row8[:, k, :], flipped[:, (q - 2) % 2, :], start=True, stop=True)
                    last.then_inc(sem["spread"], 1)
                    lo, hi = span(q, 3)
                    pe.wait_ge(sem["maxed"], at("maxed", i, q, 3))
                    pe.wait_ge(sem["merged"], at("merged", i, q, 4))
                    for n, u in enumerate(range(lo, hi)):
                        a = slice(n * GAT_HEADS, (n + 1) * GAT_HEADS)
                        last = nc.tensor.matmul(ps_top[:, a], hotT[:, u, :], top_new[:, (q - 3) % Q, a], start=True, stop=True)
                    last.then_inc(sem["seen"], 1)
                    pe.wait_ge(sem["hot"], at("hot", i, q, 0))
                    pe.wait_ge(sem["flipped"], at("flipped", i, q, 2))
                    lo, hi = span(q, 0)
                    for n, u in enumerate(range(lo, hi)):
                        last = nc.tensor.transpose(ps_t[:, n * P:(n + 1) * P], hot[:, u, :], c.ident[:])
                    last.then_inc(sem["turn"], 1)
                    pe.wait_ge(sem["weighted"], at("weighted", i, q, 3))
                    lo, hi = span(q, 3)
                    for n, u in enumerate(range(lo, hi)):
                        a = slice(n * GAT_HEADS, (n + 1) * GAT_HEADS)
                        nc.tensor.matmul(ps_a[:, n * F:(n + 1) * F], hot[:, u, :], weighted[:, n * F:(n + 1) * F], start=True, stop=True)
                        last = nc.tensor.matmul(ps_den[:, a], hot[:, u, :], weight[:, (q - 3) % 2, a], start=True, stop=True)
                    last.then_inc(sem["summed"], 1)
                for u in range(BODY - GROUP, BODY):
                    pe.wait_ge(gathered[u], i * 16 + 16)
            loop(pe, body)

        @block.scalar
        def _(ac):
            for k in ("hotT", "relu", "flipped", "scaled", "weighted"):
                ac.sem_inc(sem[k], UP)
            own = s(name + "_weights")

            def body(i):
                for q in range(Q):
                    ac.wait_ge(sem["maxed"], at("maxed", i, q, 3))
                    nc.scalar.activation(scale_[:, (q - 3) % Q, :], drop[:, (q - 3) % Q, :], ACT.Exp).then_inc(sem["scaled"], 1)
                    ac.wait_ge(sem["flip"], at("flip", i, q, 2))
                    nc.scalar.copy(flipped[:, (q - 2) % 2, :], ps_t[0:HG, 0:P]).then_inc(sem["flipped"], 1)
                    ac.wait_ge(sem["mix"], at("mix", i, q, 1))
                    nc.scalar.activation(pos_part[:, (q - 1) % 2, :], ps_x[:], ACT.Relu, scale=1.0 - SLOPE).then_inc(sem["relu"], 1)
                    ac.wait_ge(sem["shifted"], at("shifted", i, q, 3))
                    w = weight[:, (q - 3) % 2, :]
                    nc.scalar.activation(w, shifted_[:, (q - 3) % 2, :], ACT.Exp).then_inc(own, 1)
                    ac.wait_ge(own, i * Q + q + 1)
                    ac.wait_ge(sem["summed"], at("summed", i, q, 4))
                    lo, _ = span(q, 3)
                    for n in range(GROUP):
                        for h in range(GAT_HEADS):
                            k = n * GAT_HEADS + h
                            ins = nc.scalar.activation(weighted[:, n * F + h * C:n * F + (h + 1) * C], rows_[:, lo + n, h * C:(h + 1) * C],
                                                       ACT.Copy, scale=w[:, k:k + 1])
                    ins.then_inc(sem["weighted"], 1)
                    ac.wait_ge(sem["turn"], at("turn", i, q, 0))
                    ac.wait_ge(sem["maxed"], at("maxed", i, q, 4))
                    lo, hi = span(q, 0)
                    flat = lambda b: b[:, lo:hi, :].rearrange("p u n -> p (u n)")
                    nc.scalar.copy(flat(hotT), ps_t[:])
                    nc.scalar.activation(flat(mask), ps_t[:], ACT.Identity, bias=c.low[:, 0:1], scale=-LOW).then_inc(sem["hotT"], 1)
            loop(ac, body)


def gat1_finish(nc, s, c, g):
    with ExitStack() as x:
        sb = lambda n, sh: x.enter_context(nc.sbuf_tensor("p4_" + n, sh, F32))
        wt, bias, yout = sb("wt", [P, 1, 2 * D]), sb("bias", [P, C1]), sb("yout", [P, 2, D])
        loaded, inv, scaled = s("p4_loaded"), s("p4_inv"), s("p4_scaled")
        with nc.Block() as block:
            @block.sync
            def _(sp):
                sp.dma_start(wt[:, 0, 0:D], g.wl1).then_inc(loaded, 16)
                sp.dma_start(wt[:, 0, D:2 * D], g.wr1).then_inc(loaded, 16)
                sp.dma_start(bias[:], g.gb0[None, :].to_broadcast([P, C1])).then_inc(loaded, 16)
                sp.wait_ge(loaded, 48)

            @block.vector
            def _(ve):
                nc.vector.reciprocal(g.den[:], g.den[:]).then_inc(inv, 1)
                ve.wait_ge(inv, 1)
                a = g.att[:].rearrange("p t (h c) -> p (t h) c", h=GAT_HEADS)
                nc.vector.tensor_tensor(a, a, bcast(g.den[:].rearrange("p t h -> p (t h)"), C1 // GAT_HEADS), ALU.mult).then_inc(scaled, 1)

        def fill(row, k, lk):
            v = nc.vector
            lk(v.tensor_tensor(row, tile(g.att, k), bias[:], ALU.add))
            return v.tensor_scalar(row, row, 0.0, None, ALU.max)

        def take_dve(k, bank, lk):
            return nc.vector.tensor_copy(tile(g.xr2, k), bank(1)[:, 0:D])

        def take_act(k, bank, slot):
            nc.scalar.copy(tile(g.att2, k), bank(0)[:, 0:D])
            return nc.scalar.copy(yout[:, slot, :], bank(0)[:, 0:D])

        project(nc, s, c, "p4", 1, wt, [(0, D), (D, D)], fill, take_dve, take_act, 1, store=(g.table_y, yout))


def gat2_finish(nc, s, c, g):
    with nc.sbuf_tensor("g2_bias", [P, D], F32) as bias:
        loaded, dve = s("gf_loaded"), s("gf_dve")
        with nc.Block() as block:
            @block.sync
            def _(sp):
                sp.dma_start(bias[:], g.gb1[None, :].to_broadcast([P, D])).then_inc(loaded, 16)

            @block.vector
            def _(ve):
                v = nc.vector
                lk = link(ve, dve)
                lk(v.reciprocal(g.den[:], g.den[:]))
                a = g.att2[:].rearrange("p t (h c) -> p (t h) c", h=GAT_HEADS)
                lk(v.tensor_tensor(a, a, bcast(g.den[:].rearrange("p t h -> p (t h)"), D // GAT_HEADS), ALU.mult))
                lk(v.tensor_tensor(g.x[:], g.x[:], g.att2[:], ALU.add))
                ve.wait_ge(loaded, 16)
                lk(v.tensor_tensor(g.x[:], g.x[:], bias[:].unsqueeze(1).to_broadcast([P, T, D]), ALU.add))


TILES0, TILES1 = (-(-(2 * N + ne * (P - 1)) // P) // 2 * 2 for ne in (16, 8))


class Semaphores:

    def __init__(self, nc):
        self.nc, self.known = nc, {}

    def __call__(self, name):
        self.known[name] = self.nc.alloc_semaphore(name=name)
        return self.known[name]

    def close(self):
        self.nc.clear_and_free_semaphores(list(self.known.values()))
        self.nc.all_engine_barrier()
        self.known.clear()


class Shared:
    pass


def build(nc, io, out):
    g = Shared()
    g.out = out
    g.x_in, g.src, g.dst = io["x"], io["src"], io["dst"]
    g.w1_l, g.w1_r, g.b1, g.w2_l, g.w2_r, g.b2 = (io["L0_gnn_" + n] for n in ("w1_l", "w1_r", "b1", "w2_l", "w2_r", "b2"))
    g.w_qkv, g.b_qkv, g.w_proj, g.b_proj, g.temperature = (io["L0_mix_" + n] for n in ("Wqkv", "bqkv", "Wproj", "bproj", "temperature"))
    g.gate_w0, g.gate_b0, g.e0_w1, g.e0_w2, g.e0_w3 = (io["L0_ffn_" + n] for n in ("gate_w", "gate_b", "w1", "w2", "w3"))
    g.wl0, g.wr0, g.att_w0, g.gb0 = (io["L1_gnn_" + n] for n in ("Wl0", "Wr0", "att0", "b0"))
    g.wl1, g.wr1, g.att_w1, g.gb1 = (io["L1_gnn_" + n] for n in ("Wl1", "Wr1", "att1", "b1"))
    g.w_qkv1, g.mem_kv, g.w_out1, g.b_out1, g.g_out1, g.g_pre = (
        io["L1_mix_" + n] for n in ("w_qkv", "mem_kv", "w_out", "b_out", "g_out", "g_pre"))
    g.gate_w1, g.gate_b1, g.e1_w1, g.e1_b1, g.e1_w2, g.e1_b2 = (
        io["L1_ffn_" + n] for n in ("gate_w", "gate_b", "W1", "b1", "W2", "b2"))
    dram = lambda n, sh, d=F32: nc.dram_tensor(n, sh, d, kind="Internal").ap()
    g.table_y, g.table_l = dram("table_y", [T * P, D]), dram("table_l", [T * P, C1])
    g.table_a, g.table_b = (dram(n, [MAX_BODIES, P, 2 * BODY], I32) for n in ("table_a", "table_b"))
    g.sorted_x, g.sorted_y = dram("sorted_x", [TILES0 * P, D]), dram("sorted_y", [TILES0 * P, D])
    s = Semaphores(nc)
    with ExitStack() as x:
        sb = lambda n, sh, d=F32: x.enter_context(nc.sbuf_tensor(n, sh, d))
        c = Shared()
        c.settled = nc.alloc_semaphore(name="settled")
        c.col, c.pair_no, c.valid, c.head = sb("col", [P, P]), sb("pair_no", [P, ROUND]), sb("valid", [P, T]), sb("head", [P, 4, 32])
        c.part, c.low, c.quadf, c.row8 = sb("part", [P, 1]), sb("low", [P, 1]), sb("quadf", [P, 1]), sb("row8", [8, 8, P])
        c.ones, c.ident, c.after, c.loops = sb("ones", [P, P]), sb("ident", [P, P]), sb("after", [P, P]), sb("loops", [1, 2], I32)
        g.x, g.inv_deg = sb("x", [P, T, D]), sb("inv_deg", [P, T])
        constants(nc, s, c)
        clear_sorted(nc, s, g)
        pair_tables(nc, s, c, g.src, g.dst, g.table_a, g.table_b)
        with ExitStack() as y:
            sb = lambda n, sh: y.enter_context(nc.sbuf_tensor(n, sh, F32))
            g.own, g.qk, g.agg = sb("own", [P, T, D]), sb("qk", [P, T, 2 * D]), sb("agg", [P, T, D + 1])
            g.mix, g.mix_w = sb("mix", [P, H0 * NB, HD + 1]), sb("mix_w", [P, H0 * NB])
            with nc.sbuf_tensor("v1", [P, T, H0 * (HD + 1)], F32) as g.v1:
                layer0_project(nc, s, c, g)
                s.close()
                sage1_and_keys(nc, s, c, g)
                sage1_finish(nc, s, c, g)
            s.close()
            sage2_and_queries(nc, s, c, g)
            s.close()
            layer0_join(nc, s, c, g)
        with ExitStack() as y:
            sb = lambda n, sh, d=F32: y.enter_context(nc.sbuf_tensor(n, sh, d))
            g.xn = sb("xn", [P, T, D])
            g.route = Shared()
            g.route.slot1, g.route.slot2 = sb("slot1", [P, T], I32), sb("slot2", [P, T], I32)
            g.route.w1, g.route.w2, g.route.expert = sb("w1", [P, T]), sb("w2", [P, T]), sb("expert", [1, TILES0], I32)
            normed(nc, s, "ln_e0", g.x, g.xn)
            route(nc, s, c, "r0", g, 16, TILES0, g.gate_w0, g.gate_b0, True)
            experts(nc, s, c, "e0", g, TILES0, 512, [g.e0_w1, g.e0_w2], g.e0_w3, ACT.Silu)
            combine(nc, s, c, "c0", g)
        s.close()
        with ExitStack() as y:
            sb = lambda n, sh: y.enter_context(nc.sbuf_tensor(n, sh, F32))
            g.den, g.top = sb("den", [P, T, GAT_HEADS]), sb("top", [P, T, GAT_HEADS])
            g.xr2, g.att2 = sb("xr2", [P, T, D]), sb("att2", [P, T, D])
            with ExitStack() as z:
                sb = lambda n, sh: z.enter_context(nc.sbuf_tensor(n, sh, F32))
                g.att, g.xr = sb("att", [P, T, C1]), sb("xr", [P, T, C1])
                with ExitStack() as w:
                    sb = lambda n, sh: w.enter_context(nc.sbuf_tensor(n, sh, F32))
                    g.xn, g.vv, g.kk, g.qq = sb("xn1", [P, T, D]), sb("vv", [P, T, C1]), sb("kk", [P, T, C1]), sb("qq", [P, T, C1])
                    normed(nc, s, "ln_1", g.x, g.xn)
                    layer1_project(nc, s, c, g)
                    attention1(nc, s, c, g)
                s.close()
                gat(nc, s, c, "g1", g, g.table_l, C1, g.att, g.xr, g.att_w0)
                gat1_finish(nc, s, c, g)
            s.close()
            gat(nc, s, c, "g2", g, g.table_y, D, g.att2, g.xr2, g.att_w1)
            gat2_finish(nc, s, c, g)
        s.close()
        with ExitStack() as y:
            sb = lambda n, sh, d=F32: y.enter_context(nc.sbuf_tensor(n, sh, d))
            g.xn = sb("xn2", [P, T, D])
            g.route = Shared()
            g.route.slot1, g.route.slot2 = sb("slot1b", [P, T], I32), sb("slot2b", [P, T], I32)
            g.route.w1, g.route.w2, g.route.expert = sb("w1b", [P, T]), sb("w2b", [P, T]), sb("expert1", [1, TILES1], I32)
            normed(nc, s, "ln_e1", g.x, g.xn)
            route(nc, s, c, "r1", g, 8, TILES1, g.gate_w1, g.gate_b1, False)
            experts(nc, s, c, "e1", g, TILES1, 512, [g.e1_w1], g.e1_w2, ACT.Gelu, g.e1_b1, g.e1_b2)
            combine(nc, s, c, "c1", g, g.out)


def clear_sorted(nc, s, g):
    zeroed, stored = s("clear_zeroed"), s("clear_stored")
    with nc.sbuf_tensor("clear_zero", [P, D], F32) as zero, nc.Block() as block:
        @block.vector
        def _(ve):
            nc.vector.memset(zero[:], 0.0).then_inc(zeroed, 1)

        @block.sync
        def _(sp):
            sp.wait_ge(zeroed, 1)
            sp.dma_start(rows(g.sorted_x), zero[:].unsqueeze(1).to_broadcast([P, TILES0, D])).then_inc(stored, 16)
            sp.wait_ge(stored, 16)


_INS = ["x", "src", "dst"] + ["L0_gnn_" + n for n in ("w1_l", "w1_r", "b1", "w2_l", "w2_r", "b2")] + [
    "L0_mix_" + n for n in ("Wqkv", "bqkv", "Wproj", "bproj", "temperature")] + [
    "L0_ffn_" + n for n in ("gate_w", "gate_b", "w1", "w2", "w3")] + [
    "L1_gnn_" + n for n in ("Wl0", "Wr0", "att0", "b0", "Wl1", "Wr1", "att1", "b1")] + [
    "L1_mix_" + n for n in ("w_qkv", "mem_kv", "w_out", "b_out", "g_out", "g_pre")] + [
    "L1_ffn_" + n for n in ("gate_w", "gate_b", "W1", "b1", "W2", "b2")]


def kernel(**inputs):
    import numpy as _np
    import concourse.bacc as _bacc
    from concourse import mybir as _mybir
    from concourse.bass_utils import run_bass_kernel_spmd as _run

    nc = _bacc.Bacc("TRN2", target_bir_lowering=False, num_devices=1)
    arrays, args = {}, {}
    for name in _INS:
        a = _np.ascontiguousarray(inputs[name])
        if name == "L0_mix_temperature":
            a = a.reshape(H0)
        arrays[f"in_{name}_dram"] = a
        args[name] = nc.dram_tensor(f"in_{name}_dram", list(a.shape), _mybir.dt.from_np(a.dtype), kind="ExternalInput").ap()
    out = nc.dram_tensor("out_0_dram", [N, D], F32, kind="ExternalOutput").ap()
    build(nc, args, out)
    return _run(nc, [arrays], core_ids=[0]).results[0]["out_0_dram"]
```

```python
from contextlib import ExitStack

import concourse.bass as bass
from concourse import mybir

ALU = mybir.AluOpType
ACT = mybir.ActivationFunctionType
F32 = mybir.dt.float32
I32 = mybir.dt.int32
U32 = mybir.dt.uint32
AX = mybir.AxisListType.X

P = 128
N = 3125
T = -(-N // P)
TAIL = N - (T - 1) * P
D = 256
E = 53125
CHUNKS = -(-E // P)
CB = -(-CHUNKS // P)
BODY = 16
GROUP = 4
ROUND = 512
MAX_ROUNDS = -(-(CHUNKS * T + 4 * BODY) // ROUND)
MAX_BODIES = MAX_ROUNDS * ROUND // BODY
UN = 5
LN_EPS = 1e-5
TRUSTED = "pair_tables made it from destinations below N"
FAR = 1.0e6
LOW = -1.0e30


def link(eng, sem, i=0, per=0, base=0):
    count = [0]

    def step(ins):
        count[0] += 1
        ins.then_inc(sem, 1)
        eng.wait_ge(sem, base + i * per + count[0])
        return count[0]

    step.count = count
    return step


def back(u, slots, unroll):
    d = 1
    while ((u - d) % unroll) % slots != u % slots:
        d += 1
    return d


def tile(buf, k):
    return buf[:, bass.ds(k, 1), :].rearrange("p a f -> p (a f)")


def settle(eng, c):
    eng.sem_inc(c.settled, 1)


def bcast(ap, n):
    return ap.unsqueeze(2).to_broadcast([ap.shape[0], ap.shape[1], n])


def rows(dram, n=T):
    return dram.rearrange("(t p) f -> p t f", p=P)


def constants(nc, s, c):
    made, dve = s("const_made"), s("const_dve")
    with nc.sbuf_tensor("quadrant", [P, 2], I32) as quad, nc.Block() as block:

        @block.gpsimd
        def _(pool):
            fl = dict(allow_small_or_imprecise_dtypes=True)
            nc.gpsimd.iota(c.col[:], [[1, P]], base=0, channel_multiplier=0, **fl).then_inc(made, 1)
            nc.gpsimd.iota(c.part[:], [[0, 1]], base=0, channel_multiplier=1, **fl).then_inc(made, 1)
            nc.gpsimd.iota(c.pair_no[:], [[1, ROUND]], base=0, channel_multiplier=0, **fl).then_inc(made, 1)
            nc.gpsimd.iota(c.valid[:], [[P, T]], base=0, channel_multiplier=1, **fl).then_inc(made, 1)
            nc.gpsimd.iota(c.row8[:], [[1, 8], [0, P]], base=0, channel_multiplier=0, **fl).then_inc(made, 1)
            nc.gpsimd.iota(c.head[:], [[1, 4], [0, 32]], base=0, channel_multiplier=0, **fl).then_inc(made, 1)
            nc.gpsimd.iota(quad[:, 0:1], [[0, 1]], base=0, channel_multiplier=1).then_inc(made, 1)

        @block.vector
        def _(dve_):
            v = nc.vector
            lk = link(dve_, dve)
            dve_.wait_ge(made, 7)
            v.memset(c.ones[:], 1.0)
            v.memset(c.low[:], LOW)
            v.tensor_scalar(c.ident[:], c.col[:], c.part[:, 0:1], None, ALU.is_equal)
            v.tensor_scalar(c.after[:], c.col[:], c.part[:, 0:1], None, ALU.is_gt)
            v.tensor_single_scalar(c.valid[:], c.valid[:], float(N), ALU.is_lt)
            v.tensor_scalar(c.row8[:], c.row8[:], c.part[0:8, 0:1], None, ALU.is_equal)
            lk(v.tensor_single_scalar(quad[:, 1:2], quad[:, 0:1], 5, ALU.arith_shift_right))
            lk(v.tensor_copy(c.quadf[:], quad[:, 1:2]))
            lk(v.tensor_scalar(c.head[:], c.head[:], c.quadf[:, 0:1], None, ALU.is_equal))


def pair_tables(nc, s, c, src, dst, table_a, table_b):
    loaded, dve, act, ready, got, pe_s, prefix = (s("tab_" + x) for x in ("loaded", "dve", "act", "ready", "got", "pe", "prefix"))
    chosen, summed, staged, stored, filled = (s("tab_" + x) for x in ("chosen", "summed", "staged", "stored", "filled"))
    full = E // P
    with ExitStack() as x:
        sb = lambda n, sh, d=F32: x.enter_context(nc.sbuf_tensor("tab_" + n, sh, d))
        ii = sb("ii", [P, 2, CB, P], I32)
        srcf, dstf = sb("srcf", [P, CB, P]), sb("dstf", [P, CB, P])
        low = sb("low", [P, CB, P])
        lo, hi = sb("lo", [P, CB]), sb("hi", [P, CB])
        lo_i, hi_i = sb("lo_i", [P, CB], I32), sb("hi_i", [P, CB], I32)
        cnt, start, end, rel = sb("cnt", [P, CB]), sb("start", [P, CB]), sb("end", [P, CB]), sb("rel", [P, CB])
        tot = sb("tot", [P, CB])
        relb = sb("relb", [P, CB, P])
        pick = sb("pick", [P, CB, ROUND])
        jcur = sb("jcur", [P, ROUND])
        val, tl, dr, m1 = sb("val", [P, ROUND]), sb("tl", [P, ROUND]), sb("dr", [P, ROUND]), sb("m1", [P, ROUND])
        sa, sbb = sb("sa", [P, 2 * ROUND], I32), sb("sb", [P, 2 * ROUND], I32)
        ps = [x.enter_context(nc.psum_tensor(f"tab_ps{i}", [P, ROUND], F32)) for i in range(5)]
        ga = sa[:].rearrange("p (g w) -> p g w", w=2 * GROUP)
        gb = sbb[:].rearrange("p (g w) -> p g w", w=2 * GROUP)
        four = lambda a: a.rearrange("p (g u) -> p g u", u=GROUP)
        block = x.enter_context(nc.Block())

        @block.sync
        def _(sp):
            sp.wait_ge(filled, 1)
            for w, a in enumerate((src, dst)):
                cut = (CB - 1) * P * P
                sp.dma_start(ii[:, w, 0:CB - 1, :], a[0:cut].rearrange("(k p e) -> p k e", p=P, e=P)).then_inc(loaded, 16)
                sp.dma_start(ii[0:full - (CB - 1) * P, w, CB - 1, :], a[cut:full * P].rearrange("(p e) -> p e", e=P)).then_inc(loaded, 16)
                sp.dma_start(ii[full - (CB - 1) * P:full - (CB - 1) * P + 1, w, CB - 1, 0:E - full * P],
                             a[full * P:E].rearrange("(o e) -> o e", o=1)).then_inc(loaded, 16)
            sp.wait_ge(ready, 1)
            rounds = sp.value_load(c.loops[0:1, 1:2], min_val=1, max_val=MAX_ROUNDS)
            per = ROUND // BODY
            with sp.Fori(0, rounds) as r:
                sp.wait_ge(staged, r + 1)
                settle(sp, c)
                sp.dma_start(table_a[bass.ds(r * per, per), :, :].rearrange("b p w -> p b w"),
                             sa[:].rearrange("p (b w) -> p b w", w=2 * BODY)).then_inc(stored, 16)
                sp.dma_start(table_b[bass.ds(r * per, per), :, :].rearrange("b p w -> p b w"),
                             sbb[:].rearrange("p (b w) -> p b w", w=2 * BODY)).then_inc(stored, 16)
                sp.wait_ge(stored, r * 32 + 32)
                settle(sp, c)

        @block.vector
        def _(ve):
            v = nc.vector
            lk = link(ve, dve)
            lk(v.memset(ii[:, 0, :, :], 0))
            v.memset(ii[:, 1, :, :], -1).then_inc(filled, 1)
            ve.wait_ge(loaded, 16 * 6)
            ve.wait_ge(filled, 1)
            lk(v.tensor_copy(srcf[:], ii[:, 0, :, :]))
            lk(v.tensor_copy(dstf[:], ii[:, 1, :, :]))
            lk(v.tensor_scalar(low[:], dstf[:], 0.0, FAR, ALU.is_lt, ALU.mult))
            lk(v.tensor_tensor(low[:], low[:], dstf[:], ALU.add))
            lk(v.tensor_reduce(lo[:], low[:], AX, ALU.min))
            lk(v.tensor_reduce(hi[:], dstf[:], AX, ALU.max))
            lk(v.tensor_copy(lo_i[:], lo[:]))
            lk(v.tensor_copy(hi_i[:], hi[:]))
            lk(v.tensor_single_scalar(lo_i[:], lo_i[:], 7, ALU.arith_shift_right))
            lk(v.tensor_single_scalar(hi_i[:], hi_i[:], 7, ALU.arith_shift_right))
            lk(v.tensor_copy(lo[:], lo_i[:]))
            lk(v.tensor_copy(hi[:], hi_i[:]))
            lk(v.tensor_tensor(cnt[:], hi[:], lo[:], ALU.subtract))
            v.tensor_scalar(cnt[:], cnt[:], 1.0, 0.0, ALU.add, ALU.max).then_inc(got, 1)
            ve.wait_ge(prefix, 1)
            lk(v.tensor_copy(start[:], ps[0][:, 0:CB]))
            lk(v.tensor_copy(tot[:], ps[0][:, CB:2 * CB]))
            for k in range(1, CB):
                lk(v.tensor_tensor(start[:, k:k + 1], start[:, k:k + 1], tot[:, k - 1:k], ALU.add))
                lk(v.tensor_tensor(tot[:, k:k + 1], tot[:, k:k + 1], tot[:, k - 1:k], ALU.add))
            lk(v.tensor_tensor(end[:], start[:], cnt[:], ALU.add))
            lk(v.tensor_tensor(rel[:], lo[:], start[:], ALU.subtract))
            lk(v.tensor_copy(relb[:], bcast(rel[:], P)))
            lk(v.tensor_scalar(m1[0:1, 0:1], tot[0:1, CB - 1:CB], float(BODY - 1), None, ALU.add))
            lk(v.tensor_scalar(m1[0:1, 1:2], tot[0:1, CB - 1:CB], float(4 * BODY - 1 + ROUND - 1), None, ALU.add))
            lk(v.tensor_scalar(m1[0:1, 2:3], tot[0:1, CB - 1:CB], float(4 * BODY - 1), None, ALU.add))
            lk(v.tensor_copy(c.loops[0:1, 0:3], m1[0:1, 0:3]))
            lk(v.tensor_single_scalar(c.loops[0:1, 0:1], c.loops[0:1, 0:1], BODY.bit_length() - 1, ALU.arith_shift_right))
            lk(v.tensor_single_scalar(c.loops[0:1, 2:3], c.loops[0:1, 2:3], BODY.bit_length(), ALU.arith_shift_right))
            lk(v.tensor_single_scalar(c.loops[0:1, 1:2], c.loops[0:1, 1:2], ROUND.bit_length() - 1, ALU.arith_shift_right))
            v.tensor_copy(jcur[:], c.pair_no[:]).then_inc(ready, 1)
            ve.wait_ge(ready, 1)
            rounds = ve.value_load(c.loops[0:1, 1:2], min_val=1, max_val=MAX_ROUNDS)
            per = CB + 12
            n0 = lk.count[0]
            with ve.Fori(0, rounds) as r:
                ll = link(ve, dve, r, per, n0)
                for k in range(CB):
                    ll(v.tensor_scalar(pick[:, k, :], jcur[:], start[:, k:k + 1], None, ALU.is_ge))
                for k in range(CB):
                    v.scalar_tensor_tensor(pick[:, k, :], jcur[:], end[:, k:k + 1], pick[:, k, :], ALU.is_lt, ALU.mult).then_inc(chosen, 1)
                ve.wait_ge(summed, r + 1)
                ll(v.tensor_copy(val[:], ps[3][:]))
                ll(v.tensor_tensor(tl[:], jcur[:], val[:], ALU.mult))
                ll(v.tensor_tensor(tl[:], tl[:], ps[2][:], ALU.add))
                ll(v.scalar_tensor_tensor(dr[:], tl[:], -float(P), ps[1][:], ALU.mult, ALU.add))
                ll(v.tensor_scalar(m1[:], val[:], FAR, -FAR, ALU.mult, ALU.add))
                ll(v.tensor_tensor(dr[:], dr[:], m1[:], ALU.add))
                ll(v.tensor_copy(ga[:, :, 0:GROUP], four(ps[0][:])))
                ll(v.tensor_copy(ga[:, :, GROUP:2 * GROUP].bitcast(F32), four(dr[:])))
                ll(v.tensor_copy(gb[:, :, GROUP:2 * GROUP], four(tl[:])))
                ll(v.tensor_scalar(m1[:], dr[:], 0.0, None, ALU.is_ge))
                ll(v.scalar_tensor_tensor(m1[:], dr[:], float(P) - 0.5, m1[:], ALU.is_lt, ALU.mult))
                ll(v.tensor_scalar(jcur[:], jcur[:], float(ROUND), None, ALU.add))
                v.tensor_scalar(gb[:, :, 0:GROUP].bitcast(F32), four(m1[:]), -LOW, LOW, ALU.mult, ALU.add).then_inc(staged, 1)
                ve.wait_ge(stored, r * 32 + 32)
                assert ll.count[0] == per, ll.count

        @block.tensor
        def _(pe):
            pe.wait_ge(got, 1)
            nc.tensor.matmul(ps[0][:, 0:CB], c.after[:], cnt[:], start=True, stop=True)
            nc.tensor.matmul(ps[0][:, CB:2 * CB], c.ones[:], cnt[:], start=True, stop=True).then_inc(prefix, 1)
            pe.wait_ge(ready, 1)
            rounds = pe.value_load(c.loops[0:1, 1:2], min_val=1, max_val=MAX_ROUNDS)
            with pe.Fori(0, rounds) as r:
                pe.wait_ge(chosen, CB * r + CB)
                for q in range(4):
                    for k in range(CB):
                        w = (srcf[:, k, :], dstf[:, k, :], relb[:, k, :], c.ones[:])[q]
                        last = nc.tensor.matmul(ps[q][:], w, pick[:, k, :], start=(k == 0), stop=(k == CB - 1))
                last.then_inc(summed, 1)


def turned(nc, s, c, name, weights):
    loaded, done, copied = s(name + "_loaded"), s(name + "_turned"), s(name + "_copied")
    jobs = []
    for src, n_out, dst, col in weights:
        for r in range(n_out // P):
            jobs.append((len(jobs), src[r * P:(r + 1) * P, :], dst, col + r * P))
    with ExitStack() as x:
        raw = x.enter_context(nc.sbuf_tensor(name + "_raw", [P, len(jobs), D], F32))
        ps = x.enter_context(nc.psum_tensor(name + "_ps", [P, 2, 512], F32))
        block = x.enter_context(nc.Block())

        @block.sync
        def _(sp):
            for n, src, _, _ in jobs:
                sp.dma_start(raw[:, n, :], src).then_inc(loaded, 16)

        @block.tensor
        def _(pe):
            pe.wait_ge(loaded, 16 * len(jobs))
            for n, _, _, _ in jobs:
                if n >= 2:
                    pe.wait_ge(copied, n - 1)
                for b in range(2):
                    last = nc.tensor.transpose(ps[:, n % 2, b * P:(b + 1) * P], raw[:, n, b * P:(b + 1) * P], c.ident[:])
                last.then_inc(done, 1)

        @block.vector
        def _(ve):
            for n, _, dst, col in jobs:
                ve.wait_ge(done, n + 1)
                nc.vector.tensor_copy(dst[:, :, col:col + P], ps[:, n % 2, 0:D].rearrange("p (b o) -> p b o", b=2)).then_inc(copied, 1)


def stats(nc, s, name, x, mv):
    dve, act = s(name + "_dve"), s(name + "_act")
    with nc.sbuf_tensor(name + "_bn", [P, T, 6], F32) as bn, nc.sbuf_tensor(name + "_sd", [P, T], F32) as sd, nc.Block() as block:

        @block.vector
        def _(ve):
            v = nc.vector
            for t in range(T):
                v.bn_stats(bn[:, t, :], x[:, t, :]).then_inc(dve, 1)
            for t in range(T):
                ve.wait_ge(dve, t + 1)
                v.bn_aggr(mv[:, t, :], bn[:, t, :]).then_inc(dve, 1)
            ve.wait_ge(dve, 2 * T)
            v.tensor_scalar(sd[:], mv[:, :, 1], LN_EPS, None, ALU.add).then_inc(dve, 1)
            ve.wait_ge(act, 1)
            v.reciprocal(mv[:, :, 1], sd[:]).then_inc(dve, 1)

        @block.scalar
        def _(ac):
            ac.wait_ge(dve, 2 * T + 1)
            nc.scalar.activation(sd[:], sd[:], ACT.Sqrt).then_inc(act, 1)


def uses(u, slots, unroll):
    same = [w for w in range(unroll) if w % slots == u % slots]
    return same.index(u), len(same)


def project(nc, s, c, name, kin, weight, parts, fill, take_dve, take_act, links, store=None):
    rows_ready, turned_s, copied, product, act_done, dve_done, chain = (
        s(name + "_" + w) for w in ("rows", "turned", "copied", "product", "act", "dve", "chain"))
    stored = [s(f"{name}_stored{n}") for n in range(2)]
    steps = [(u, u % 2) for u in range(UN)]
    made = lambda i, u: i * UN + u + 1 + UN
    free = lambda i, u: i * UN + u + 1 + UN - back(u, 2, UN)
    with ExitStack() as x:
        row = x.enter_context(nc.sbuf_tensor(name + "_row", [P, 2, kin * P], F32))
        rowT = x.enter_context(nc.sbuf_tensor(name + "_rowT", [P, 2, kin * P], F32))
        ps_t = x.enter_context(nc.psum_tensor(name + "_ps_t", [P, 2, 512], F32))
        ps = [x.enter_context(nc.psum_tensor(f"{name}_ps{n}", [P, 512], F32)) for n in range(2 * len(parts))]
        block = x.enter_context(nc.Block())
        bank = lambda slot: (lambda n: ps[slot * len(parts) + n])

        @block.vector
        def _(ve):
            ve.sem_inc(rows_ready, UN)
            ve.sem_inc(dve_done, UN)
            with ve.Fori(0, T // UN) as i:
                lk = link(ve, chain, i, links * UN)

                def take(u):
                    ve.wait_ge(product, made(i, u))
                    take_dve(i * UN + u, bank(u % 2), lk).then_inc(dve_done, 1)

                for u, slot in steps:
                    ve.wait_ge(turned_s, free(i, u))
                    fill(row[:, slot, :], i * UN + u, lk).then_inc(rows_ready, 1)
                    if u:
                        take(u - 1)
                take(UN - 1)
                assert lk.count[0] == links * UN, lk.count

        @block.tensor
        def _(pe):
            pe.sem_inc(turned_s, UN)
            pe.sem_inc(product, UN)
            with pe.Fori(0, T // UN) as i:
                for u, slot in steps:
                    pe.wait_ge(rows_ready, made(i, u))
                    pe.wait_ge(copied, free(i, u))
                    for b in range(kin):
                        last = nc.tensor.transpose(ps_t[:, slot, b * P:(b + 1) * P], row[:, slot, b * P:(b + 1) * P], c.ident[:])
                    last.then_inc(turned_s, 1)
                    pe.wait_ge(copied, made(i, u))
                    if take_act:
                        pe.wait_ge(act_done, free(i, u))
                    pe.wait_ge(dve_done, free(i, u))
                    for m, (col, w) in enumerate(parts):
                        for b in range(kin):
                            last = nc.tensor.matmul(bank(slot)(m)[:, 0:w], rowT[:, slot, b * P:(b + 1) * P],
                                                    weight[:, b, col:col + w], start=(b == 0), stop=(b == kin - 1))
                    last.then_inc(product, 1)

        @block.scalar
        def _(ac):
            ac.sem_inc(copied, UN)
            ac.sem_inc(act_done, UN)
            with ac.Fori(0, T // UN) as i:
                def take(u):
                    ac.wait_ge(product, made(i, u))
                    if store:
                        before, per = uses(u, 2, UN)
                        ac.wait_ge(stored[u % 2], (i * per + before + 1) * 16)
                    take_act(i * UN + u, bank(u % 2), u % 2).then_inc(act_done, 1)

                for u, slot in steps:
                    ac.wait_ge(turned_s, made(i, u))
                    ac.wait_ge(product, free(i, u))
                    nc.scalar.copy(rowT[:, slot, :], ps_t[:, slot, 0:kin * P]).then_inc(copied, 1)
                    if u and take_act:
                        take(u - 1)
                if take_act:
                    take(UN - 1)

        if store:
            @block.sync
            def _(sp):
                dram, out = store
                for slot in range(2):
                    sp.sem_inc(stored[slot], 16)
                with sp.Fori(0, T // UN) as i:
                    for u, slot in steps:
                        sp.wait_ge(act_done, made(i, u))
                        settle(sp, c)
                        sp.dma_start(dram[bass.ds((i * UN + u) * P, P), :], out[:, slot, :]).then_inc(stored[slot], 16)
                for slot in range(2):
                    sp.wait_ge(stored[slot], 16 * (1 + T // UN * uses(slot, 2, UN)[1]))


H0, HD = 8, 32
QUAD = 17 * HD
FEAT = QUAD + HD + 1
BLOCKS = [(b * P, min(P, FEAT - b * P)) for b in range(-(-FEAT // P))]
NB = len(BLOCKS)
WRAP = HD + 16
MIX_SCALE = float(HD) ** 0.25
NORM_EPS = 1e-12


def shifted(buf, h):
    a = buf[:, h, :]
    step = a.ap[0]
    return (bass.AP(a.tensor, a.offset, [step, [1, 17], [1, HD]]), bass.AP(a.tensor, a.offset, [step, [0, 17], [1, HD]]))


def layer0_project(nc, s, c, g):
    with nc.sbuf_tensor("p0_wt", [P, 2, 2 * D + 3 * D], F32) as wt:
        turned(nc, s, c, "w0", [(g.w1_l, D, wt, 0), (g.w1_r, D, wt, D), (g.w_qkv[2 * D:3 * D, :], D, wt, 2 * D),
                                (g.w_qkv[0:2 * D, :], 2 * D, wt, 3 * D)])
        with ExitStack() as x:
            sb = lambda n, sh: x.enter_context(nc.sbuf_tensor("p0_" + n, sh, F32))
            yout, sq, ss = sb("yout", [P, 2, D]), sb("sq", [P, 2 * D]), sb("ss", [P, T, 2 * H0])
            xs, mv = g.x, sb("mv", [P, T, 2])
            bias1, bias_qkv = sb("bias1", [P, D]), sb("bias_qkv", [P, 3 * D])
            pre, post = sb("pre", [P, 2 * H0]), sb("post", [P, 2 * H0])
            loaded, filled, dve, act = s("p0_loaded"), s("p0_filled"), s("p0_dve2"), s("p0_act2")
            with nc.Block() as block:
                @block.vector
                def _(ve):
                    nc.vector.memset(xs[:, T - 1, :], 0.0).then_inc(filled, 1)

                @block.sync
                def _(sp):
                    sp.dma_start(bias1[:], g.b1[None, :].to_broadcast([P, D])).then_inc(loaded, 16)
                    sp.dma_start(bias_qkv[:], g.b_qkv[None, :].to_broadcast([P, 3 * D])).then_inc(loaded, 16)
                    sp.dma_start(post[:, 0:H0], g.temperature[None, :].to_broadcast([P, H0])).then_inc(loaded, 16)
                    sp.wait_ge(filled, 1)
                    full = (T - 1) * P
                    sp.dma_start(xs[:, 0:T - 1, :], g.x_in[0:full, :].rearrange("(t p) f -> p t f", p=P)).then_inc(loaded, 16)
                    sp.dma_start(xs[0:TAIL, T - 1, :], g.x_in[full:N, :]).then_inc(loaded, 16)
                    sp.wait_ge(loaded, 16 * 5)
            stats(nc, s, "ln0", xs, mv)

            def fill(row, k, lk):
                mean_rstd = tile(mv, k)
                return nc.vector.tensor_scalar(row, tile(xs, k), mean_rstd[:, 0:1], mean_rstd[:, 1:2], ALU.subtract, ALU.mult)

            def take_dve(k, bank, lk):
                v = nc.vector
                v.tensor_tensor(tile(g.own, k), bank(1)[:, 0:D], bias1[:], ALU.add)
                lk(v.tensor_tensor(tile(g.qk, k), bank(2)[:], bias_qkv[:, 0:2 * D], ALU.add))
                lk(v.tensor_tensor(sq[:], tile(g.qk, k), tile(g.qk, k), ALU.mult))
                lk(v.tensor_reduce(tile(ss, k), sq[:].rearrange("p (h d) -> p h d", d=HD), AX, ALU.add))
                return v.tensor_tensor(tile(g.v1, k).rearrange("p (h e) -> p h e", h=H0)[:, :, 0:HD],
                                       bank(1)[:, D:2 * D].rearrange("p (h e) -> p h e", h=H0),
                                       bias_qkv[:, 2 * D:3 * D].rearrange("p (h e) -> p h e", h=H0), ALU.add)

            def take_act(k, bank, slot):
                return nc.scalar.copy(yout[:, slot, :], bank(0)[:, 0:D])

            project(nc, s, c, "p0", 2, wt, [(0, D), (D, 2 * D), (3 * D, 2 * D)], fill, take_dve, take_act, 3,
                    store=(g.table_y, yout))
            with nc.Block() as block:
                @block.vector
                def _(ve):
                    v = nc.vector
                    lk = link(ve, dve)
                    v.memset(g.v1[:].rearrange("p t (h e) -> p (t h) e", h=H0)[:, :, HD:HD + 1], 1.0)
                    v.memset(pre[:, 0:H0], MIX_SCALE ** 2)
                    v.memset(pre[:, H0:2 * H0], 1.0)
                    v.tensor_scalar(post[:, 0:H0], post[:, 0:H0], MIX_SCALE ** 2, None, ALU.mult)
                    lk(v.memset(post[:, H0:2 * H0], MIX_SCALE))
                    wide = lambda a: a[:].unsqueeze(1).to_broadcast([P, T, 2 * H0])
                    lk(v.tensor_tensor(ss[:], ss[:], wide(pre), ALU.mult))
                    ve.wait_ge(act, 1)
                    lk(v.tensor_scalar(ss[:], ss[:], NORM_EPS, None, ALU.max))
                    lk(v.reciprocal(ss[:], ss[:]))
                    lk(v.tensor_tensor(ss[:], ss[:], wide(post), ALU.mult))
                    for t in range(0, T, UN):
                        qk = g.qk[:, t:t + UN, :].rearrange("p t (h d) -> p (t h) d", d=HD)
                        v.tensor_tensor(qk, qk, bcast(ss[:, t:t + UN, :].rearrange("p t h -> p (t h)"), HD), ALU.mult)
                    lk(v.tensor_scalar(g.v1[:, T - 1, :], g.v1[:, T - 1, :], c.valid[:, T - 1:T], None, ALU.mult))

                @block.scalar
                def _(ac):
                    ac.wait_ge(dve, 2)
                    nc.scalar.activation(ss[:], ss[:], ACT.Sqrt).then_inc(act, 1)


AHEAD = 4
UNITS = 512 // (HD + 1)
MBANKS = -(-H0 * NB // UNITS)
SLOTS = 4


def sage(nc, s, c, name, table, width, total, g, pre, beside, ring):
    quarter = BODY // GROUP
    got, copied_a = s(name + "_got"), s(name + "_index")
    gathered = [s(f"{name}_gathered{u}") for u in range(BODY)]
    placed = s(name + "_placed")
    hot_s, summed, added, ones_s = s(name + "_onehot"), s(name + "_summed"), s(name + "_added"), s(name + "_ones")
    with ExitStack() as x:
        rows_ = x.enter_context(nc.sbuf_tensor(name + "_rows", [P, BODY, width], F32))
        hot = x.enter_context(nc.sbuf_tensor(name + "_hot", [P, BODY, P], F32))
        table_ = x.enter_context(nc.sbuf_tensor(name + "_table", [P, AHEAD * 2, 2 * BODY], I32))
        now = x.enter_context(nc.sbuf_tensor(name + "_now", [P, quarter, 2, GROUP], I32))
        index = x.enter_context(nc.sbuf_tensor(name + "_ix", [P, BODY], I32))
        ps = [x.enter_context(nc.psum_tensor(f"{name}_ps{n}", [P, 512], F32)) for n in range(ring)]
        block = x.enter_context(nc.Block())
        made = lambda i, u: (i + 1) * BODY + u + 1
        added_by = lambda i, u: (i + AHEAD) * BODY + u + 1

        def loops(eng, body, extra):
            n = eng.value_load(c.loops[0:1, 0:1], min_val=T + 1, max_val=MAX_BODIES)
            with eng.Fori(0, T) as i:
                body(i, extra)
            with eng.Fori(T, n) as i:
                body(i, None)

        @block.sync
        def _(sp):
            def body(i, extra):
                sp.wait_ge(added, added_by(i - AHEAD, BODY - 1))
                settle(sp, c)
                for k, source in enumerate((g.table_a, g.table_b)):
                    sp.dma_start(table_[:, bass.ds((i % AHEAD) * 2 + k, 1), :].rearrange("p a w -> p (a w)"),
                                 source[bass.ds(i, 1), :, :].rearrange("b p w -> (b p) w")).then_inc(got, 16)
                sp.wait_ge(got, i * 32 + 32)
                settle(sp, c)
            loops(sp, body, None)

        @block.gpsimd
        def _(pool):
            pool.sem_inc(copied_a, quarter)

            def body(i, extra):
                pool.wait_ge(got, i * 32 + 32)
                settle(pool, c)
                for q in range(quarter):
                    pool.wait_ge(summed, made(i, q * GROUP + GROUP - 1) - BODY)
                    settle(pool, c)
                    nc.gpsimd.tensor_copy(index[:, q * GROUP:(q + 1) * GROUP], table_[:, bass.ds((i % AHEAD) * 2, 1), q * 2 * GROUP:q * 2 * GROUP + GROUP].rearrange("p a w -> p (a w)")).then_inc(copied_a, 1)
                    pool.wait_ge(copied_a, (i + 1) * quarter + q + 1)
                    settle(pool, c)
                    for u in range(q * GROUP, (q + 1) * GROUP):
                        nc.gpsimd.indirect_dma_start(rows_[:, u, 0:D], None, table,
                                                     bass.IndirectOffsetOnAxis(ap=index[:, u:u + 1], axis=0)).then_inc(gathered[u], 16)
            loops(pool, body, None)

        @block.vector
        def _(ve):
            v = nc.vector
            ve.sem_inc(hot_s, quarter)
            ve.sem_inc(added, AHEAD * BODY)
            if width > D:
                v.memset(rows_[:, :, D:width], 1.0).then_inc(ones_s, 1)
            if "dve" in pre:
                pre["dve"](ve)

            def one_hot(i, q):
                ve.wait_ge(summed, made(i, q * GROUP + GROUP - 1) - BODY)
                lk = link(ve, placed, i, quarter, q)
                lk(v.tensor_copy(now[:, q, :, :], table_[:, bass.ds((i % AHEAD) * 2, 2), q * 2 * GROUP + GROUP:(q + 1) * 2 * GROUP]))
                places = now[:, q, 0, :].bitcast(F32)
                v.tensor_tensor(hot[:, q * GROUP:(q + 1) * GROUP, :], c.col[:].unsqueeze(1).to_broadcast([P, GROUP, P]),
                                bcast(places, P), ALU.is_equal).then_inc(hot_s, 1)

            def body(i, extra):
                ve.wait_ge(got, i * 32 + 32)
                settle(ve, c)
                one_hot(i, 0)
                one_hot(i, 1)
                for u in range(BODY):
                    q = u // GROUP
                    if u % GROUP == 0 and 1 <= q and q + 1 < quarter:
                        one_hot(i, q + 1)
                    if u % GROUP == 0:
                        tiles = nc.values_load_multi_w_load_instructions(
                            now[0:1, q, 1, :], engines=[mybir.EngineType.DVE], min_val=0, max_val=T - 1,
                            skip_runtime_bounds_check_because=TRUSTED)[1]
                    t = tiles[u % GROUP]
                    if extra:
                        extra["dve"](ve, i, u)
                    ve.wait_ge(summed, made(i, u))
                    ve.wait_ge(added, added_by(i, u) - 1)
                    v.tensor_tensor(tile(total, t), tile(total, t), ps[u % ring][:, 0:width], ALU.add).then_inc(added, 1)
                if extra and "dve_end" in extra:
                    extra["dve_end"](ve, i)
            loops(ve, body, beside)

        @block.tensor
        def _(pe):
            pe.sem_inc(summed, BODY)
            if width > D:
                pe.wait_ge(ones_s, 1)
            if "pe" in pre:
                pre["pe"](pe)

            def body(i, extra):
                for u in range(BODY):
                    if u % GROUP == 0:
                        pe.wait_ge(hot_s, (i + 1) * quarter + u // GROUP + 1)
                    pe.wait_ge(gathered[u], i * 16 + 16)
                    pe.wait_ge(added, added_by(i, u) - back(u, ring, BODY))
                    nc.tensor.matmul(ps[u % ring][:, 0:width], hot[:, u, :], rows_[:, u, :], start=True, stop=True).then_inc(summed, 1)
                    if extra:
                        extra["pe"](pe, i, u)
            loops(pe, body, beside)

        if "act" in beside:
            @block.scalar
            def _(ac):
                pre["act"](ac)
                with ac.Fori(0, T) as i:
                    for u in range(BODY):
                        beside["act"](ac, i, u)


def features(nc, s, c, name, g, column, x):
    wrapped, made, linear, used = s(name + "_wrapped"), s(name + "_features"), s(name + "_linear"), s(name + "_used")
    vals = x.enter_context(nc.sbuf_tensor(name + "_vals", [P, H0, WRAP], F32))
    feat = x.enter_context(nc.sbuf_tensor(name + "_feat", [P, SLOTS, FEAT], F32))
    count = lambda i, h: (i + 1) * H0 + h + 1

    def act_start(ac):
        ac.sem_inc(linear, H0)

    def dve_start(ve):
        nc.vector.memset(feat[:, :, FEAT - 1:FEAT], 1.0).then_inc(made, H0)

    def wrap(ac, i):
        ac.wait_ge(made, (i + 1) * H0)
        ac.wait_ge(linear, (i + 1) * H0)
        heads = tile(g.qk, i)[:, column:column + D].rearrange("p (h d) -> p h d", d=HD)
        nc.scalar.copy(vals[:, :, 0:HD], heads).then_inc(wrapped, 1)
        nc.scalar.copy(vals[:, :, HD:WRAP], heads[:, :, 0:WRAP - HD]).then_inc(wrapped, 1)

    def lin(ac, i, h):
        ac.wait_ge(wrapped, i * 2 + 2)
        ac.wait_ge(used, count(i, h) - SLOTS)
        nc.scalar.copy(feat[:, h % SLOTS, QUAD:QUAD + HD], vals[:, h, 0:HD]).then_inc(linear, 1)

    def quad(ve, i, h):
        ve.wait_ge(wrapped, i * 2 + 2)
        ve.wait_ge(used, count(i, h) - SLOTS)
        other, own = shifted(vals, h)
        nc.vector.tensor_tensor(feat[:, h % SLOTS, 0:QUAD].rearrange("p (s i) -> p s i", i=HD), own, other, ALU.mult).then_inc(made, 1)

    def ready(pe, i, h):
        pe.wait_ge(made, count(i, h))
        pe.wait_ge(linear, count(i, h))
    return feat, used, act_start, dve_start, wrap, lin, quad, ready


def sage1_and_keys(nc, s, c, g):
    with ExitStack() as x:
        feat, used, act_start, dve_start, wrap, lin, quad, ready = features(nc, s, c, "kf", g, D, x)
        zero = x.enter_context(nc.sbuf_tensor("kf_zero", [1, P + 512], F32))
        ps_m = [x.enter_context(nc.psum_tensor(f"kf_m{n}", [P, 512], F32)) for n in range(MBANKS)]
        zeroed, weights, cleared = s("kf_zeroed"), s("kf_weights"), s("kf_cleared")
        place = lambda h, b: (ps_m[(h * NB + b) // UNITS], (h * NB + b) % UNITS * (HD + 1))

        def dve_pre(ve):
            nc.vector.memset(zero[:], 0.0).then_inc(zeroed, 1)
            nc.vector.memset(g.agg[:], 0.0).then_inc(cleared, 1)
            ve.wait_ge(cleared, 1)
            dve_start(ve)

        def pe_pre(pe):
            pe.sem_inc(used, H0)
            pe.wait_ge(zeroed, 1)
            pe.wait_ge(made0, H0)
            for m in ps_m:
                nc.tensor.matmul(m[:], zero[:, 0:P], zero[:, P:P + 512], start=True, stop=False, skip_group_check=True)

        def pe_beside(pe, i, u):
            if u % 2:
                h = u // 2
                ready(pe, i, h)
                for b, (f, w) in enumerate(BLOCKS):
                    m, col = place(h, b)
                    last = nc.tensor.matmul(m[0:w, col:col + HD + 1], feat[:, h % SLOTS, f:f + w],
                                            tile(g.v1, i)[:, h * (HD + 1):(h + 1) * (HD + 1)],
                                            start=False, stop=False, skip_group_check=True)
                last.then_inc(used, 1)

        def act_beside(ac, i, u):
            if u == 0:
                wrap(ac, i)
            if u % 2 == 0:
                lin(ac, i, u // 2)

        def dve_beside(ve, i, u):
            if u % 2 == 0:
                quad(ve, i, u // 2)

        made0 = s.known["kf_features"]
        sage(nc, s, c, "sage1", g.table_y, D + 1, g.agg, g, dict(dve=dve_pre, pe=pe_pre, act=act_start),
             dict(dve=dve_beside, pe=pe_beside, act=act_beside), 3)
        with nc.Block() as block:
            @block.vector
            def _(ve):
                v = nc.vector
                lk = link(ve, weights)
                w = g.mix_w[:].rearrange("p (h b) -> p h b", b=NB)
                lk(v.memset(w[:, :, 0:NB - 1], 1.0 / N))
                v.memset(w[0:HD, :, 0:1], 0.5 / N)
                lk(v.memset(w[0:HD, :, NB - 1:NB], 0.5 / N))
                lk(v.memset(w[HD:2 * HD, :, NB - 1:NB], MIX_SCALE ** 2 / N))
                lk(v.memset(w[2 * HD:P, :, NB - 1:NB], MIX_SCALE ** 4 / N))
                for n in range(MBANKS):
                    units = min(UNITS, H0 * NB - n * UNITS)
                    v.tensor_tensor(g.mix[:, n * UNITS:n * UNITS + units, :],
                                    ps_m[n][:, 0:units * (HD + 1)].rearrange("p (n e) -> p n e", e=HD + 1),
                                    bcast(g.mix_w[:, n * UNITS:n * UNITS + units], HD + 1), ALU.mult)


def sage2_and_queries(nc, s, c, g):
    with ExitStack() as x:
        feat, used, act_start, dve_start, wrap, lin, quad, ready = features(nc, s, c, "qf", g, 0, x)
        featT = x.enter_context(nc.sbuf_tensor("qf_featT", [P, 2, NB * P], F32))
        inv = x.enter_context(nc.sbuf_tensor("qf_inv", [P, H0], F32))
        ps_t = [x.enter_context(nc.psum_tensor(f"qf_t{n}", [P, 512], F32)) for n in range(4)]
        ps_y = x.enter_context(nc.psum_tensor("qf_y", [P, 512], F32))
        copied, made_y, taken, inv_s, cleared = s("qf_copied"), s("qf_made_y"), s("qf_taken"), s("qf_inv_s"), s("qf_cleared")
        count = lambda i, h: (i + 1) * H0 + h + 1

        def dve_pre(ve):
            nc.vector.memset(g.agg[:, :, 0:D], 0.0).then_inc(cleared, 1)
            ve.wait_ge(cleared, 1)
            ve.sem_inc(taken, 1)
            dve_start(ve)

        def pe_pre(pe):
            pe.sem_inc(used, H0)
            pe.sem_inc(made_y, H0)

        def turn(pe, i, h):
            ready(pe, i, h)
            pe.wait_ge(copied, count(i, h) - 2)
            for b, (f, w) in enumerate(BLOCKS):
                out = ps_t[2 * (h % 2)][:, b * P:(b + 1) * P] if b < NB - 1 else ps_t[2 * (h % 2) + 1][0:w, 0:P]
                last = nc.tensor.transpose(out, feat[:, h % SLOTS, f:f + w], c.ident[:])
            last.then_inc(used, 1)

        def times_mix(pe, i, h):
            pe.wait_ge(copied, count(i, h))
            if h == 0:
                pe.wait_ge(taken, i + 1)
            for b, (f, w) in enumerate(BLOCKS):
                last = nc.tensor.matmul(ps_y[:, h * (HD + 1):(h + 1) * (HD + 1)], featT[0:w, h % 2, b * P:(b + 1) * P],
                                        g.mix[0:w, h * NB + b, :], start=(b == 0), stop=(b == NB - 1))
            last.then_inc(made_y, 1)

        def pe_beside(pe, i, u):
            if u % 2 == 0:
                turn(pe, i, u // 2)
            elif u > 1:
                times_mix(pe, i, u // 2 - 1)
            if u == BODY - 1:
                times_mix(pe, i, H0 - 1)

        def act_pre(ac):
            act_start(ac)
            ac.sem_inc(copied, H0)

        def act_beside(ac, i, u):
            if u == 0:
                wrap(ac, i)
            if u % 2 == 0:
                lin(ac, i, u // 2)
            else:
                h = u // 2
                ac.wait_ge(used, count(i, h))
                ac.wait_ge(made_y, count(i, h) - 2)
                w = BLOCKS[-1][1]
                nc.scalar.copy(featT[:, h % 2, 0:(NB - 1) * P], ps_t[2 * (h % 2)][:])
                nc.scalar.copy(featT[0:w, h % 2, (NB - 1) * P:NB * P], ps_t[2 * (h % 2) + 1][0:w, 0:P]).then_inc(copied, 1)

        def dve_beside(ve, i, u):
            if u % 2 == 0:
                quad(ve, i, u // 2)

        def dve_end(ve, i):
            ve.wait_ge(made_y, (i + 2) * H0)
            y = ps_y[:, 0:H0 * (HD + 1)].rearrange("p (h e) -> p h e", e=HD + 1)
            nc.vector.reciprocal(inv[:], y[:, :, HD]).then_inc(inv_s, 1)
            ve.wait_ge(inv_s, i + 1)
            nc.vector.tensor_tensor(tile(g.qk, i)[:, 0:D].rearrange("p (h e) -> p h e", e=HD), y[:, :, 0:HD],
                                    bcast(inv[:], HD), ALU.mult).then_inc(taken, 1)

        sage(nc, s, c, "sage2", g.table_y, D, g.agg[:, :, 0:D], g, dict(dve=dve_pre, pe=pe_pre, act=act_pre),
             dict(dve=dve_beside, dve_end=dve_end, pe=pe_beside, act=act_beside), 3)


def sage1_finish(nc, s, c, g):
    with ExitStack() as x:
        sb = lambda n, sh: x.enter_context(nc.sbuf_tensor("p1_" + n, sh, F32))
        wt, yout, bias2, mid = sb("wt", [P, 2, 2 * D]), sb("yout", [P, 2, D]), sb("bias2", [P, D]), sb("mid", [P, 2, D])
        dve, loaded = s("p1_dve2"), s("p1_loaded")
        turned(nc, s, c, "w1", [(g.w2_l, D, wt, 0), (g.w2_r, D, wt, D)])
        with nc.Block() as block:
            @block.sync
            def _(sp):
                sp.dma_start(bias2[:], g.b2[None, :].to_broadcast([P, D])).then_inc(loaded, 16)
                sp.wait_ge(loaded, 16)

            @block.vector
            def _(ve):
                lk = link(ve, dve)
                lk(nc.vector.tensor_scalar(g.inv_deg[:], g.agg[:, :, D], 1.0, None, ALU.max))
                lk(nc.vector.reciprocal(g.inv_deg[:], g.inv_deg[:]))

        def fill(row, k, lk):
            v = nc.vector
            lk(v.scalar_tensor_tensor(row, tile(g.agg, k)[:, 0:D], tile_col(g.inv_deg, k), tile(g.own, k), ALU.mult, ALU.add))
            return v.tensor_scalar(row, row, 0.0, None, ALU.max)

        def take_dve(k, bank, lk):
            return nc.vector.tensor_tensor(tile(g.own, k), bank(1)[:, 0:D], bias2[:], ALU.add)

        def take_act(k, bank, slot):
            return nc.scalar.copy(yout[:, slot, :], bank(0)[:, 0:D])

        project(nc, s, c, "p1", 2, wt, [(0, D), (D, D)], fill, take_dve, take_act, 1, store=(g.table_y, yout))


def tile_col(buf, k):
    return buf[:, bass.ds(k, 1)]


def normed(nc, s, name, x, out):
    with nc.sbuf_tensor(name + "_mv", [P, T, 2], F32) as mv:
        stats(nc, s, name, x, mv)
        with nc.Block() as block:
            @block.vector
            def _(ve):
                for t in range(T):
                    nc.vector.tensor_scalar(out[:, t, :], x[:, t, :], mv[:, t, 0:1], mv[:, t, 1:2], ALU.subtract, ALU.mult)


def layer0_join(nc, s, c, g):
    with ExitStack() as x:
        sb = lambda n, sh: x.enter_context(nc.sbuf_tensor("j0_" + n, sh, F32))
        wt, bias = sb("wt", [P, 2, D]), sb("bias", [P, D])
        loaded = s("j0_loaded")
        turned(nc, s, c, "wj", [(g.w_proj, D, wt, 0)])
        with nc.Block() as block:
            @block.sync
            def _(sp):
                sp.dma_start(bias[:], g.b_proj[None, :].to_broadcast([P, D])).then_inc(loaded, 16)
                sp.wait_ge(loaded, 16)

        def fill(row, k, lk):
            return nc.vector.tensor_copy(row, tile(g.qk, k)[:, 0:D])

        def take_dve(k, bank, lk):
            v = nc.vector
            lk(v.scalar_tensor_tensor(tile(g.own, k), tile(g.agg, k)[:, 0:D], tile_col(g.inv_deg, k), tile(g.own, k), ALU.mult, ALU.add))
            v.tensor_tensor(tile(g.x, k), tile(g.x, k), bias[:], ALU.add)
            lk(v.tensor_tensor(tile(g.own, k), tile(g.own, k), bank(0)[:, 0:D], ALU.add))
            return v.tensor_tensor(tile(g.x, k), tile(g.x, k), tile(g.own, k), ALU.add)

        project(nc, s, c, "j0", 2, wt, [(0, D)], fill, take_dve, None, 2)


def route(nc, s, c, name, g, ne, tiles, gate_w, gate_b, renorm):
    r = g.route
    with ExitStack() as x:
        sb = lambda n, sh, d=F32: x.enter_context(nc.sbuf_tensor(f"{name}_{n}", sh, d))
        wg, bg = sb("wg", [P, 2, ne]), sb("bg", [P, ne])
        prob = sb("prob", [P, T, ne])
        loaded = s(name + "_loaded")
        with nc.Block() as block:
            @block.sync
            def _(sp):
                sp.dma_start(wg[:], gate_w.rearrange("(b p) e -> p b e", p=P)).then_inc(loaded, 16)
                sp.dma_start(bg[:], gate_b[None, :].to_broadcast([P, ne])).then_inc(loaded, 16)
                sp.wait_ge(loaded, 32)

        def fill(row, k, lk):
            return nc.vector.tensor_copy(row, tile(g.xn, k))

        def take_dve(k, bank, lk):
            return nc.vector.tensor_tensor(tile(prob, k), bank(0)[:, 0:ne], bg[:], ALU.add)

        project(nc, s, c, name + "g", 2, wg, [(0, ne)], fill, take_dve, None, 0)

        one, two, both = sb("one", [P, T, ne]), sb("two", [P, T, ne]), sb("both", [P, T, ne])
        m, top, which = sb("m", [P, T]), sb("top", [P, T, 8]), sb("which", [P, T, 8], U32)
        whichf, eid = sb("whichf", [P, T, 8]), sb("eid", [P, T, ne])
        tot, run, pos = sb("tot", [P, ne, T]), sb("run", [P, ne, T]), sb("pos", [P, T, ne])
        ones_row = sb("ones_row", [P, ne * T])
        cnt, tl, first, tli, base = (sb(n, [P, ne]) for n in ("cnt", "tl", "first", "tli", "base"))
        cnt_i = sb("cnt_i", [P, ne], I32)
        tno, over, sl = sb("tno", [P, tiles, ne]), sb("over", [P, tiles, ne]), sb("sl", [P, T])
        exf = sb("exf", [P, tiles])
        ps_in, ps_all = (x.enter_context(nc.psum_tensor(f"{name}_{n}", [P, 512], F32)) for n in ("ps_in", "ps_all"))
        dve, act, chosen, counted, made, index, sent = (s(f"{name}_{n}") for n in ("dve", "act", "chosen", "counted", "made", "index", "sent"))
        with nc.Block() as block:
            @block.gpsimd
            def _(pool):
                fl = dict(allow_small_or_imprecise_dtypes=True)
                nc.gpsimd.iota(eid[:], [[0, T], [1, ne]], base=0, channel_multiplier=0, **fl).then_inc(made, 1)
                nc.gpsimd.iota(tno[:], [[1, tiles], [0, ne]], base=0, channel_multiplier=0, **fl).then_inc(made, 1)
                for k, (slot, n) in enumerate([(q, t) for t in range(T) for q in (r.slot1, r.slot2)]):
                    rows_n = P if n < T - 1 else TAIL
                    if k == 0:
                        pool.wait_ge(index, 2)
                    nc.gpsimd.indirect_dma_start(g.sorted_x, bass.IndirectOffsetOnAxis(ap=slot[0:rows_n, n:n + 1], axis=0),
                                                 g.xn[0:rows_n, n, :], None).then_inc(sent, 16)
                pool.wait_ge(sent, 16 * 2 * T)

            @block.scalar
            def _(ac):
                ac.wait_ge(dve, 2)
                nc.scalar.activation(prob[:], prob[:], ACT.Exp).then_inc(act, 1)

            @block.tensor
            def _(pe):
                pe.wait_ge(chosen, 1)
                nc.tensor.matmul(ps_in[:, 0:T * ne], c.after[:], both[:].rearrange("p t e -> p (t e)"), start=True, stop=True)
                nc.tensor.matmul(ps_all[:, 0:T * ne], c.ones[:], both[:].rearrange("p t e -> p (t e)"), start=True, stop=True).then_inc(counted, 1)

            @block.vector
            def _(ve):
                v = nc.vector
                lk = link(ve, dve)
                lk(v.tensor_reduce(m[:], prob[:], AX, ALU.max))
                lk(v.tensor_tensor(prob[:], prob[:], bcast(m[:], ne), ALU.subtract))
                ve.wait_ge(act, 1)
                lk(v.tensor_reduce(m[:], prob[:], AX, ALU.add))
                lk(v.reciprocal(m[:], m[:]))
                lk(v.tensor_tensor(prob[:], prob[:], bcast(m[:], ne), ALU.mult))
                for t in range(T):
                    v.max(top[:, t, :], prob[:, t, :]).then_inc(dve, 1)
                lk.count[0] += T
                ve.wait_ge(dve, lk.count[0])
                for t in range(T):
                    v.max_index(which[:, t, :], top[:, t, :], prob[:, t, :]).then_inc(dve, 1)
                lk.count[0] += T
                ve.wait_ge(dve, lk.count[0])
                lk(v.tensor_copy(whichf[:], which[:]))
                ve.wait_ge(made, 2)
                for e, k in ((one, 0), (two, 1)):
                    lk(v.tensor_tensor(e[:], eid[:], bcast(whichf[:, :, k], ne), ALU.is_equal))
                    lk(v.tensor_tensor(e[:], e[:], bcast(c.valid[:], ne), ALU.mult))
                v.tensor_tensor(both[:], one[:], two[:], ALU.add).then_inc(chosen, 1)
                if renorm:
                    lk(v.tensor_tensor(m[:], top[:, :, 0], top[:, :, 1], ALU.add))
                    lk(v.reciprocal(m[:], m[:]))
                    v.tensor_tensor(r.w1[:], top[:, :, 0], m[:], ALU.mult)
                    v.tensor_tensor(r.w2[:], top[:, :, 1], m[:], ALU.mult)
                else:
                    v.tensor_copy(r.w1[:], top[:, :, 0])
                    v.tensor_copy(r.w2[:], top[:, :, 1])
                ve.wait_ge(counted, 1)
                lk(v.memset(ones_row[:], 1.0))
                lk(v.tensor_copy(tot[:], ps_all[:, 0:T * ne].rearrange("p (t e) -> p e t", e=ne)))
                flat = lambda a: a[:].rearrange("p e t -> p (e t)")
                lk(v.tensor_tensor_scan(flat(run), ones_row[:], flat(tot), 0.0, ALU.mult, ALU.add))
                lk(v.tensor_copy(cnt[:, 0:1], run[:, 0:1, T - 1]))
                lk(v.tensor_tensor(cnt[:, 1:ne], run[:, 1:ne, T - 1], run[:, 0:ne - 1, T - 1], ALU.subtract))
                lk(v.tensor_scalar(tl[:], cnt[:], float(P - 1), None, ALU.add))
                lk(v.tensor_copy(cnt_i[:], tl[:]))
                lk(v.tensor_single_scalar(cnt_i[:], cnt_i[:], 7, ALU.arith_shift_right))
                lk(v.tensor_copy(tl[:], cnt_i[:]))
                lk(v.tensor_tensor_scan(tli[:], ones_row[:, 0:ne], tl[:], 0.0, ALU.mult, ALU.add))
                lk(v.tensor_tensor(first[:], tli[:], tl[:], ALU.subtract))
                lk(v.tensor_tensor(base[:], run[:, :, T - 1], cnt[:], ALU.subtract))
                lk(v.scalar_tensor_tensor(base[:], first[:], float(P), base[:], ALU.mult, ALU.subtract))
                lk(v.tensor_tensor(run[:], run[:], tot[:], ALU.subtract))
                lk(v.tensor_tensor(run[:], run[:], bcast(base[:], T), ALU.add))
                lk(v.tensor_tensor(pos[:], ps_in[:, 0:T * ne].rearrange("p (t e) -> p t e", e=ne), run[:].rearrange("p e t -> p t e"), ALU.add))
                for e, slot in ((one, r.slot1), (two, r.slot2)):
                    lk(v.tensor_tensor(e[:], e[:], pos[:], ALU.mult))
                    lk(v.tensor_reduce(sl[:], e[:], AX, ALU.add))
                    v.tensor_copy(slot[:], sl[:]).then_inc(index, 1)
                lk(v.tensor_tensor(over[:], tno[:], tli[:].unsqueeze(1).to_broadcast([P, tiles, ne]), ALU.is_ge))
                lk(v.tensor_reduce(exf[:], over[:], AX, ALU.add))
                lk(v.tensor_scalar(exf[:], exf[:], float(ne - 1), None, ALU.min))
                lk(v.tensor_copy(r.expert[:, 0:tiles], exf[0:1, :]))
                lk(v.tensor_copy(over[0:1, :, 0], exf[0:1, :]))
                lk(v.memset(r.fresh[:], 1))
                lk(v.tensor_tensor(exf[0:1, 2:tiles], exf[0:1, 2:tiles], over[0:1, 0:tiles - 2, 0], ALU.not_equal))
                lk(v.tensor_copy(r.fresh[:, 2:tiles], exf[0:1, 2:tiles]))


def experts(nc, s, c, name, g, tiles, hidden, w_in, w_out, act, b_in=None, b_out=None):
    HB = hidden // P
    nw = len(w_in)
    with ExitStack() as x:
        sb = lambda n, sh: x.enter_context(nc.sbuf_tensor(f"{name}_{n}", sh, F32))
        wi = [sb(f"wi{n}", [P, 2, 2, hidden]) for n in range(nw)]
        wo = sb("wo", [P, 2, HB, D])
        xin, xT, out = sb("xin", [P, 2, D]), sb("xT", [P, 2, D]), sb("out", [P, 2, D])
        gate, hid = sb("gate", [P, 2, hidden]), sb("hid", [P, 2, hidden])
        if b_in is not None:
            bias_in, bias_out = sb("bias_in", [P, 2, HB]), sb("bias_out", [P, 2, D])
        ps_t = x.enter_context(nc.psum_tensor(name + "_ps_t", [P, 512], F32))
        ps_h = [[x.enter_context(nc.psum_tensor(f"{name}_ps_h{n}{k}", [P, 512], F32)) for k in range(2)] for n in range(nw)]
        ps_o = [x.enter_context(nc.psum_tensor(f"{name}_ps_o{k}", [P, 512], F32)) for k in range(2)]
        more = 1 if b_in is not None else 0
        loaded_x, loaded_in, loaded_out = ([s(f"{name}_loaded_{w}{k}") for k in range(2)] for w in ("x", "in", "out"))
        stored = [s(f"{name}_stored{k}") for k in range(2)]
        turned_s, copied, hidden_s, gated, ready, made, taken = (
            s(f"{name}_{n}") for n in ("turned", "copied", "hidden", "gated", "ready", "made", "taken"))
        block = x.enter_context(nc.Block())

        done = lambda i: i + 1 + 2

        def steps(eng, step):
            step(0, 0, 0, first=True)
            with eng.Fori(0, (tiles - 2) // 2) as j:
                step(2 * j + 1, 1, j)
                step(2 * j + 2, 0, j + 1)
            step(tiles - 1, 1, tiles // 2 - 1, last=True)

        before = lambda k, n: n if k else n - 1
        behind = lambda k, n: n + 1 if k else n

        @block.sync
        def _(sp):
            with sp.Fori(0, tiles // 2) as j:
                for k in range(2):
                    i = 2 * j + k
                    e = sp.value_load(g.route.expert[0:1, bass.ds(i, 1)], min_val=0, max_val=w_out.shape[0] - 1)
                    fresh = sp.value_load(g.route.fresh[0:1, bass.ds(i, 1)], min_val=0, max_val=1)
                    one = lambda a: a[bass.ds(e, 1)]
                    sp.wait_ge(hidden_s, done(i) - 2)
                    settle(sp, c)
                    if more:
                        sp.wait_ge(ready, done(i) - 2)
                        settle(sp, c)
                    with sp.If(fresh > 0):
                        for n in range(nw):
                            sp.dma_start(wi[n][:, k], one(w_in[n]).rearrange("o (b p) f -> p (o b) f", p=P)).then_inc(loaded_in[k], 16)
                        if more:
                            with nc.allow_non_contiguous_dma(reason="one value per hidden column"):
                                sp.dma_start(bias_in[:, k, :], one(b_in).rearrange("o (b p) -> p (o b)", p=P)).then_inc(loaded_in[k], 16)
                    with sp.If(fresh < 1):
                        sp.sem_inc(loaded_in[k], 16 * (nw + more))
                    sp.wait_ge(made, done(i) - 2)
                    if more:
                        sp.wait_ge(taken, done(i) - 2)
                    settle(sp, c)
                    with sp.If(fresh > 0):
                        sp.dma_start(wo[:, k], one(w_out).rearrange("o (b p) f -> p (o b) f", p=P)).then_inc(loaded_out[k], 16)
                        if more:
                            sp.dma_start(bias_out[:, k, :], one(b_out).to_broadcast([P, D])).then_inc(loaded_out[k], 16)
                    with sp.If(fresh < 1):
                        sp.sem_inc(loaded_out[k], 16 * (1 + more))

        @block.gpsimd
        def _(pool):
            with pool.Fori(0, tiles // 2) as j:
                for k in range(2):
                    i = 2 * j + k
                    pool.wait_ge(turned_s, done(i) - 2)
                    settle(pool, c)
                    pool.dma_start(xin[:, k, :], g.sorted_x[bass.ds(i * P, P), :]).then_inc(loaded_x[k], 16)

        @block.tensor
        def _(pe):
            for count in (turned_s, hidden_s, made):
                pe.sem_inc(count, 2)

            def turn(i, k, n):
                pe.wait_ge(loaded_x[k], (n + 1) * 16)
                pe.wait_ge(copied, done(i) - 1)
                for b in range(2):
                    last = nc.tensor.transpose(ps_t[:, b * P:(b + 1) * P], xin[:, k, b * P:(b + 1) * P], c.ident[:])
                last.then_inc(turned_s, 1)

            def hide(i, k, n):
                pe.wait_ge(loaded_in[k], (n + 1) * (16 * (nw + more)))
                pe.wait_ge(copied, done(i))
                pe.wait_ge(ready, done(i) - 2)
                for m in range(nw):
                    for hb in range(HB):
                        o = ps_h[m][k][:, hb * P:(hb + 1) * P]
                        for b in range(2):
                            last = nc.tensor.matmul(o, wi[m][:, k, b, hb * P:(hb + 1) * P], xT[:, k, b * P:(b + 1) * P],
                                                    start=(b == 0), stop=(b == 1))
                last.then_inc(hidden_s, 1)

            def give(i, k, n):
                pe.wait_ge(loaded_out[k], (n + 1) * (16 * (1 + more)))
                pe.wait_ge(ready, done(i))
                pe.wait_ge(taken, done(i) - 2)
                o = ps_o[k][:, 0:D]
                for hb in range(HB):
                    last = nc.tensor.matmul(o, hid[:, k, hb * P:(hb + 1) * P], wo[:, k, hb, :],
                                            start=(hb == 0), stop=(hb == HB - 1))
                last.then_inc(made, 1)

            def step(i, k, n, first=False, last=False):
                if first:
                    turn(i, k, n)
                hide(i, k, n)
                if not last:
                    turn(i + 1, 1 - k, behind(k, n))
                if not first:
                    give(i - 1, 1 - k, before(k, n))
                if last:
                    give(i, k, n)

            steps(pe, step)

        @block.scalar
        def _(ac):
            ac.sem_inc(copied, 2)
            for k in range(2):
                ac.sem_inc(stored[k], 16)
            hidden_by = gated if nw > 1 else ready
            if nw == 1:
                ac.sem_inc(ready, 2)

            def copy(i, k):
                ac.wait_ge(turned_s, done(i))
                ac.wait_ge(hidden_s, done(i) - 2)
                nc.scalar.copy(xT[:, k, :], ps_t[:, 0:D]).then_inc(copied, 1)

            def store(i, k):
                ac.wait_ge(taken, done(i))
                settle(ac, c)
                ac.dma_start(g.sorted_y[bass.ds(i * P, P), :], out[:, k, :]).then_inc(stored[k], 16)

            def step(i, k, n, first=False, last=False):
                if first:
                    copy(i, k)
                ac.wait_ge(hidden_s, done(i))
                ac.wait_ge(ready if nw > 1 else made, done(i) - 2)
                to = gate if nw > 1 else hid
                if more:
                    for hb in range(HB):
                        a = slice(hb * P, (hb + 1) * P)
                        ins = nc.scalar.activation(to[:, k, a], ps_h[0][k][:, a], act, bias=bias_in[:, k, hb:hb + 1])
                else:
                    ins = nc.scalar.activation(to[:, k, :], ps_h[0][k][:], act)
                ins.then_inc(hidden_by, 1)
                if not last:
                    copy(i + 1, 1 - k)
                if not first:
                    store(i - 1, 1 - k)
                if last:
                    store(i, k)

            steps(ac, step)
            for k in range(2):
                ac.wait_ge(stored[k], 16 * (1 + tiles // 2))

        @block.vector
        def _(ve):
            ve.sem_inc(taken, 2)
            if nw > 1:
                ve.sem_inc(ready, 2)

            def take(i, k, n):
                ve.wait_ge(made, done(i))
                ve.wait_ge(stored[k], (n + 1) * 16)
                if more:
                    ins = nc.vector.tensor_tensor(out[:, k, :], ps_o[k][:, 0:D], bias_out[:, k, :], ALU.add)
                else:
                    ins = nc.vector.tensor_copy(out[:, k, :], ps_o[k][:, 0:D])
                ins.then_inc(taken, 1)

            def step(i, k, n, first=False, last=False):
                if nw > 1:
                    ve.wait_ge(gated, i + 1)
                    ve.wait_ge(made, done(i) - 2)
                    nc.vector.tensor_tensor(hid[:, k, :], gate[:, k, :], ps_h[1][k][:], ALU.mult).then_inc(ready, 1)
                if not first:
                    take(i - 1, 1 - k, before(k, n))
                if last:
                    take(i, k, n)

            steps(ve, step)


def combine(nc, s, c, name, g, out=None):
    r = g.route
    SL = 4
    with ExitStack() as x:
        y = [x.enter_context(nc.sbuf_tensor(f"{name}_y{n}", [P, SL, D], F32)) for n in range(2)]
        got = [s(f"{name}_got{n}") for n in range(SL)]
        first, added, stored = s(name + "_first"), s(name + "_added"), s(name + "_stored")
        with nc.Block() as block:
            @block.gpsimd
            def _(pool):
                for t in range(T):
                    if t >= SL:
                        pool.wait_ge(added, t - SL + 1)
                    for n, slot in enumerate((r.slot1, r.slot2)):
                        nc.gpsimd.indirect_dma_start(y[n][:, t % SL, :], None, g.sorted_y,
                                                     bass.IndirectOffsetOnAxis(ap=slot[:, t:t + 1], axis=0)).then_inc(got[t % SL], 16)

            @block.vector
            def _(ve):
                v = nc.vector
                for t in range(T):
                    ve.wait_ge(got[t % SL], 32 * (t // SL + 1))
                    v.scalar_tensor_tensor(g.x[:, t, :], y[0][:, t % SL, :], r.w1[:, t:t + 1], g.x[:, t, :], ALU.mult, ALU.add).then_inc(first, 1)
                    ve.wait_ge(first, t + 1)
                    v.scalar_tensor_tensor(g.x[:, t, :], y[1][:, t % SL, :], r.w2[:, t:t + 1], g.x[:, t, :], ALU.mult, ALU.add).then_inc(added, 1)

            if out is not None:
                @block.sync
                def _(sp):
                    full = (T - 1) * P
                    for t in range(0, T - 1, 4):
                        sp.wait_ge(added, t + 4)
                        sp.dma_start(out[t * P:(t + 4) * P, :].rearrange("(t p) f -> p t f", p=P), g.x[:, t:t + 4, :]).then_inc(stored, 16)
                    sp.wait_ge(added, T)
                    sp.dma_start(out[full:N, :], g.x[0:TAIL, T - 1, :]).then_inc(stored, 16)
                    sp.wait_ge(stored, 16 * ((T - 1) // 4 + 1))


H1, HEADS1 = 32, 4
C1 = H1 * HEADS1
MEM = 4
SLOPE = 0.2
GAT_HEADS = 2
UP = 20
WIDE = 2 * BODY


def layer1_project(nc, s, c, g):
    W = 2 * C1 + 3 * C1
    with ExitStack() as x:
        sb = lambda n, sh: x.enter_context(nc.sbuf_tensor("p2_" + n, sh, F32))
        wt, gp, sq, rn = sb("wt", [P, 2, W]), sb("gp", [P, 2]), sb("sq", [P, D]), sb("rn", [P, T])
        loaded, dve, act = s("p2_loaded"), s("p2_dve2"), s("p2_act2")
        with nc.Block() as block:
            @block.sync
            def _(sp):
                k_out = lambda a: a.rearrange("(b p) o -> p b o", p=P)
                sp.dma_start(wt[:, :, 0:C1], k_out(g.wl0)).then_inc(loaded, 16)
                sp.dma_start(wt[:, :, C1:2 * C1], k_out(g.wr0)).then_inc(loaded, 16)
                sp.dma_start(wt[:, :, 2 * C1:3 * C1], k_out(g.w_qkv1[:, 2 * C1:3 * C1])).then_inc(loaded, 16)
                sp.dma_start(wt[:, :, 3 * C1:W], k_out(g.w_qkv1[:, 0:2 * C1])).then_inc(loaded, 16)
                with nc.allow_non_contiguous_dma(reason="256 values, one per weight row"):
                    sp.dma_start(gp[:], g.g_pre.rearrange("(b p) -> p b", p=P)).then_inc(loaded, 16)

            @block.vector
            def _(ve):
                v = nc.vector
                lk = link(ve, dve)
                for t in range(T):
                    lk(v.tensor_tensor_reduce(sq[:], g.xn[:, t, :], g.xn[:, t, :], 1.0, 0.0, ALU.mult, ALU.add, rn[:, t:t + 1]))
                ve.wait_ge(loaded, 80)
                for b in range(2):
                    v.tensor_scalar(wt[:, b, 2 * C1:W], wt[:, b, 2 * C1:W], gp[:, b:b + 1], float(D) ** 0.5, ALU.mult, ALU.mult)
                ve.wait_ge(act, 1)
                lk(v.tensor_scalar(rn[:], rn[:], NORM_EPS, None, ALU.max))
                lk(v.reciprocal(rn[:], rn[:]))

            @block.scalar
            def _(ac):
                ac.wait_ge(dve, T)
                nc.scalar.activation(rn[:], rn[:], ACT.Sqrt).then_inc(act, 1)

        def fill(row, k, lk):
            return nc.vector.tensor_copy(row, tile(g.xn, k))

        def take_dve(k, bank, lk):
            v = nc.vector
            v.tensor_copy(tile(g.xr, k), bank(1)[:, 0:C1])
            v.tensor_scalar(tile(g.vv, k), bank(1)[:, C1:2 * C1], tile_col(rn, k), None, ALU.mult)
            v.tensor_scalar(tile(g.kk, k), bank(2)[:, C1:2 * C1], tile_col(rn, k), None, ALU.mult)
            return v.tensor_scalar(tile(g.qq, k), bank(2)[:, 0:C1], tile_col(rn, k), None, ALU.mult)

        yout = sb("yout", [P, 2, C1])

        def take_act(k, bank, slot):
            nc.scalar.copy(tile(g.att, k), bank(0)[:, 0:C1])
            return nc.scalar.copy(yout[:, slot, :], bank(0)[:, 0:C1])

        project(nc, s, c, "p2", 2, wt, [(0, C1), (C1, 2 * C1), (3 * C1, 2 * C1)], fill, take_dve, take_act, 0, store=(g.table_l, yout))


def attention1(nc, s, c, g):
    with ExitStack() as x:
        sb = lambda n, sh: x.enter_context(nc.sbuf_tensor("la_" + n, sh, F32))
        wp, bias, gout = sb("wp", [P, 1, D]), sb("bias", [P, D]), sb("gout", [P, D])
        o, ss = g.xr2, sb("ss", [P, T])
        with ExitStack() as y:
            sb = lambda n, sh: y.enter_context(nc.sbuf_tensor("la_" + n, sh, F32))
            pen, km, top, mk, mv = sb("pen", [P, 1]), sb("km", [P, C1]), sb("top", [P, 2]), sb("mk", [P, MEM]), sb("mv", [P, MEM])
            diag, mrow, mkT, mvT = sb("diag", [P, P]), sb("mrow", [P, C1]), sb("mkT", [MEM, C1]), sb("mvT", [MEM, C1])
            wout, ctx_m, z = sb("wout", [P, D]), sb("ctx_m", [P, P]), sb("z", [P, 1])
            qm = sb("qm", [P, T * HEADS1])
            ps = [y.enter_context(nc.psum_tensor(f"la_ps{n}", [P, 512], F32)) for n in range(5)]
            loaded, dve, act, pe_s = s("la_loaded"), s("la_dve"), s("la_act"), s("la_pe")
            kmx, qe, ke, cx, ctxd = s("la_keymax"), s("la_q"), s("la_k"), s("la_diag"), s("la_masked")
            with nc.Block() as block:
                @block.sync
                def _(sp):
                    sp.dma_start(mk[:], g.mem_kv[0].rearrange("h d m -> (h d) m")).then_inc(loaded, 16)
                    sp.dma_start(mv[:], g.mem_kv[1].rearrange("h d m -> (h d) m")).then_inc(loaded, 16)
                    sp.dma_start(wout[:], g.w_out1).then_inc(loaded, 16)
                    sp.dma_start(bias[:], g.b_out1[None, :].to_broadcast([P, D])).then_inc(loaded, 16)
                    sp.dma_start(gout[:], g.g_out1[None, :].to_broadcast([P, D])).then_inc(loaded, 16)

                @block.vector
                def _(ve):
                    v = nc.vector
                    lk = link(ve, dve)
                    last = g.kk[:, T - 1, :]
                    lk(v.tensor_scalar(pen[:], c.valid[:, T - 1:T], -LOW, LOW, ALU.mult, ALU.add))
                    lk(v.tensor_scalar(last, last, c.valid[:, T - 1:T], pen[:, 0:1], ALU.mult, ALU.add))
                    v.tensor_reduce(km[:], g.kk[:].rearrange("p t c -> p c t"), AX, ALU.max).then_inc(kmx, 1)
                    q = g.qq[:].rearrange("p t (h d) -> p (t h) d", d=H1)
                    lk(v.tensor_reduce(qm[:], q, AX, ALU.max))
                    v.tensor_tensor(q, q, bcast(qm[:], H1), ALU.subtract).then_inc(qe, 1)
                    ve.wait_ge(loaded, 80)
                    lk(v.tensor_reduce(top[:, 0:1], mk[:], AX, ALU.max))
                    ve.wait_ge(pe_s, 1)
                    lk(v.tensor_reduce(top[:, 1:2], ps[0][:, 0:P], AX, ALU.max))
                    lk(v.tensor_tensor(top[:, 0:1], top[:, 0:1], top[:, 1:2], ALU.max))
                    v.tensor_scalar(diag[:], c.ident[:], top[:, 0:1], None, ALU.mult).then_inc(cx, 1)
                    ve.wait_ge(pe_s, 2)
                    lk(v.tensor_copy(mrow[:], ps[1][:, 0:C1]))
                    lk(v.tensor_tensor(mkT[:], ps[0][0:MEM, P:2 * P], mrow[0:MEM, :], ALU.subtract))
                    lk(v.tensor_copy(mvT[:], ps[0][0:MEM, 2 * P:3 * P]))
                    v.tensor_tensor(g.kk[:], g.kk[:], mrow[:].unsqueeze(1).to_broadcast([P, T, C1]), ALU.subtract).then_inc(ke, 1)
                    ve.wait_ge(act, 1)
                    lk(v.tensor_reduce(qm[:], q, AX, ALU.add))
                    lk(v.reciprocal(qm[:], qm[:]))
                    lk(v.tensor_tensor(q, q, bcast(qm[:], H1), ALU.mult))
                    ve.wait_ge(pe_s, 3)
                    v.tensor_tensor(ctx_m[:], ps[2][:, 0:P], c.head[:].rearrange("p h d -> p (h d)"), ALU.mult).then_inc(ctxd, 1)
                    lk(v.reciprocal(z[:], ps[3][:, 0:1]))
                    lk(v.tensor_scalar(z[:], z[:], float(H1) ** -0.5, None, ALU.mult))
                    lk(v.tensor_scalar(gout[:], gout[:], float(D) ** 0.5, None, ALU.mult))
                    ve.wait_ge(pe_s, 4)
                    lk(v.tensor_scalar(wp[:, 0, :], ps[4][:, 0:D], z[:, 0:1], None, ALU.mult))

                @block.scalar
                def _(ac):
                    ac.wait_ge(qe, 1)
                    nc.scalar.activation(g.qq[:], g.qq[:], ACT.Exp).then_inc(act, 1)
                    ac.wait_ge(ke, 1)
                    nc.scalar.activation(g.kk[:], g.kk[:], ACT.Exp).then_inc(act, 1)
                    nc.scalar.activation(mkT[:], mkT[:], ACT.Exp).then_inc(act, 1)

                @block.tensor
                def _(pe):
                    pe.wait_ge(loaded, 80)
                    pe.wait_ge(kmx, 1)
                    nc.tensor.transpose(ps[0][:, 0:P], km[:], c.ident[:])
                    nc.tensor.transpose(ps[0][0:MEM, P:2 * P], mk[:], c.ident[:])
                    nc.tensor.transpose(ps[0][0:MEM, 2 * P:3 * P], mv[:], c.ident[:]).then_inc(pe_s, 1)
                    pe.wait_ge(cx, 1)
                    nc.tensor.matmul(ps[1][:, 0:C1], c.ones[:], diag[:], start=True, stop=True).then_inc(pe_s, 1)
                    pe.wait_ge(act, 3)
                    for t in range(T):
                        nc.tensor.matmul(ps[2][:, 0:P], g.vv[:, t, :], g.kk[:, t, :], start=(t == 0), stop=False)
                        nc.tensor.matmul(ps[3][:, 0:1], g.kk[:, t, :], c.ones[:, 0:1], start=(t == 0), stop=False)
                    nc.tensor.matmul(ps[2][:, 0:P], mvT[:], mkT[:], start=False, stop=True)
                    nc.tensor.matmul(ps[3][:, 0:1], mkT[:], c.ones[0:MEM, 0:1], start=False, stop=True).then_inc(pe_s, 1)
                    pe.wait_ge(ctxd, 1)
                    nc.tensor.matmul(ps[4][:, 0:D], ctx_m[:], wout[:], start=True, stop=True).then_inc(pe_s, 1)

        def fill(row, k, lk):
            return nc.vector.tensor_copy(row, tile(g.qq, k))

        sq = x.enter_context(nc.sbuf_tensor("la_sq", [P, D], F32))

        def take_dve(k, bank, lk):
            v = nc.vector
            lk(v.tensor_tensor(tile(o, k), bank(0)[:, 0:D], bias[:], ALU.add))
            lk(v.tensor_tensor(sq[:], tile(o, k), tile(o, k), ALU.mult))
            return v.tensor_reduce(tile_col(ss, k), sq[:], AX, ALU.add)

        project(nc, s, c, "p3", 1, wp, [(0, D)], fill, take_dve, None, 2)
        dve, act = s("la_dve2"), s("la_act2")
        with nc.Block() as block:
            @block.scalar
            def _(ac):
                nc.scalar.activation(ss[:], ss[:], ACT.Sqrt).then_inc(act, 1)

            @block.vector
            def _(ve):
                v = nc.vector
                lk = link(ve, dve)
                v.tensor_tensor(g.x[:], g.x[:], g.xn[:], ALU.add)
                ve.wait_ge(act, 1)
                lk(v.tensor_scalar(ss[:], ss[:], NORM_EPS, None, ALU.max))
                lk(v.reciprocal(ss[:], ss[:]))
                lk(v.tensor_tensor(o[:], o[:], bcast(ss[:], D), ALU.mult))
                lk(v.tensor_tensor(o[:], o[:], gout[:].unsqueeze(1).to_broadcast([P, T, D]), ALU.mult))
                lk(v.tensor_tensor(g.x[:], g.x[:], o[:], ALU.add))


def gat(nc, s, c, name, g, table, F, acc, xr, att_w):
    C = F // GAT_HEADS
    Q = WIDE // GROUP
    HG = GROUP * GAT_HEADS
    LAG = dict(hot=0, turn=1, hotT=1, mix=2, relu=2, leaky=3, logit=3, flip=4, flipped=4, spread=4, maxed=5,
               scaled=6, seen=6, shifted=7, weighted=7, summed=7, merged=8)
    EARLY = 2
    sem = {k: s(f"{name}_{k}") for k in LAG}
    got, copied_a, dve, own = s(name + "_got"), s(name + "_index"), s(name + "_dve"), s(name + "_weights")
    gathered = [s(f"{name}_gathered{q}") for q in range(Q)]
    with ExitStack() as x:
        sb = lambda n, sh, d=F32: x.enter_context(nc.sbuf_tensor(f"{name}_{n}", sh, d))
        rows_, hot, hotT, mask = (sb(n, [P, WIDE, w]) for n, w in (("rows", F), ("hot", P), ("hotT", P), ("mask", P)))
        relu, fifth, leaky, junk, junk_m = sb("relu", [P, GROUP * F]), sb("fifth", [P, GROUP * F]), sb("leaky", [P, GROUP * F]), sb("junk", [P, HG, C]), sb("junk_m", [P, HG, P])
        att = sb("att", [P, F])
        logit, flipped = sb("logit", [P, Q, HG]), sb("flipped", [HG, HG * P])
        high, top_new, drop, scale_ = sb("high", [P, HG]), sb("top_new", [P, Q, HG]), sb("drop", [P, Q, HG]), sb("scale", [P, Q, HG])
        masked, shifted_, weight = sb("masked", [P, HG]), sb("shifted", [P, 2, HG]), sb("weight", [P, 2, HG])
        weighted = sb("weighted", [P, GROUP * F])
        zero = sb("zero", [1, P + 512])
        table_ = sb("table", [P, AHEAD * 2, 2 * WIDE], I32)
        now = sb("now", [P, Q, 2, 2 * GROUP], I32)
        index = sb("ix", [P, WIDE], I32)
        pb = lambda n, w: x.enter_context(nc.psum_tensor(f"{name}_{n}", [P, w], F32))
        ps_t, ps_x, ps_m, ps_a, ps_s = pb("ps_t", 512), pb("ps_x", GROUP * F), pb("ps_m", 1024), pb("ps_a", GROUP * F), pb("ps_s", 512)
        ps_top, ps_den = ps_s[:, 0:HG], ps_s[:, 64:64 + HG]
        loaded, init, zeroed = s(name + "_loaded"), s(name + "_init"), s(name + "_zeroed")
        with nc.sbuf_tensor(name + "_tmp", [P, UN, F], F32) as tmp, nc.Block() as block:
            @block.sync
            def _(sp):
                sp.dma_start(att[:], att_w.rearrange("h c -> (h c)")[None, :].to_broadcast([P, F])).then_inc(loaded, 16)

            @block.tensor
            def _(pe):
                pe.wait_ge(zeroed, 1)
                for bank in (ps_t, ps_x, ps_m, ps_a, ps_s):
                    for a in range(0, bank.shape[1], 512):
                        nc.tensor.matmul(bank[:, a:a + 512], zero[:, 0:P], zero[:, P:P + 512], start=True, stop=True)

            @block.gpsimd
            def _(pool):
                for b in (rows_, hotT, index, now):
                    nc.gpsimd.memset(b[:], 0)

            @block.vector
            def _(ve):
                v = nc.vector
                v.memset(zero[:], 0).then_inc(zeroed, 1)
                for b in (hot, logit, top_new, drop, shifted_, weight, relu, fifth):
                    v.memset(b[:], 0)
                v.memset(mask[:], LOW)
                v.memset(scale_[:], 1.0)
                v.memset(g.den[:], 1.0)
                ve.wait_ge(loaded, 16)
                with ve.Fori(0, T // UN) as i:
                    lk = link(ve, init, i, 5)
                    five = lambda b: b[:, bass.ds(i * UN, UN), :]
                    own_logit = junk_m[:, 0, 0:UN * GAT_HEADS]
                    lk(v.tensor_tensor(tmp[:], five(acc), five(xr), ALU.add))
                    lk(v.scalar_tensor_tensor(tmp[:], tmp[:], SLOPE, tmp[:], ALU.mult, ALU.max))
                    lk(v.tensor_tensor(tmp[:], tmp[:], att[:].unsqueeze(1).to_broadcast([P, UN, F]), ALU.mult))
                    lk(v.tensor_reduce(own_logit, tmp[:].rearrange("p t (h c) -> p (t h) c", c=C), AX, ALU.add))
                    lk(v.tensor_copy(five(g.top).rearrange("p t h -> p (t h)"), own_logit))

        block = x.enter_context(nc.Block())

        def at(stage, i, q, lag):
            return i * Q + (q - lag + LAG[stage] + 1 + UP)

        def place(i, q):
            return table_[:, bass.ds((i % AHEAD) * 2, 2), q * 2 * GROUP:(q + 1) * 2 * GROUP]

        def tile_nos(engine, q, lag):
            return nc.values_load_multi_w_load_instructions(
                now[0:1, (q - lag) % Q, 1, GROUP:2 * GROUP], engines=[engine], min_val=0, max_val=T - 1,
                skip_runtime_bounds_check_because=TRUSTED)[1]

        span = lambda q, lag: ((q - lag) % Q * GROUP, ((q - lag) % Q + 1) * GROUP)
        heads = lambda u: slice(u * GAT_HEADS, (u + 1) * GAT_HEADS)

        def loop(eng, body):
            n = eng.value_load(c.loops[0:1, 2:3], min_val=2, max_val=MAX_BODIES // 2)
            with eng.Fori(0, n) as i:
                body(i)
            return n

        @block.sync
        def _(sp):
            def body(i):
                sp.wait_ge(sem["merged"], at("merged", i - AHEAD, Q - 1, 0))
                settle(sp, c)
                for k, source in enumerate((g.table_a, g.table_b)):
                    sp.dma_start(table_[:, bass.ds((i % AHEAD) * 2 + k, 1), :].rearrange("p a (b w) -> p (a b) w", b=2),
                                 source[bass.ds(i * 2, 2), :, :].rearrange("b p w -> p b w")).then_inc(got, 16)
                sp.wait_ge(got, i * 32 + 32)
                settle(sp, c)
            loop(sp, body)

        @block.gpsimd
        def _(pool):
            pool.sem_inc(copied_a, Q)
            pool.sem_inc(sem["leaky"], UP)

            def gather(q):
                for u in range(q * GROUP, (q + 1) * GROUP):
                    nc.gpsimd.indirect_dma_start(rows_[:, u, :], None, table,
                                                 bass.IndirectOffsetOnAxis(ap=index[:, u:u + 1], axis=0)).then_inc(gathered[q], 16)

            for q in range(Q - EARLY, Q):
                gather(q)

            def body(i):
                pool.wait_ge(got, i * 32 + 32)
                settle(pool, c)
                for q in range(Q):
                    pool.wait_ge(sem["relu"], at("relu", i, q, 3))
                    pool.wait_ge(sem["logit"], at("logit", i, q, 4))
                    nc.gpsimd.tensor_tensor(leaky[:], fifth[:], relu[:], ALU.add).then_inc(sem["leaky"], 1)
                    if q >= Q - EARLY:
                        pool.wait_ge(gathered[q], i * (16 * GROUP) + 16 * GROUP)
                    pool.wait_ge(sem["weighted"], at("weighted", i, q, Q))
                    settle(pool, c)
                    nc.gpsimd.tensor_copy(index[:, q * GROUP:(q + 1) * GROUP],
                                          table_[:, bass.ds((i % AHEAD) * 2, 1), q * 2 * GROUP:q * 2 * GROUP + GROUP].rearrange("p a w -> p (a w)")).then_inc(copied_a, 1)
                    pool.wait_ge(copied_a, (i + 1) * Q + q + 1)
                    settle(pool, c)
                    gather(q)
            n = loop(pool, body)
            for q in range(Q - EARLY, Q):
                pool.wait_ge(gathered[q], n * (16 * GROUP) + 16 * GROUP)

        @block.vector
        def _(ve):
            v = nc.vector
            for k in ("hot", "logit", "maxed", "shifted", "merged"):
                ve.sem_inc(sem[k], UP)
            PER = Q * (4 * GROUP + 1)

            def body(i):
                lk = link(ve, dve, i, PER)

                def logits(q):
                    ve.wait_ge(sem["leaky"], at("leaky", i, q, 3))
                    settle(ve, c)
                    for u in range(GROUP):
                        for h in range(GAT_HEADS):
                            k = u * GAT_HEADS + h
                            ins = v.tensor_tensor_reduce(junk[:, k, :], leaky[:, u * F + h * C:u * F + (h + 1) * C], att[:, h * C:(h + 1) * C],
                                                         1.0, 0.0, ALU.mult, ALU.add, logit[:, (q - 3) % Q, k:k + 1])
                    ins.then_inc(sem["logit"], 1)

                def maxima(q):
                    ve.wait_ge(sem["spread"], at("spread", i, q, 5))
                    settle(ve, c)
                    tiles = tile_nos(mybir.EngineType.DVE, q, 5)
                    lo, _ = span(q, 5)
                    for k in range(HG):
                        ins = v.tensor_tensor_reduce(junk_m[:, k, :], ps_m[:, k * P:(k + 1) * P], mask[:, lo + k // GAT_HEADS, :],
                                                     1.0, LOW, ALU.add, ALU.max, high[:, k:k + 1])
                    lk(ins)
                    for u, t in enumerate(tiles):
                        a = heads(u)
                        new, old = top_new[:, (q - 5) % Q, a], tile(g.top, t)
                        lk(v.tensor_tensor(new, old, high[:, a], ALU.max))
                        lk(v.tensor_tensor(drop[:, (q - 5) % Q, a], old, new, ALU.subtract))
                        last = v.tensor_tensor(old, new, new, ALU.max)
                        if u < GROUP - 1:
                            lk(last)
                    last.then_inc(sem["maxed"], 1)
                    ve.wait_ge(sem["maxed"], at("maxed", i, q, 5))

                def merge(q):
                    ve.wait_ge(sem["summed"], at("summed", i, q, 8))
                    ve.wait_ge(sem["scaled"], at("scaled", i, q, 8))
                    settle(ve, c)
                    for u, t in enumerate(tile_nos(mybir.EngineType.DVE, q, 8)):
                        sc = scale_[:, (q - 8) % Q, heads(u)]
                        for h in range(GAT_HEADS):
                            k = u * GAT_HEADS + h
                            den = tile(g.den, t)[:, h:h + 1]
                            v.scalar_tensor_tensor(den, den, sc[:, h:h + 1], ps_den[:, k:k + 1], ALU.mult, ALU.add)
                            col = tile(acc, t)[:, h * C:(h + 1) * C]
                            last = v.scalar_tensor_tensor(col, col, sc[:, h:h + 1], ps_a[:, k * C:(k + 1) * C], ALU.mult, ALU.add)
                        if u < GROUP - 1:
                            lk(last)
                    last.then_inc(sem["merged"], 1)
                    ve.wait_ge(sem["merged"], at("merged", i, q, 8))

                def one_hot(q):
                    lo, hi = span(q, 0)
                    lk(v.tensor_copy(now[:, q, :, :], place(i, q)))
                    places = now[:, q, 0, GROUP:2 * GROUP].bitcast(F32)
                    v.tensor_tensor(hot[:, lo:hi, :], c.col[:].unsqueeze(1).to_broadcast([P, GROUP, P]), bcast(places, P),
                                    ALU.is_equal).then_inc(sem["hot"], 1)

                def shift(q):
                    ve.wait_ge(sem["seen"], at("seen", i, q, 7))
                    ve.wait_ge(sem["summed"], at("summed", i, q, 8))
                    pen = now[:, (q - 7) % Q, 1, 0:GROUP].bitcast(F32)
                    lk(v.tensor_tensor(masked[:].rearrange("p (u h) -> p u h", h=GAT_HEADS),
                                       logit[:, (q - 7) % Q, :].rearrange("p (u h) -> p u h", h=GAT_HEADS), bcast(pen, GAT_HEADS), ALU.add))
                    v.tensor_tensor(shifted_[:, (q - 7) % 2, :], masked[:], ps_top, ALU.subtract).then_inc(sem["shifted"], 1)

                ve.wait_ge(got, i * 32 + 32)
                for q in range(Q):
                    maxima(q)
                    shift(q)
                    merge(q)
                    one_hot(q)
                    logits(q)
                assert lk.count[0] == PER, lk.count

            loop(ve, body)

        @block.tensor
        def _(pe):
            for k in ("turn", "mix", "flip", "spread", "seen", "summed"):
                pe.sem_inc(sem[k], UP)

            def body(i):
                for q in range(Q):
                    pe.wait_ge(sem["hot"], at("hot", i, q, 1))
                    pe.wait_ge(sem["hotT"], at("hotT", i, q, 2))
                    lo, hi = span(q, 1)
                    for n, u in enumerate(range(lo, hi)):
                        last = nc.tensor.transpose(ps_t[:, n * P:(n + 1) * P], hot[:, u, :], c.ident[:])
                    last.then_inc(sem["turn"], 1)
                    pe.wait_ge(sem["maxed"], at("maxed", i, q, 5))
                    nc.tensor.transpose(ps_m[0:HG, 0:P], logit[:, (q - 4) % Q, :], c.ident[:]).then_inc(sem["flip"], 1)
                    lo, hi = span(q, 2)
                    pe.wait_ge(gathered[(q - 2) % Q], i * (16 * GROUP) + 16 * GROUP)
                    pe.wait_ge(sem["relu"], at("relu", i, q, 3))
                    settle(pe, c)
                    tiles = tile_nos(mybir.EngineType.PE, q, 2)
                    many = 512 // F
                    for n in range(0, GROUP, many):
                        nc.tensor.matmul(ps_x[:, n * F:(n + many) * F], c.ident[:], rows_[:, lo + n:lo + n + many, :], start=True, stop=False,
                                         skip_group_check=True)
                    for n, u in enumerate(range(lo, hi)):
                        last = nc.tensor.matmul(ps_x[:, n * F:(n + 1) * F], hotT[:, u, :], tile(xr, tiles[n]), start=False, stop=True,
                                                skip_group_check=True)
                    last.then_inc(sem["mix"], 1)
                    lo, hi = span(q, 6)
                    pe.wait_ge(sem["merged"], at("merged", i, q, 8))
                    for n, u in enumerate(range(lo, hi)):
                        last = nc.tensor.matmul(ps_top[:, heads(n)], hotT[:, u, :], top_new[:, (q - 6) % Q, heads(n)], start=True, stop=True)
                    last.then_inc(sem["seen"], 1)
                    pe.wait_ge(sem["flipped"], at("flipped", i, q, 4))
                    for k in range(0, HG * P, 512):
                        last = nc.tensor.matmul(ps_m[:, k:k + 512], c.ones[0:HG, :], flipped[:, k:k + 512], start=True, stop=True)
                    last.then_inc(sem["spread"], 1)
                    pe.wait_ge(sem["weighted"], at("weighted", i, q, 7))
                    lo, hi = span(q, 7)
                    for n, u in enumerate(range(lo, hi)):
                        nc.tensor.matmul(ps_a[:, n * F:(n + 1) * F], hot[:, u, :], weighted[:, n * F:(n + 1) * F], start=True, stop=True)
                        last = nc.tensor.matmul(ps_den[:, heads(n)], hot[:, u, :], weight[:, (q - 7) % 2, heads(n)], start=True, stop=True)
                    last.then_inc(sem["summed"], 1)
            loop(pe, body)

        @block.scalar
        def _(ac):
            for k in ("hotT", "relu", "flipped", "scaled", "weighted"):
                ac.sem_inc(sem[k], UP)

            def body(i):
                for q in range(Q):
                    ac.wait_ge(sem["shifted"], at("shifted", i, q, 7))
                    w = weight[:, (q - 7) % 2, :]
                    nc.scalar.activation(w, shifted_[:, (q - 7) % 2, :], ACT.Exp).then_inc(own, 1)
                    ac.wait_ge(own, i * Q + q + 1)
                    ac.wait_ge(sem["summed"], at("summed", i, q, 8))
                    lo, _ = span(q, 7)
                    for n in range(GROUP):
                        for h in range(GAT_HEADS):
                            k = n * GAT_HEADS + h
                            ins = nc.scalar.activation(weighted[:, k * C:(k + 1) * C], rows_[:, lo + n, h * C:(h + 1) * C],
                                                       ACT.Copy, scale=w[:, k:k + 1])
                    ins.then_inc(sem["weighted"], 1)
                    ac.wait_ge(sem["turn"], at("turn", i, q, 1))
                    ac.wait_ge(sem["seen"], at("seen", i, q, 7))
                    lo, hi = span(q, 1)
                    flat = lambda b: b[:, lo:hi, :].rearrange("p u n -> p (u n)")
                    nc.scalar.copy(flat(hotT), ps_t[:])
                    nc.scalar.activation(flat(mask), ps_t[:], ACT.Identity, bias=c.low[:, 0:1], scale=-LOW).then_inc(sem["hotT"], 1)
                    ac.wait_ge(sem["maxed"], at("maxed", i, q, 6))
                    nc.scalar.activation(scale_[:, (q - 6) % Q, :], drop[:, (q - 6) % Q, :], ACT.Exp).then_inc(sem["scaled"], 1)
                    ac.wait_ge(sem["flip"], at("flip", i, q, 4))
                    for k in range(HG):
                        ins = nc.scalar.activation(flipped[:, k * P:(k + 1) * P], ps_m[0:HG, 0:P], ACT.Copy, scale=c.ident[0:HG, k:k + 1])
                    ins.then_inc(sem["flipped"], 1)
                    ac.wait_ge(sem["mix"], at("mix", i, q, 2))
                    ac.wait_ge(sem["leaky"], at("leaky", i, q, 3))
                    nc.scalar.activation(relu[:], ps_x[:], ACT.Relu, scale=1.0 - SLOPE)
                    nc.scalar.activation(fifth[:], ps_x[:], ACT.Copy, scale=SLOPE).then_inc(sem["relu"], 1)
            loop(ac, body)


def gat1_finish(nc, s, c, g):
    with ExitStack() as x:
        sb = lambda n, sh: x.enter_context(nc.sbuf_tensor("p4_" + n, sh, F32))
        wt, bias, yout = sb("wt", [P, 1, 2 * D]), sb("bias", [P, C1]), sb("yout", [P, 2, D])
        loaded, inv, scaled = s("p4_loaded"), s("p4_inv"), s("p4_scaled")
        with nc.Block() as block:
            @block.sync
            def _(sp):
                sp.dma_start(wt[:, 0, 0:D], g.wl1).then_inc(loaded, 16)
                sp.dma_start(wt[:, 0, D:2 * D], g.wr1).then_inc(loaded, 16)
                sp.dma_start(bias[:], g.gb0[None, :].to_broadcast([P, C1])).then_inc(loaded, 16)
                sp.wait_ge(loaded, 48)

            @block.vector
            def _(ve):
                nc.vector.reciprocal(g.den[:], g.den[:]).then_inc(inv, 1)
                ve.wait_ge(inv, 1)
                a = g.att[:].rearrange("p t (h c) -> p (t h) c", h=GAT_HEADS)
                nc.vector.tensor_tensor(a, a, bcast(g.den[:].rearrange("p t h -> p (t h)"), C1 // GAT_HEADS), ALU.mult).then_inc(scaled, 1)

        def fill(row, k, lk):
            v = nc.vector
            lk(v.tensor_tensor(row, tile(g.att, k), bias[:], ALU.add))
            return v.tensor_scalar(row, row, 0.0, None, ALU.max)

        def take_dve(k, bank, lk):
            return nc.vector.tensor_copy(tile(g.xr2, k), bank(1)[:, 0:D])

        def take_act(k, bank, slot):
            nc.scalar.copy(tile(g.att2, k), bank(0)[:, 0:D])
            return nc.scalar.copy(yout[:, slot, :], bank(0)[:, 0:D])

        project(nc, s, c, "p4", 1, wt, [(0, D), (D, D)], fill, take_dve, take_act, 1, store=(g.table_y, yout))


def gat2_finish(nc, s, c, g):
    with nc.sbuf_tensor("g2_bias", [P, D], F32) as bias:
        loaded, dve = s("gf_loaded"), s("gf_dve")
        with nc.Block() as block:
            @block.sync
            def _(sp):
                sp.dma_start(bias[:], g.gb1[None, :].to_broadcast([P, D])).then_inc(loaded, 16)

            @block.vector
            def _(ve):
                v = nc.vector
                lk = link(ve, dve)
                lk(v.reciprocal(g.den[:], g.den[:]))
                a = g.att2[:].rearrange("p t (h c) -> p (t h) c", h=GAT_HEADS)
                lk(v.tensor_tensor(a, a, bcast(g.den[:].rearrange("p t h -> p (t h)"), D // GAT_HEADS), ALU.mult))
                lk(v.tensor_tensor(g.x[:], g.x[:], g.att2[:], ALU.add))
                ve.wait_ge(loaded, 16)
                lk(v.tensor_tensor(g.x[:], g.x[:], bias[:].unsqueeze(1).to_broadcast([P, T, D]), ALU.add))


TILES0, TILES1 = (-(-((2 * N + ne * (P - 1)) // P) // 2) * 2 for ne in (16, 8))


class Semaphores:

    def __init__(self, nc):
        self.nc, self.known = nc, {}

    def __call__(self, name):
        self.known[name] = self.nc.alloc_semaphore(name=name)
        return self.known[name]

    def close(self):
        self.nc.clear_and_free_semaphores(list(self.known.values()))
        self.nc.all_engine_barrier()
        self.known.clear()


class Shared:
    pass


def build(nc, io, out):
    g = Shared()
    g.out = out
    g.x_in, g.src, g.dst = io["x"], io["src"], io["dst"]
    g.w1_l, g.w1_r, g.b1, g.w2_l, g.w2_r, g.b2 = (io["L0_gnn_" + n] for n in ("w1_l", "w1_r", "b1", "w2_l", "w2_r", "b2"))
    g.w_qkv, g.b_qkv, g.w_proj, g.b_proj, g.temperature = (io["L0_mix_" + n] for n in ("Wqkv", "bqkv", "Wproj", "bproj", "temperature"))
    g.gate_w0, g.gate_b0, g.e0_w1, g.e0_w2, g.e0_w3 = (io["L0_ffn_" + n] for n in ("gate_w", "gate_b", "w1", "w2", "w3"))
    g.wl0, g.wr0, g.att_w0, g.gb0 = (io["L1_gnn_" + n] for n in ("Wl0", "Wr0", "att0", "b0"))
    g.wl1, g.wr1, g.att_w1, g.gb1 = (io["L1_gnn_" + n] for n in ("Wl1", "Wr1", "att1", "b1"))
    g.w_qkv1, g.mem_kv, g.w_out1, g.b_out1, g.g_out1, g.g_pre = (
        io["L1_mix_" + n] for n in ("w_qkv", "mem_kv", "w_out", "b_out", "g_out", "g_pre"))
    g.gate_w1, g.gate_b1, g.e1_w1, g.e1_b1, g.e1_w2, g.e1_b2 = (
        io["L1_ffn_" + n] for n in ("gate_w", "gate_b", "W1", "b1", "W2", "b2"))
    dram = lambda n, sh, d=F32: nc.dram_tensor(n, sh, d, kind="Internal").ap()
    g.table_y, g.table_l = dram("table_y", [T * P, D]), dram("table_l", [T * P, C1])
    g.table_a, g.table_b = (dram(n, [MAX_BODIES, P, 2 * BODY], I32) for n in ("table_a", "table_b"))
    g.sorted_x, g.sorted_y = dram("sorted_x", [TILES0 * P, D]), dram("sorted_y", [TILES0 * P, D])
    s = Semaphores(nc)
    with ExitStack() as x:
        sb = lambda n, sh, d=F32: x.enter_context(nc.sbuf_tensor(n, sh, d))
        c = Shared()
        c.settled = nc.alloc_semaphore(name="settled")
        c.col, c.pair_no, c.valid, c.head = sb("col", [P, P]), sb("pair_no", [P, ROUND]), sb("valid", [P, T]), sb("head", [P, 4, 32])
        c.part, c.low, c.quadf, c.row8 = sb("part", [P, 1]), sb("low", [P, 1]), sb("quadf", [P, 1]), sb("row8", [8, 8, P])
        c.ones, c.ident, c.after, c.loops = sb("ones", [P, P]), sb("ident", [P, P]), sb("after", [P, P]), sb("loops", [1, 3], I32)
        g.x, g.inv_deg = sb("x", [P, T, D]), sb("inv_deg", [P, T])
        constants(nc, s, c)
        clear_sorted(nc, s, g)
        pair_tables(nc, s, c, g.src, g.dst, g.table_a, g.table_b)
        with ExitStack() as y:
            sb = lambda n, sh: y.enter_context(nc.sbuf_tensor(n, sh, F32))
            g.own, g.qk, g.agg = sb("own", [P, T, D]), sb("qk", [P, T, 2 * D]), sb("agg", [P, T, D + 1])
            g.mix, g.mix_w = sb("mix", [P, H0 * NB, HD + 1]), sb("mix_w", [P, H0 * NB])
            with nc.sbuf_tensor("v1", [P, T, H0 * (HD + 1)], F32) as g.v1:
                layer0_project(nc, s, c, g)
                s.close()
                sage1_and_keys(nc, s, c, g)
                sage1_finish(nc, s, c, g)
            s.close()
            sage2_and_queries(nc, s, c, g)
            s.close()
            layer0_join(nc, s, c, g)
        with ExitStack() as y:
            sb = lambda n, sh, d=F32: y.enter_context(nc.sbuf_tensor(n, sh, d))
            g.xn = sb("xn", [P, T, D])
            g.route = Shared()
            g.route.slot1, g.route.slot2 = sb("slot1", [P, T], I32), sb("slot2", [P, T], I32)
            g.route.w1, g.route.w2, g.route.expert = sb("w1", [P, T]), sb("w2", [P, T]), sb("expert", [1, TILES0], I32)
            g.route.fresh = sb("fresh", [1, TILES0], I32)
            normed(nc, s, "ln_e0", g.x, g.xn)
            route(nc, s, c, "r0", g, 16, TILES0, g.gate_w0, g.gate_b0, True)
            experts(nc, s, c, "e0", g, TILES0, 512, [g.e0_w1, g.e0_w2], g.e0_w3, ACT.Silu)
            combine(nc, s, c, "c0", g)
        s.close()
        with ExitStack() as y:
            sb = lambda n, sh: y.enter_context(nc.sbuf_tensor(n, sh, F32))
            g.den, g.top = sb("den", [P, T, GAT_HEADS]), sb("top", [P, T, GAT_HEADS])
            g.xr2, g.att2 = sb("xr2", [P, T, D]), sb("att2", [P, T, D])
            with ExitStack() as z:
                sb = lambda n, sh: z.enter_context(nc.sbuf_tensor(n, sh, F32))
                g.att, g.xr = sb("att", [P, T, C1]), sb("xr", [P, T, C1])
                with ExitStack() as w:
                    sb = lambda n, sh: w.enter_context(nc.sbuf_tensor(n, sh, F32))
                    g.xn, g.vv, g.kk, g.qq = sb("xn1", [P, T, D]), sb("vv", [P, T, C1]), sb("kk", [P, T, C1]), sb("qq", [P, T, C1])
                    normed(nc, s, "ln_1", g.x, g.xn)
                    layer1_project(nc, s, c, g)
                    attention1(nc, s, c, g)
                s.close()
                gat(nc, s, c, "g1", g, g.table_l, C1, g.att, g.xr, g.att_w0)
                gat1_finish(nc, s, c, g)
            s.close()
            gat(nc, s, c, "g2", g, g.table_y, D, g.att2, g.xr2, g.att_w1)
            gat2_finish(nc, s, c, g)
        s.close()
        with ExitStack() as y:
            sb = lambda n, sh, d=F32: y.enter_context(nc.sbuf_tensor(n, sh, d))
            g.xn = sb("xn2", [P, T, D])
            g.route = Shared()
            g.route.slot1, g.route.slot2 = sb("slot1b", [P, T], I32), sb("slot2b", [P, T], I32)
            g.route.w1, g.route.w2, g.route.expert = sb("w1b", [P, T]), sb("w2b", [P, T]), sb("expert1", [1, TILES1], I32)
            g.route.fresh = sb("fresh1", [1, TILES1], I32)
            normed(nc, s, "ln_e1", g.x, g.xn)
            route(nc, s, c, "r1", g, 8, TILES1, g.gate_w1, g.gate_b1, False)
            experts(nc, s, c, "e1", g, TILES1, 512, [g.e1_w1], g.e1_w2, ACT.Gelu, g.e1_b1, g.e1_b2)
            combine(nc, s, c, "c1", g, g.out)


def clear_sorted(nc, s, g):
    zeroed, stored = s("clear_zeroed"), s("clear_stored")
    with nc.sbuf_tensor("clear_zero", [P, D], F32) as zero, nc.Block() as block:
        @block.vector
        def _(ve):
            nc.vector.memset(zero[:], 0.0).then_inc(zeroed, 1)

        @block.sync
        def _(sp):
            sp.wait_ge(zeroed, 1)
            sp.dma_start(rows(g.sorted_x), zero[:].unsqueeze(1).to_broadcast([P, TILES0, D])).then_inc(stored, 16)
            sp.wait_ge(stored, 16)


_INS = ["x", "src", "dst"] + ["L0_gnn_" + n for n in ("w1_l", "w1_r", "b1", "w2_l", "w2_r", "b2")] + [
    "L0_mix_" + n for n in ("Wqkv", "bqkv", "Wproj", "bproj", "temperature")] + [
    "L0_ffn_" + n for n in ("gate_w", "gate_b", "w1", "w2", "w3")] + [
    "L1_gnn_" + n for n in ("Wl0", "Wr0", "att0", "b0", "Wl1", "Wr1", "att1", "b1")] + [
    "L1_mix_" + n for n in ("w_qkv", "mem_kv", "w_out", "b_out", "g_out", "g_pre")] + [
    "L1_ffn_" + n for n in ("gate_w", "gate_b", "W1", "b1", "W2", "b2")]


def kernel(**inputs):
    import numpy as _np
    import concourse.bacc as _bacc
    from concourse import mybir as _mybir
    from concourse.bass_utils import run_bass_kernel_spmd as _run

    nc = _bacc.Bacc("TRN2", target_bir_lowering=False, num_devices=1)
    arrays, args = {}, {}
    for name in _INS:
        a = _np.ascontiguousarray(inputs[name])
        if name == "L0_mix_temperature":
            a = a.reshape(H0)
        arrays[f"in_{name}_dram"] = a
        args[name] = nc.dram_tensor(f"in_{name}_dram", list(a.shape), _mybir.dt.from_np(a.dtype), kind="ExternalInput").ap()
    out = nc.dram_tensor("out_0_dram", [N, D], F32, kind="ExternalOutput").ap()
    build(nc, args, out)
    return _run(nc, [arrays], core_ids=[0]).results[0]["out_0_dram"]
```
